# Optimizing a Trainium2 kernel written in Bass

```python
import numpy as np
import jax
import jax.numpy as jnp

def _softmax(x, axis=-1):
    return jax.nn.softmax(x, axis=axis)

def _gelu(x):
    return jax.nn.gelu(x, approximate=True)

def _silu(x):
    return jax.nn.silu(x)

def _sigmoid(x):
    return jax.nn.sigmoid(x)

def _layernorm(x, axis=-1, eps=1e-05):
    m = jnp.mean(x, axis=axis, keepdims=True)
    v = jnp.var(x, axis=axis, keepdims=True)
    return (x - m) / jnp.sqrt(v + eps)

def _scatter_add(tgt, idx, src, axis=0):
    return tgt.at[idx].add(src)

def _segment_sum(src, seg, n):
    return jax.ops.segment_sum(src, seg, n)
kernel_name = 'mk_seq_postln_d1_jaxref_r4_d7c0d8'

def setup_inputs(seed: int=0):
    np.random.seed(seed)
    _w = jnp.asarray

    def _L0_attn_setup():
        import jax, jax.numpy as jnp
        import numpy as np
        B, T, C, HS = (4, 512, 256, 16)
        H = C // HS
        LAYER_ID, N_LAYER = (2, 24)
        D_MIX, D_DECAY = (32, 64)
        LN_EPS = 1e-05

        def _wkv6(r, k, v, w, u):
            wd = jnp.exp(-jnp.exp(w))
            rT, kT, vT, wT = (a.transpose(1, 0, 2, 3) for a in (r, k, v, wd))

            def step(S, ins):
                r_t, k_t, v_t, w_t = ins
                kv = jnp.einsum('bhi,bhj->bhij', k_t, v_t)
                y_t = jnp.einsum('bhi,bhij->bhj', r_t, S + u[None, :, :, None] * kv)
                return (w_t[..., None] * S + kv, y_t)
            S0 = jnp.zeros((r.shape[0], H, HS, HS), r.dtype)
            _, ys = jax.lax.scan(step, S0, (rT, kT, vT, wT))
            return ys.transpose(1, 0, 2, 3)
        key = jax.random.key(seed)
        ks = jax.random.split(key, 8)
        r01 = LAYER_ID / (N_LAYER - 1)
        r10 = 1.0 - LAYER_ID / N_LAYER
        ddd = np.arange(C, dtype=np.float64) / C
        tm = lambda p: (1.0 - ddd ** p).reshape(1, 1, C).astype(np.float32)
        time_maa_x = tm(r10)
        time_maa_w = tm(r10)
        time_maa_k = tm(r10)
        time_maa_v = (1.0 - (ddd ** r10 + 0.3 * r01)).reshape(1, 1, C).astype(np.float32)
        time_maa_r = tm(0.5 * r10)
        n = np.arange(C, dtype=np.float64)
        decay = (-6.0 + 5.0 * (n / (C - 1)) ** (0.7 + 1.3 * r01)).reshape(1, 1, C).astype(np.float32)
        zig = ((n + 1) % 3 - 1) * 0.1
        faaaa = (r01 * (1.0 - n / (C - 1)) + zig).reshape(H, HS).astype(np.float32)
        u01 = lambda k, s: jax.random.uniform(k, s, jnp.float32, -0.01, 0.01)
        return {'x': jax.random.normal(ks[0], (B, T, C), jnp.float32), 'time_maa_x': jnp.asarray(time_maa_x), 'time_maa_w': jnp.asarray(time_maa_w), 'time_maa_k': jnp.asarray(time_maa_k), 'time_maa_v': jnp.asarray(time_maa_v), 'time_maa_r': jnp.asarray(time_maa_r), 'time_maa_w1': u01(ks[1], (C, D_MIX * 4)), 'time_maa_w2': u01(ks[2], (4, D_MIX, C)), 'time_decay': jnp.asarray(decay), 'time_decay_w1': u01(ks[3], (C, D_DECAY)), 'time_decay_w2': u01(ks[4], (D_DECAY, C)), 'time_faaaa': jnp.asarray(faaaa), 'W_r': jax.random.normal(ks[5], (C, C), jnp.float32) * 0.02, 'W_k': jax.random.normal(ks[6], (C, C), jnp.float32) * 0.02, 'W_v': jax.random.normal(ks[7], (C, C), jnp.float32) * 0.02, 'W_o': jax.random.normal(jax.random.fold_in(key, 99), (C, C), jnp.float32) * 0.02, 'ln_g': jnp.ones((C,), jnp.float32), 'ln_b': jnp.zeros((C,), jnp.float32)}
    _L0_attn_in = _L0_attn_setup()

    def _L0_ffn_setup():
        import jax, jax.numpy as jnp
        import numpy as np
        import math
        E = 32
        K = 2
        CF = 1.2
        D = 256
        F = 1024
        key = jax.random.key(seed)
        ks = jax.random.split(key, 7)
        s = 0.02
        return {'x': jax.random.normal(ks[0], (4, 512, D), jnp.float32), 'gate_w': jax.random.normal(ks[1], (D, E), jnp.float32) * s, 'gate_b': jnp.zeros((E,), jnp.float32), 'w1': jax.random.normal(ks[2], (E, D, F), jnp.float32) * s, 'b1': jnp.zeros((E, F), jnp.float32), 'w2': jax.random.normal(ks[3], (E, F, D), jnp.float32) * s, 'b2': jnp.zeros((E, D), jnp.float32)}
    _L0_ffn_in = _L0_ffn_setup()
    _d = {'L0_attn_x': _L0_attn_in['x'], 'L0_attn_time_maa_x': _L0_attn_in['time_maa_x'], 'L0_attn_time_maa_w': _L0_attn_in['time_maa_w'], 'L0_attn_time_maa_k': _L0_attn_in['time_maa_k'], 'L0_attn_time_maa_v': _L0_attn_in['time_maa_v'], 'L0_attn_time_maa_r': _L0_attn_in['time_maa_r'], 'L0_attn_time_maa_w1': _L0_attn_in['time_maa_w1'], 'L0_attn_time_maa_w2': _L0_attn_in['time_maa_w2'], 'L0_attn_time_decay': _L0_attn_in['time_decay'], 'L0_attn_time_decay_w1': _L0_attn_in['time_decay_w1'], 'L0_attn_time_decay_w2': _L0_attn_in['time_decay_w2'], 'L0_attn_time_faaaa': _L0_attn_in['time_faaaa'], 'L0_attn_W_r': _L0_attn_in['W_r'], 'L0_attn_W_k': _L0_attn_in['W_k'], 'L0_attn_W_v': _L0_attn_in['W_v'], 'L0_attn_W_o': _L0_attn_in['W_o'], 'L0_attn_ln_g': _L0_attn_in['ln_g'], 'L0_attn_ln_b': _L0_attn_in['ln_b'], 'L0_ffn_gate_w': _L0_ffn_in['gate_w'], 'L0_ffn_gate_b': _L0_ffn_in['gate_b'], 'L0_ffn_w1': _L0_ffn_in['w1'], 'L0_ffn_b1': _L0_ffn_in['b1'], 'L0_ffn_w2': _L0_ffn_in['w2'], 'L0_ffn_b2': _L0_ffn_in['b2']}
    _x0 = _d['L0_attn_x']
    _d['L0_attn_x'] = jax.random.normal(jax.random.fold_in(jax.random.key(seed), 1), (2, 4096, 256), dtype=_x0.dtype)
    del _x0
    return _d

def reference(L0_attn_x, L0_attn_time_maa_x, L0_attn_time_maa_w, L0_attn_time_maa_k, L0_attn_time_maa_v, L0_attn_time_maa_r, L0_attn_time_maa_w1, L0_attn_time_maa_w2, L0_attn_time_decay, L0_attn_time_decay_w1, L0_attn_time_decay_w2, L0_attn_time_faaaa, L0_attn_W_r, L0_attn_W_k, L0_attn_W_v, L0_attn_W_o, L0_attn_ln_g, L0_attn_ln_b, L0_ffn_gate_w, L0_ffn_gate_b, L0_ffn_w1, L0_ffn_b1, L0_ffn_w2, L0_ffn_b2):

    def _L0_attn_ref(x, time_maa_x, time_maa_w, time_maa_k, time_maa_v, time_maa_r, time_maa_w1, time_maa_w2, time_decay, time_decay_w1, time_decay_w2, time_faaaa, W_r, W_k, W_v, W_o, ln_g, ln_b):
        import jax, jax.numpy as jnp
        import numpy as np
        B, T, C, HS = (4, 512, 256, 16)
        H = C // HS
        LAYER_ID, N_LAYER = (2, 24)
        D_MIX, D_DECAY = (32, 64)
        LN_EPS = 1e-05

        def _wkv6(r, k, v, w, u):
            wd = jnp.exp(-jnp.exp(w))
            rT, kT, vT, wT = (a.transpose(1, 0, 2, 3) for a in (r, k, v, wd))

            def step(S, ins):
                r_t, k_t, v_t, w_t = ins
                kv = jnp.einsum('bhi,bhj->bhij', k_t, v_t)
                y_t = jnp.einsum('bhi,bhij->bhj', r_t, S + u[None, :, :, None] * kv)
                return (w_t[..., None] * S + kv, y_t)
            S0 = jnp.zeros((r.shape[0], H, HS, HS), r.dtype)
            _, ys = jax.lax.scan(step, S0, (rT, kT, vT, wT))
            return ys.transpose(1, 0, 2, 3)
        b, t, c = x.shape
        xx = jnp.concatenate([jnp.zeros_like(x[:, :1]), x[:, :-1]], axis=1) - x
        xxx = x + xx * time_maa_x
        m = jnp.tanh(xxx @ time_maa_w1).reshape(b, t, 4, D_MIX)
        m = jnp.einsum('btfd,fdc->fbtc', m, time_maa_w2)
        mw, mk, mv, mr = (m[0], m[1], m[2], m[3])
        xw = x + xx * (time_maa_w + mw)
        xk = x + xx * (time_maa_k + mk)
        xv = x + xx * (time_maa_v + mv)
        xr = x + xx * (time_maa_r + mr)
        r = (xr @ W_r).reshape(b, t, H, HS)
        k = (xk @ W_k).reshape(b, t, H, HS)
        v = (xv @ W_v).reshape(b, t, H, HS)
        ww = jnp.tanh(xw @ time_decay_w1) @ time_decay_w2
        w = (time_decay + ww).reshape(b, t, H, HS)
        y = _wkv6(r, k, v, w, time_faaaa).reshape(b, t, c)
        mu = jnp.mean(y, axis=-1, keepdims=True)
        var = jnp.mean(jnp.square(y - mu), axis=-1, keepdims=True)
        y = (y - mu) * jax.lax.rsqrt(var + LN_EPS) * ln_g + ln_b
        return y @ W_o

    def _L0_ffn_ref(x, gate_w, gate_b, w1, b1, w2, b2):
        import jax, jax.numpy as jnp
        import numpy as np
        import math
        E = 32
        K = 2
        CF = 1.2
        D = 256
        F = 1024
        orig_shape = x.shape
        xt = x.reshape(-1, D)
        T = xt.shape[0]
        C = int(math.ceil(T * K / E * CF))
        logits = xt @ gate_w + gate_b
        probs = jax.nn.softmax(logits, axis=-1)
        top_w, top_i = jax.lax.top_k(probs, K)
        w = top_w / jnp.sum(top_w, axis=-1, keepdims=True)
        flat_e = top_i.reshape(-1)
        oh = jax.nn.one_hot(flat_e, E, dtype=jnp.int32)
        pos_all = jnp.cumsum(oh, axis=0) - 1
        pos = jnp.take_along_axis(pos_all, flat_e[:, None], axis=1)[:, 0]
        valid = pos < C
        pos_d = jnp.where(valid, pos, C)
        x_rep = jnp.repeat(xt, K, axis=0)
        xe = jnp.zeros((E, C, D), x.dtype).at[flat_e, pos_d].add(x_rep, mode='drop')
        he = jax.nn.gelu(jnp.einsum('ecd,edf->ecf', xe, w1) + b1[:, None, :], approximate=False)
        ye = jnp.einsum('ecf,efd->ecd', he, w2) + b2[:, None, :]
        y_flat = ye[flat_e, jnp.minimum(pos, C - 1)] * valid[:, None].astype(x.dtype)
        y = (y_flat.reshape(T, K, D) * w[..., None]).sum(axis=1)
        return y.reshape(orig_shape)
    x = L0_attn_x
    x = _layernorm(x + _L0_attn_ref(x, L0_attn_time_maa_x, L0_attn_time_maa_w, L0_attn_time_maa_k, L0_attn_time_maa_v, L0_attn_time_maa_r, L0_attn_time_maa_w1, L0_attn_time_maa_w2, L0_attn_time_decay, L0_attn_time_decay_w1, L0_attn_time_decay_w2, L0_attn_time_faaaa, L0_attn_W_r, L0_attn_W_k, L0_attn_W_v, L0_attn_W_o, L0_attn_ln_g, L0_attn_ln_b), axis=-1)
    x = _layernorm(x + _L0_ffn_ref(x, L0_ffn_gate_w, L0_ffn_gate_b, L0_ffn_w1, L0_ffn_b1, L0_ffn_w2, L0_ffn_b2), axis=-1)
    return x

_drawn_inputs = setup_inputs


def setup_inputs(seed=0):
    import zlib

    import numpy as np

    out = dict(_drawn_inputs(seed))
    spreads = {'L0_attn_ln_g': (1.0, 0.2),
     'L0_attn_ln_b': (0.0, 0.1),
     'L0_ffn_gate_b': (0.0, 0.1),
     'L0_ffn_b1': (0.0, 0.345),
     'L0_ffn_b2': (0.0, 0.1)}
    factors = {'L0_attn_time_maa_x': 8.0,
     'L0_attn_time_maa_w': 39.292,
     'L0_attn_time_maa_w1': 8.0,
     'L0_attn_time_maa_w2': 8.0,
     'L0_attn_time_decay_w1': 36.82,
     'L0_attn_time_decay_w2': 33.98,
     'L0_attn_time_faaaa': 6.069}
    for name, (base, spread) in spreads.items():
        noise = np.random.default_rng([zlib.crc32(name.encode()), seed]).standard_normal(out[name].shape)
        drawn = base * np.exp(spread * noise) if base else spread * noise
        out[name] = jnp.asarray(drawn.astype(out[name].dtype))
    for name, factor in factors.items():
        out[name] = (out[name] * factor).astype(out[name].dtype)
    return out
```

```python
from contextlib import ExitStack

import concourse.bass as bass
from concourse import mybir

F32 = mybir.dt.float32
BF16 = mybir.dt.bfloat16
U32 = mybir.dt.uint32
ALU = mybir.AluOpType
ACT = mybir.ActivationFunctionType
AX = mybir.AxisListType

P = 128
BATCH = 2
LN_EPS = 1e-5


def stage_value(index, per_stage, within):
    return index * per_stage + within


def wait_from(eng, sem, value):
    if not isinstance(value, int) or value > 0:
        eng.wait_ge(sem, value)


def rwkv_moe(nc, x, maa_x, maa_w, maa_k, maa_v, maa_r, maa_w1, maa_w2, decay, decay_w1, decay_w2,
             faaaa, W_r, W_k, W_v, W_o, ln_g, ln_b, gate_w, gate_b, w1, b1, w2, b2, out):
    B, T, C = x.shape
    E = gate_w.shape[1]
    NTOK = B * T
    NT = NTOK // P
    NSLOT = E * expert_slots(NTOK, E)
    assert B == BATCH

    x_rows = x.rearrange("b t c -> (b t) c")
    out_rows = out.rearrange("b t c -> (b t) c")
    x1_dram = nc.dram_tensor("x1_rows", (NTOK, C), F32, kind="Internal").ap()
    xe_dram = nc.dram_tensor("expert_in_rows", (NSLOT, C), F32, kind="Internal").ap()
    ye_dram = nc.dram_tensor("expert_out_rows", (NSLOT, C), F32, kind="Internal").ap()

    whole = ExitStack()
    with whole:
        def keep_sb(name, shape, dt):
            return whole.enter_context(nc.sbuf_tensor(name, shape, dt))

        ident = keep_sb("ident", [P, P], F32)
        slot_of = keep_sb("slot_of", [P, NT, 2], U32)
        weight_of = keep_sb("weight_of", [P, NT, 2], F32)

        time_mix(nc, x_rows, x1_dram, xe_dram, maa_x, maa_w, maa_k, maa_v, maa_r, maa_w1, maa_w2, decay,
                 decay_w1, decay_w2, faaaa, W_r, W_k, W_v, W_o, ln_g, ln_b, gate_w, gate_b, ident,
                 slot_of, weight_of)
        experts(nc, xe_dram, ye_dram, w1, b1, w2, b2, ident)
        combine(nc, x1_dram, ye_dram, out_rows, slot_of, weight_of)


def expert_slots(tokens, n_experts):
    return -(-tokens * 2 * 12 // (n_experts * 10))


def time_mix(nc, x_rows, x1_dram, xe_dram, maa_x, maa_w, maa_k, maa_v, maa_r, maa_w1, maa_w2, decay,
             decay_w1, decay_w2, faaaa, W_r, W_k, W_v, W_o, ln_g, ln_b, gate_w, gate_b, ident,
             slot_of, weight_of):
    NTOK, C = x_rows.shape
    H, HS = faaaa.shape
    MIX, DMIX, _ = maa_w2.shape
    DDEC = decay_w1.shape[1]
    E = gate_w.shape[1]
    NH = C // P
    HPH = P // HS
    TC = 512
    NCHUNK = NTOK // TC
    CPB = NCHUNK // BATCH
    TPC = TC // P
    NU = NH * HS
    QUAD = 4
    NQ = NU // QUAD
    QH = NQ // NH
    NPAIR = NU // 2
    SLOTS = 2 * NPAIR
    CAP = expert_slots(NTOK, E)
    NSLOT = E * CAP
    SKIP = 1 << 20
    assert NCHUNK % 2 == 0 and MIX * DMIX == P and NSLOT < SKIP

    with ExitStack() as ctx:
        def sb(name, shape, dt=F32):
            return ctx.enter_context(nc.sbuf_tensor(name, shape, dt))

        def psum(name, shape):
            return ctx.enter_context(nc.psum_tensor(name, shape, F32))

        def sem(name):
            return ctx.enter_context(nc.semaphore(name))

        mu_x = sb("mu_x", [P, NH])
        mu = sb("mu", [P, MIX, NH])
        u_col = sb("u_col", [P, NH])
        decay_col = sb("decay_col", [P, NH])
        g_col = sb("g_col", [P, NH])
        b_col = sb("b_col", [P, NH])
        eps_col = sb("eps_col", [P, 1])
        w1_sb = sb("maa_w1_sb", [P, NH, P])
        w2_sb = sb("maa_w2_sb", [P, MIX, C])
        dw1_sb = sb("dw1_sb", [P, NH, DDEC])
        dw2_sb = sb("dw2_sb", [DDEC, C])
        wr_sb = sb("wr_sb", [P, NH, C])
        wk_sb = sb("wk_sb", [P, NH, C])
        wv_sb = sb("wv_sb", [P, NH, C])
        wo_sb = sb("wo_sb", [P, NH, C])
        gate_sb = sb("gate_sb", [P, NH, E])
        gate_bias = sb("gate_bias", [P, E])
        pick_v = sb("pick_v", [P, HS, P], BF16)
        sum_y = sb("sum_y", [P, QUAD, 32])
        sum_head = sb("sum_head", [P, HS, HPH])
        before = sb("before", [P, P], BF16)
        ones = sb("ones", [P, P], BF16)
        expert_id = sb("expert_id", [P, E])
        expert_base = sb("expert_base", [P, E])
        keep = sb("keep", [P, NCHUNK])
        keep_now = sb("keep_now", [P, 2])
        zeros = sb("zeros", [P, 1024])
        x_tok = sb("x_tok", [P, TPC, C])
        xT = sb("xT", [P, NH, TC + 1])
        xx = sb("xx", [P, NH, TC])
        xm = sb("xm", [P, 3, NH, TC])
        hid = sb("hid", [P, TC])
        hid_w = sb("hid_w", [DDEC, TC])
        w_rate = sb("w_rate", [P, TC])
        to_jh = sb("to_jh", [P, P])
        v_full = sb("v_full", [P, NH, TC])
        wT = sb("wT", [P, 2, NH, TC])
        kT = sb("kT", [P, 2, NH, TC])
        rT = sb("rT", [P, 2, NH, TC])
        uT = sb("uT", [P, 2, NH, TC])
        v3 = sb("v3", [P, 2, 3, NH, TC], BF16)
        S = sb("S", [P, NH, QH, QUAD, TC + 1])
        prod = sb("prod", [P, 2, QUAD, TC])
        yT = sb("yT", [P, NH, TC])
        y_tok = sb("y_tok", [P, TPC, C])
        x_res = sb("x_res", [P, TPC, C])
        x1 = sb("x1", [P, TPC, C])
        stats = sb("stats", [P, 2, TPC, 6])
        mv = sb("mv", [P, 2, TPC, 2])
        rstd = sb("rstd", [P, 2, TPC])
        logits = sb("logits", [P, TPC, E])
        top = sb("top", [P, TPC, 8])
        top_i = sb("top_i", [P, TPC, 8], U32)
        top_f = sb("top_f", [P, TPC, 2])
        onehot = sb("onehot", [P, 2, TPC, E])
        hits = sb("hits", [P, TPC, E], BF16)
        seen = sb("seen", [P, E], BF16)
        scratch = sb("scratch", [P, 2, TPC, E])
        pos = sb("pos", [P, 2, TPC])
        base = sb("base", [P, 2, TPC])
        valid = sb("valid", [P, 2, TPC])
        slot_f = sb("slot_f", [P, 2, TPC])
        put_f = sb("put_f", [P, 2, TPC])
        put_slot = sb("put_slot", [P, TPC, 2], U32)
        gap = sb("gap", [P, TPC])
        ratio = sb("ratio", [P, TPC])
        share = sb("share", [P, 2, TPC])

        vb = psum("vb", [P, 2, 2, TC])
        ypsum = psum("ypsum", [P, NH, TC])
        pa = psum("pa", [P, TC])
        pc = psum("pc", [P, TC])

        s_const = sem("s_const")
        v_high = sem("v_high")
        v_rest = sem("v_rest")
        s_perm_kept = sem("s_perm_kept")
        s_perm = sem("s_perm")
        s_pool_const = sem("s_pool_const")
        s_w = sem("s_w")
        s_vperm = sem("s_vperm")
        s_zero = sem("s_zero")
        s_fill = sem("s_fill")
        x_loaded = sem("x_loaded")
        a_full = sem("a_full")
        a_drained = sem("a_drained")
        x_moved = sem("x_moved")
        keep_set = sem("keep_set")
        wait_carrier = sem("wait_carrier")
        xx_done = sem("xx_done")
        xxx_done = sem("xxx_done")
        mix_psum_read = sem("mix_psum_read")
        mixed = sem("mixed")
        rate_done = sem("rate_done")
        w_done = sem("w_done")
        v_split = sem("v_split")
        ruk_done = sem("ruk_done")
        u_done = sem("u_done")
        vb_full = sem("vb_full")
        kv_done = sem("kv_done")
        scanned = sem("scanned")
        start_set = sem("start_set")
        prod_done = sem("prod_done")
        reduced = sem("reduced")
        y_summed = sem("y_summed")
        c_full = sem("c_full")
        c_drained = sem("c_drained")
        res_loaded = sem("res_loaded")
        x1_stored = sem("x1_stored")
        s_dve = sem("s_dve")
        root_done = sem("root_done")
        ratio_done = sem("ratio_done")
        scattered = sem("scattered")

        wo_raw = xm[:, 1]

        def per_chan(v):
            return v.rearrange("(h p) -> p h", p=P)

        loads = [
            (mu_x[:], per_chan(maa_x[0, 0])),
            (mu[:, 0, :], per_chan(maa_w[0, 0])),
            (mu[:, 1, :], per_chan(maa_k[0, 0])),
            (mu[:, 2, :], per_chan(maa_v[0, 0])),
            (mu[:, 3, :], per_chan(maa_r[0, 0])),
            (decay_col[:], per_chan(decay[0, 0])),
            (u_col[:], per_chan(faaaa.rearrange("h i -> (h i)"))),
            (w1_sb[:], maa_w1.rearrange("(h p) n -> p h n", p=P)),
            (dw1_sb[:], decay_w1.rearrange("(h p) n -> p h n", p=P)),
            (dw2_sb[:], decay_w2),
            (wr_sb[:], W_r.rearrange("(h p) n -> p h n", p=P)),
            (wk_sb[:], W_k.rearrange("(h p) n -> p h n", p=P)),
            (xm[:, 0, :, 0:C], W_v.rearrange("(h p) n -> p h n", p=P)),
            (gate_sb[:], gate_w.rearrange("(h p) n -> p h n", p=P)),
            (gate_bias[:], gate_b.partition_broadcast(P)),
            (wo_raw[:, :, 0:C], W_o.rearrange("(h p) n -> p h n", p=P)),
            (wo_raw[:, :, C], per_chan(ln_g)),
            (wo_raw[:, :, C + 1], per_chan(ln_b)),
        ]
        FILL = 4 * P
        assert NSLOT % 4 == 0
        AT = {"x0": 0, "x1": 1, "hid": 3, "mw0": 4, "mw1": 5, "mk0": 6, "mk1": 7, "mv0": 8, "mv1": 9,
              "dw": 10, "K0": 11, "K1": 12, "V0": 13, "V1": 14, "mr0": 15, "mr1": 16, "e0": 17, "e1": 18,
              "R0": 21, "R1": 22, "B0": 25, "B1": 26}
        FA = {name: k for k, name in enumerate(AT)}
        NA = len(FA)
        MIXES = ["w", "k", "v", "r"]
        XM_OF = {"w": 0, "k": 1, "v": 2, "r": 0}
        C_AT = {"turn": 3, "stat1": 6, "root1": 7, "norm1": 8, "back": 10, "wo": 13, "stat2": 16, "root2": 17,
                "norm2": 18, "x1T": 20, "gate": 22, "top": 23, "ratio": 24, "count": 25, "place": 27,
                "scatter": 28}
        NCF = 10
        LN1_AT = 3 * TPC + 1
        X1_AT = 6 * TPC + 2
        GAP_AT = X1_AT + 2 * TPC + 1
        HITS_AT = GAP_AT + 4
        PUT_AT = HITS_AT + TPC + 11
        NCH = PUT_AT + 5
        N_CONST_POOL = 1
        N_CONST = N_CONST_POOL + 5 + NCHUNK // CPB

        block = ctx.enter_context(nc.Block())

        @block.sync
        def _(sp):
            sp.dma_start(x_tok[:], x_rows[0:TC, :].rearrange("(q p) c -> p q c", p=P)).then_inc(x_loaded, 16)
            for to, of in loads:
                sp.dma_start(to, of, allow_slow_non_contiguous=True).then_inc(s_w, 16)
            sp.wait_ge(s_zero, 1)
            for f in range(MIX):
                sp.dma_start(w2_sb[f * DMIX:(f + 1) * DMIX, f, :], maa_w2[f]).then_inc(s_w, 16)
            sp.wait_ge(s_zero, 2)
            for row in range(0, NSLOT, FILL):
                n = min(FILL, NSLOT - row)
                rows = xe_dram[row:row + n, :]
                sp.dma_start(rows.rearrange("(p q) c -> p (q c)", q=4), zeros[0:n // 4, :]).then_inc(s_fill, 16)

            def chunk_io(i, do_a, do_c):
                if do_c:
                    wait_from(sp, c_drained, stage_value(i - 1, NCF, 0) if isinstance(i, int)
                              else stage_value(i, NCF, -NCF))
                    sp.dma_start(x_res[:], x_rows[bass.ds(i * TC - TC, TC), :].rearrange("(q p) c -> p q c", p=P)
                                 ).then_inc(res_loaded, 16)
                if do_a:
                    sp.wait_ge(a_full, stage_value(i, NA, 2))
                    sp.dma_start(x_tok[:], x_rows[bass.ds(i * TC + TC, TC), :].rearrange("(q p) c -> p q c", p=P)
                                 ).then_inc(x_loaded, 16)
                if do_c:
                    store_x1(i - 1)

            def store_x1(c):
                sp.wait_ge(s_dve, stage_value(c, NCH, X1_AT))
                sp.dma_start(x1_dram[bass.ds(c * TC, TC), :].rearrange("(q p) c -> p q c", p=P), x1[:]
                             ).then_inc(x1_stored, 16)

            chunk_io(0, True, False)
            with sp.Fori(1, NCHUNK - 1) as i:
                chunk_io(i, True, True)
            chunk_io(NCHUNK - 1, False, True)
            chunk_io_last = NCHUNK
            sp.wait_ge(c_drained, stage_value(NCHUNK - 1, NCF, 0))
            sp.dma_start(x_res[:], x_rows[(chunk_io_last - 1) * TC:chunk_io_last * TC, :]
                         .rearrange("(q p) c -> p q c", p=P)).then_inc(res_loaded, 16)
            store_x1(NCHUNK - 1)
            sp.wait_ge(x1_stored, 16 * NCHUNK)

        def chunks(eng, body, stage_a, stage_c):
            for s in range(SLOTS):
                stage_a(0, 0, s)
            body(0, 0, True, False)
            with eng.Fori(0, NCHUNK // 2 - 1) as n:
                body(2 * n + 1, 1, True, True)
                body(2 * n + 2, 0, True, True)
            body(NCHUNK - 1, 1, False, True)
            for s in range(SLOTS + 1):
                stage_c(NCHUNK - 1, 1, s)

        @block.tensor
        def _(pe):
            pe.wait_ge(s_const, N_CONST)
            pe.wait_ge(s_w, 16 * (len(loads) + MIX))
            for half, bank in enumerate((pa, pc)):
                pe.matmul(bank[:, 0:C + 2], to_jh[:], wo_raw[:, half, 0:C + 2], start=True, stop=True
                          ).then_inc(s_perm, 1)
            pe.wait_ge(s_perm_kept, 3 * NH)
            pe.wait_ge(s_vperm, 1)

            def a_fill(i, name):
                wait_from(pe, a_drained, stage_value(i, NA, FA[name]))

            def stage_a(i, par, s):
                if s == AT["x0"]:
                    pe.wait_ge(x_loaded, stage_value(i, 16, 16))
                for h in range(NH):
                    if s == AT[f"x{h}"]:
                        a_fill(i, f"x{h}")
                        for q in range(TPC):
                            last = pe.transpose(pa[:, q * P:(q + 1) * P], x_tok[:, q, h * P:(h + 1) * P], ident[:])
                        last.then_inc(a_full, 1)
                if s == AT["hid"]:
                    a_fill(i, "hid")
                    pe.wait_ge(xxx_done, stage_value(i, NH, NH))
                    for h in range(NH):
                        last = pe.matmul(pa[:], w1_sb[:, h, :], xm[:, 2, h, :], start=h == 0, stop=h == NH - 1)
                    last.then_inc(a_full, 1)
                for f, n in enumerate(MIXES):
                    for h in range(NH):
                        if s == AT[f"m{n}{h}"]:
                            a_fill(i, f"m{n}{h}")
                            pe.matmul(pa[:], w2_sb[:, f, h * P:(h + 1) * P], hid[:], start=True, stop=True
                                      ).then_inc(a_full, 1)
                if s == AT["dw"]:
                    a_fill(i, "dw")
                    pe.wait_ge(mixed, stage_value(i, MIX * NH, NH))
                    for h in range(NH):
                        last = pe.matmul(pa[0:DDEC, :], dw1_sb[:, h, :], xm[:, XM_OF["w"], h, :],
                                         start=h == 0, stop=h == NH - 1)
                    last.then_inc(a_full, 1)
                for n, w_sb, order in (("K", wk_sb, 1), ("V", wv_sb, 2), ("R", wr_sb, 3)):
                    for h in range(NH):
                        if s == AT[f"{n}{h}"]:
                            a_fill(i, f"{n}{h}")
                            pe.wait_ge(mixed, stage_value(i, MIX * NH, (order + 1) * NH))
                            for g in range(NH):
                                last = pe.matmul(pa[:], w_sb[:, g, h * P:(h + 1) * P],
                                                 xm[:, XM_OF[n.lower()], g, :], start=g == 0, stop=g == NH - 1)
                            last.then_inc(a_full, 1)
                for h in range(NH):
                    if s == AT[f"e{h}"]:
                        a_fill(i, f"e{h}")
                        pe.matmul(pa[:], dw2_sb[:, h * P:(h + 1) * P], hid_w[:], start=True, stop=True
                                  ).then_inc(a_full, 1)
                    if s == AT[f"B{h}"]:
                        a_fill(i, f"B{h}")
                        pe.wait_ge(ruk_done, stage_value(i, NH, h + 1))
                        pe.matmul(pa[:], sum_head[:].rearrange("p j h -> p (j h)"), xx[:, h, :],
                                  start=True, stop=True).then_inc(a_full, 1)

            def c_fill(i, k):
                wait_from(pe, c_drained, stage_value(i, NCF, k))

            def stage_c(i, par, s):
                for k in range(2):
                    if s == C_AT["turn"] + k:
                        c_fill(i, k)
                        pe.wait_ge(y_summed, stage_value(i, NH, NH))
                        for t in range(2):
                            for h in range(NH):
                                last = pe.transpose(pc[:, t * C + h * P:t * C + (h + 1) * P],
                                                    yT[:, h, (2 * k + t) * P:(2 * k + t + 1) * P], ident[:])
                        last.then_inc(c_full, 1)
                    if s == C_AT["back"] + k:
                        c_fill(i, 2 + k)
                        pe.wait_ge(s_dve, stage_value(i, NCH, LN1_AT))
                        for h in range(NH):
                            for t in range(2):
                                last = pe.transpose(pc[:, h * 2 * P + t * P:h * 2 * P + (t + 1) * P],
                                                    y_tok[:, 2 * k + t, h * P:(h + 1) * P], ident[:])
                        last.then_inc(c_full, 1)
                    if s == C_AT["wo"] + k:
                        c_fill(i, 4 + k)
                        for t in range(2):
                            for h in range(NH):
                                last = pe.matmul(pc[:, t * C:(t + 1) * C], yT[:, h, (2 * k + t) * P:(2 * k + t + 1) * P],
                                                 wo_sb[:, h, :], start=h == 0, stop=h == NH - 1)
                        last.then_inc(c_full, 1)
                    if s == C_AT["x1T"] + k:
                        c_fill(i, 6 + k)
                        pe.wait_ge(s_dve, stage_value(i, NCH, X1_AT))
                        for h in range(NH):
                            for t in range(2):
                                last = pe.transpose(pc[:, h * 2 * P + t * P:h * 2 * P + (t + 1) * P],
                                                    x1[:, 2 * k + t, h * P:(h + 1) * P], ident[:])
                        last.then_inc(c_full, 1)
                if s == C_AT["gate"]:
                    c_fill(i, 8)
                    for t in range(TPC):
                        for h in range(NH):
                            last = pe.matmul(pc[:, t * E:(t + 1) * E], yT[:, h, t * P:(t + 1) * P],
                                             gate_sb[:, h, :], start=h == 0, stop=h == NH - 1)
                    last.then_inc(c_full, 1)
                if s == C_AT["count"]:
                    c_fill(i, 9)
                    pe.wait_ge(s_dve, stage_value(i, NCH, HITS_AT))
                    for t in range(TPC):
                        pe.matmul(pc[:, t * E:(t + 1) * E], ones[:], seen[:], start=True, stop=False)
                        for b in range(t):
                            pe.matmul(pc[:, t * E:(t + 1) * E], ones[:], hits[:, b, :], start=False, stop=False)
                        last = pe.matmul(pc[:, t * E:(t + 1) * E], before[:], hits[:, t, :], start=False, stop=True)
                    last.then_inc(c_full, 1)

            def spread_v(i, par, p):
                half, jj, g0 = p // (NPAIR // NH), (p % (NPAIR // NH)) // 2, 2 * (p % 2)
                wait_from(pe, scanned, stage_value(i, NU, 2 * p - 2))
                if p == 0:
                    pe.wait_ge(v_split, stage_value(i, 3, 3))
                for g in range(2):
                    j = (g0 + g) * QH + jj
                    for part in range(3):
                        last = pe.matmul(vb[:, p % 2, g, :], pick_v[:, j, :], v3[:, par, part, half, :],
                                         start=part == 0, stop=part == 2)
                    last.then_inc(vb_full, 1)

            def reduce_y(i, q):
                half, jj = q // QH, q % QH
                pe.wait_ge(prod_done, stage_value(i, NQ, q + 1))
                if jj == 0:
                    wait_from(pe, y_summed, stage_value(i, NH, half + 1 - NH))
                for g in range(QUAD):
                    last = pe.matmul(ypsum[32 * g:32 * g + 32, half, :], sum_y[:, jj, :], prod[:, q % 2, g, :],
                                     start=jj == 0, stop=jj == QH - 1)
                last.then_inc(reduced, 1)

            def body(i, par, do_a, do_c):
                for p in range(NPAIR):
                    if do_a:
                        stage_a(i + 1, 1 - par, 2 * p)
                    spread_v(i, par, p)
                    if p == 1 and do_c:
                        reduce_y(i - 1, NQ - 1)
                    if do_c:
                        stage_c(i - 1, 1 - par, 2 * p)
                    if do_a:
                        stage_a(i + 1, 1 - par, 2 * p + 1)
                    if p >= 3 and p % 2 == 1:
                        reduce_y(i, (p - 3) // 2)
                    if do_c:
                        stage_c(i - 1, 1 - par, 2 * p + 1)

            def last_c(i, par, s):
                if s == 0:
                    reduce_y(i, NQ - 1)
                stage_c(i, par, s)

            chunks(pe, body, stage_a, last_c)

        @block.vector
        def _(dve):
            nc.vector.memset(w2_sb[:], 0.0).then_inc(s_zero, 1)
            nc.vector.memset(zeros[:], 0.0).then_inc(s_zero, 1)
            nc.vector.memset(seen[:], 0.0).then_inc(s_const, 1)
            nc.vector.memset(S[:], 0.0).then_inc(s_const, 1)
            nc.vector.memset(xT[:], 0.0).then_inc(s_const, 1)
            nc.vector.memset(eps_col[:], LN_EPS).then_inc(s_const, 1)
            nc.vector.memset(keep[:], 1.0).then_inc(s_const, 1)
            dve.wait_ge(s_const, N_CONST_POOL + 5)
            for b in range(NCHUNK // CPB):
                nc.vector.memset(keep[:, b * CPB:b * CPB + 1], 0.0).then_inc(s_const, 1)
            dve.wait_ge(s_w, 16 * (len(loads) + MIX))
            for g in range(NH):
                last = nc.vector.tensor_copy(
                    wv_sb[:, g, :].rearrange("p (a j h) -> p a j h", a=NH, j=HS),
                    xm[:, 0, g, 0:C].rearrange("p (a h j) -> p a j h", a=NH, j=HS))
            last.then_inc(s_vperm, 1)
            dve.wait_ge(s_perm, NH)
            for half, bank in enumerate((pa, pc)):
                nc.vector.tensor_copy(wo_sb[:, half, :], bank[:, 0:C]).then_inc(s_perm_kept, 1)
                nc.vector.tensor_copy(g_col[:, half:half + 1], bank[:, C:C + 1]).then_inc(s_perm_kept, 1)
                nc.vector.tensor_copy(b_col[:, half:half + 1], bank[:, C + 1:C + 2]).then_inc(s_perm_kept, 1)
            dve.wait_ge(s_perm_kept, 3 * NH)
            dve.wait_ge(s_vperm, 1)
            dve.wait_ge(s_const, N_CONST)

            def stage_a(i, par, s):
                if s == 0:
                    dve.tensor_scalar(keep_now[:, par:par + 1], keep[:, bass.ds(i, 1)], 1.0, None, ALU.mult
                                      ).then_inc(keep_set, 1)
                if s == 2:
                    dve.wait_ge(x_moved, stage_value(i, 1, 1))
                    dve.wait_ge(a_drained, stage_value(i, NA, NH))
                    wait_from(dve, a_full, stage_value(i, NA, 0))
                    dve.tensor_tensor(xx[:], xT[:, :, 0:TC], xT[:, :, 1:TC + 1], ALU.subtract).then_inc(xx_done, 1)
                    dve.wait_ge(xx_done, stage_value(i, 1, 1))
                    for h in range(NH):
                        dve.scalar_tensor_tensor(xm[:, 2, h, :], xx[:, h, :], mu_x[:, h:h + 1], xT[:, h, 1:TC + 1],
                                                 ALU.mult, ALU.add).then_inc(xxx_done, 1)
                for f, n in enumerate(MIXES):
                    for h in range(NH):
                        if s == AT[f"m{n}{h}"]:
                            dve.wait_ge(a_full, stage_value(i, NA, FA[f"m{n}{h}"] + 1))
                            if n == "v":
                                dve.wait_ge(a_full, stage_value(i, NA, FA["hid"] + 1))
                            if n == "r":
                                dve.wait_ge(a_full, stage_value(i, NA, FA["dw"] + 1))
                            dve.scalar_tensor_tensor(xm[:, XM_OF[n], h, :], pa[:], mu[:, f, h:h + 1], xx[:, h, :],
                                                     ALU.add, ALU.mult).then_inc(a_drained, 1)
                if s == AT["V1"] + 1:
                    dve.wait_ge(a_drained, stage_value(i, NA, FA["V1"] + 1))
                    dve.tensor_tensor(xm[:, 2], v_full[:], v3[:, par, 0], ALU.subtract).then_inc(v_rest, 1)
                if s == AT["V1"] + 4:
                    dve.wait_ge(v_split, stage_value(i, 3, 2))
                    dve.tensor_tensor(v3[:, par, 2], xm[:, 2], v3[:, par, 1], ALU.subtract).then_inc(v_split, 1)
                if s == AT["B0"] - 1:
                    dve.wait_ge(a_drained, stage_value(i, NA, FA["R1"] + 1))
                    for h in range(NH):
                        dve.scalar_tensor_tensor(xx[:, h, :], rT[:, par, h, :], u_col[:, h:h + 1], kT[:, par, h, :],
                                                 ALU.mult, ALU.mult).then_inc(ruk_done, 1)
                for h in range(NH):
                    if s == AT[f"B{h}"]:
                        dve.wait_ge(a_full, stage_value(i, NA, FA[f"B{h}"] + 1))
                        dve.tensor_tensor(uT[:, par, h, :], pa[:], v_full[:, h, :], ALU.mult).then_inc(a_drained, 1)

            def chain(i, k):
                dve.wait_ge(s_dve, stage_value(i, NCH, k))

            def root(i, k, which):
                dve.wait_ge(root_done, stage_value(i, 2, which + 1))
                dve.reciprocal(rstd[:, which, :], rstd[:, which, :]).then_inc(s_dve, 1)

            def statistics(src, which, first):
                for t in range(TPC):
                    dve.bn_stats(stats[:, which, t, :], src[:, t, :]).then_inc(s_dve, 1)
                return first + TPC

            def stage_c(i, par, s):
                if s == C_AT["stat1"]:
                    dve.wait_ge(c_drained, stage_value(i, NCF, 2))
                    k = statistics(y_tok, 0, 0)
                    chain(i, k)
                    dve.sem_inc(wait_carrier, 1)
                    for t in range(TPC):
                        dve.bn_aggr(mv[:, 0, t, :], stats[:, 0, t, :]).then_inc(s_dve, 1)
                if s == C_AT["norm1"]:
                    root(i, 0, 0)
                    chain(i, 2 * TPC + 1)
                    for t in range(TPC):
                        dve.tensor_scalar(y_tok[:, t, :], y_tok[:, t, :], mv[:, 0, t, 0:1], rstd[:, 0, t:t + 1],
                                          ALU.subtract, ALU.mult).then_inc(s_dve, 1)
                for k in range(2):
                    if s == C_AT["wo"] + k:
                        dve.wait_ge(c_full, stage_value(i, NCF, 5 + k))
                        if k == 0:
                            dve.wait_ge(res_loaded, stage_value(i, 16, 16))
                            wait_from(dve, x1_stored, stage_value(i, 16, 0))
                            wait_from(dve, scattered, stage_value(i, 16 * 2 * TPC, 0))
                        dve.tensor_tensor(x1[:, 2 * k:2 * k + 2, :], pc[:].rearrange("p (t c) -> p t c", t=2),
                                          x_res[:, 2 * k:2 * k + 2, :], ALU.add).then_inc(c_drained, 1)
                if s == C_AT["stat2"]:
                    dve.wait_ge(c_drained, stage_value(i, NCF, 6))
                    statistics(x1, 1, 0)
                    chain(i, 4 * TPC + 1)
                    dve.sem_inc(wait_carrier, 1)
                    for t in range(TPC):
                        dve.bn_aggr(mv[:, 1, t, :], stats[:, 1, t, :]).then_inc(s_dve, 1)
                if s == C_AT["norm2"]:
                    root(i, 0, 1)
                    chain(i, 5 * TPC + 2)
                    for t in range(TPC):
                        dve.tensor_scalar(x1[:, t, :], x1[:, t, :], mv[:, 1, t, 0:1], rstd[:, 1, t:t + 1],
                                          ALU.subtract, ALU.mult).then_inc(s_dve, 1)
                if s == C_AT["gate"]:
                    dve.wait_ge(c_full, stage_value(i, NCF, 9))
                    dve.tensor_tensor(logits[:], pc[:, 0:TPC * E].rearrange("p (t e) -> p t e", t=TPC),
                                      gate_bias[:, None, :].to_broadcast([P, TPC, E]), ALU.add
                                      ).then_inc(c_drained, 1)
                if s == C_AT["top"]:
                    dve.wait_ge(c_drained, stage_value(i, NCF, 9))
                    dve.sem_inc(wait_carrier, 1)
                    for t in range(TPC):
                        dve.max(top[:, t, :], logits[:, t, :]).then_inc(s_dve, 1)
                    chain(i, X1_AT + TPC)
                    dve.sem_inc(wait_carrier, 1)
                    for t in range(TPC):
                        dve.max_index(top_i[:, t, :], top[:, t, :], logits[:, t, :]).then_inc(s_dve, 1)
                    dve.tensor_tensor(gap[:], top[:, :, 1], top[:, :, 0], ALU.subtract).then_inc(s_dve, 1)
                    chain(i, GAP_AT)
                    dve.tensor_copy(top_f[:], top_i[:, :, 0:2]).then_inc(s_dve, 1)
                    chain(i, GAP_AT + 1)
                    for c in range(2):
                        dve.tensor_tensor(onehot[:, c], expert_id[:, None, :].to_broadcast([P, TPC, E]),
                                          top_f[:, :, c:c + 1].to_broadcast([P, TPC, E]), ALU.is_equal
                                          ).then_inc(s_dve, 1)
                    chain(i, GAP_AT + 3)
                    dve.tensor_tensor(hits[:], onehot[:, 0], onehot[:, 1], ALU.add).then_inc(s_dve, 1)
                if s == C_AT["place"]:
                    dve.wait_ge(c_full, stage_value(i, NCF, 10))
                    for c in range(2):
                        ins = dve.tensor_tensor(scratch[:, c], pc[:, 0:TPC * E].rearrange("p (t e) -> p t e", t=TPC),
                                                onehot[:, c], ALU.mult)
                        ins.then_inc(s_dve, 1)
                    chain(i, HITS_AT + 2)
                    dve.tensor_reduce(pos[:], scratch[:], AX.X, ALU.add).then_inc(c_drained, 1)
                    dve.wait_ge(c_drained, stage_value(i, NCF, 10))
                    for c in range(2):
                        dve.tensor_tensor(scratch[:, c], expert_base[:, None, :].to_broadcast([P, TPC, E]),
                                          onehot[:, c], ALU.mult).then_inc(s_dve, 1)
                    chain(i, HITS_AT + 4)
                    dve.tensor_reduce(base[:], scratch[:], AX.X, ALU.add).then_inc(s_dve, 1)
                    for t in range(TPC):
                        dve.tensor_tensor(seen[:], seen[:], hits[:, t, :], ALU.add).then_inc(s_dve, 1)
                        chain(i, HITS_AT + 6 + t)
                    k = HITS_AT + 5 + TPC
                    dve.tensor_scalar(valid[:], pos[:], float(CAP), None, ALU.is_lt).then_inc(s_dve, 1)
                    dve.tensor_scalar(slot_f[:], pos[:], float(CAP - 1), None, ALU.min).then_inc(s_dve, 1)
                    dve.tensor_scalar(put_f[:], pos[:], float(CAP), float(SKIP), ALU.is_ge, ALU.mult
                                      ).then_inc(s_dve, 1)
                    chain(i, k + 3)
                    dve.tensor_tensor(slot_f[:], slot_f[:], base[:], ALU.add).then_inc(s_dve, 1)
                    chain(i, k + 4)
                    dve.tensor_tensor(put_f[:], put_f[:], slot_f[:], ALU.add).then_inc(s_dve, 1)
                    chain(i, k + 5)
                    wait_from(dve, scattered, stage_value(i, 16 * 2 * TPC, 0))
                    dve.tensor_copy(put_slot[:], put_f[:].rearrange("p c t -> p t c")).then_inc(s_dve, 1)
                    dve.tensor_scalar(slot_of[:, bass.ds(i * TPC, TPC), :], slot_f[:].rearrange("p c t -> p t c"),
                                      1.0, None, ALU.mult).then_inc(s_dve, 1)
                    dve.wait_ge(ratio_done, stage_value(i, 1, 1))
                    dve.tensor_scalar(share[:, 1, :], ratio[:], 1.0, None, ALU.add).then_inc(s_dve, 1)
                    chain(i, k + 8)
                    dve.reciprocal(share[:, 0, :], share[:, 1, :]).then_inc(s_dve, 1)
                    chain(i, k + 9)
                    dve.tensor_tensor(share[:, 1, :], share[:, 0, :], ratio[:], ALU.mult).then_inc(s_dve, 1)
                    chain(i, k + 10)
                    dve.tensor_tensor(weight_of[:, bass.ds(i * TPC, TPC), :], share[:].rearrange("p c t -> p t c"),
                                      valid[:].rearrange("p c t -> p t c"), ALU.mult).then_inc(s_dve, 1)

            def sum_y_half(i, par, half):
                dve.wait_ge(reduced, stage_value(i, NQ, (half + 1) * QH))
                dve.tensor_tensor(yT[:, half, :], ypsum[:, half, :], uT[:, par, half, :], ALU.add
                                  ).then_inc(y_summed, 1)

            def body(i, par, do_a, do_c):
                for p in range(NPAIR):
                    half = p // (NPAIR // NH)
                    q = p // 2
                    if do_a:
                        stage_a(i + 1, 1 - par, 2 * p)
                    if p == 0:
                        dve.wait_ge(a_drained, stage_value(i, NA, NA))
                        dve.wait_ge(w_done, stage_value(i, NH, NH))
                    for g in range(2):
                        dve.wait_ge(vb_full, stage_value(i, NU, 2 * p + g + 1))
                        dve.tensor_tensor(vb[:, p % 2, g, :], vb[:, p % 2, g, :], kT[:, par, half, :], ALU.mult
                                          ).then_inc(kv_done, 1)
                    if p % 2 == 0:
                        dve.wait_ge(start_set, stage_value(i, NQ, q + 1))
                    for g in range(2):
                        line = S[:, half, q % QH, 2 * (p % 2) + g, :]
                        dve.wait_ge(kv_done, stage_value(i, NU, 2 * p + g + 1))
                        dve.tensor_tensor_scan(line[:, 1:TC + 1], wT[:, par, half, :], vb[:, p % 2, g, :],
                                               line[:, 0:1], ALU.mult, ALU.add).then_inc(scanned, 1)
                    if p == 1 and do_c:
                        sum_y_half(i - 1, 1 - par, 1)
                    if do_c:
                        stage_c(i - 1, 1 - par, 2 * p)
                    if do_a:
                        stage_a(i + 1, 1 - par, 2 * p + 1)
                    if do_c:
                        stage_c(i - 1, 1 - par, 2 * p + 1)
                    if p == NPAIR - 1:
                        sum_y_half(i, par, 0)

            def last_c(i, par, s):
                if s == 0:
                    sum_y_half(i, par, 1)
                stage_c(i, par, s)

            chunks(dve, body, stage_a, last_c)

        @block.scalar
        def _(act):
            act.wait_ge(s_w, 16 * (len(loads) + MIX))
            act.wait_ge(s_perm_kept, 3 * NH)
            act.wait_ge(s_const, N_CONST)

            def drain(i, name):
                act.wait_ge(a_full, stage_value(i, NA, FA[name] + 1))

            def stage_a(i, par, s):
                if s == 0:
                    wait_from(act, mixed, stage_value(i, MIX * NH, 0))
                    wait_from(act, a_drained, stage_value(i, NA, 0))
                    act.wait_ge(keep_set, stage_value(i, 1, 1))
                    act.activation(xT[:, :, 0], xT[:, :, TC], ACT.Copy, scale=keep_now[:, par:par + 1]
                                   ).then_inc(x_moved, 1)
                    act.wait_ge(x_moved, stage_value(i, 1, 1))
                for h in range(NH):
                    if s == AT[f"x{h}"]:
                        drain(i, f"x{h}")
                        act.activation(xT[:, h, 1:TC + 1], pa[:], ACT.Copy).then_inc(a_drained, 1)
                if s == AT["hid"]:
                    drain(i, "hid")
                    act.activation(hid[:], pa[:], ACT.Tanh).then_inc(a_drained, 1)
                if s == AT["dw"]:
                    drain(i, "dw")
                    act.activation(hid_w[:], pa[0:DDEC, :], ACT.Tanh).then_inc(a_drained, 1)
                for h in range(NH):
                    if s == AT[f"K{h}"]:
                        drain(i, f"K{h}")
                        wait_from(act, scanned, stage_value(i, NU, -NU) if not isinstance(i, int) else (i - 1) * NU)
                        act.activation(kT[:, par, h, :], pa[:], ACT.Copy).then_inc(a_drained, 1)
                    if s == AT[f"V{h}"]:
                        drain(i, f"V{h}")
                        act.activation(v3[:, par, 0, h, :], pa[:], ACT.Copy).then_inc(v_high, 1)
                        act.wait_ge(v_high, stage_value(i, NH, h + 1))
                        act.activation(v_full[:, h, :], pa[:], ACT.Copy).then_inc(a_drained, 1)
                    if s == AT[f"e{h}"]:
                        drain(i, f"e{h}")
                        wait_from(act, w_done, stage_value(i, NH, h))
                        act.activation(w_rate[:], pa[:], ACT.Exp, bias=decay_col[:, h:h + 1]).then_inc(a_drained, 1)
                        act.wait_ge(a_drained, stage_value(i, NA, FA[f"e{h}"] + 1))
                        act.activation(wT[:, par, h, :], w_rate[:], ACT.Exp, scale=-1.0).then_inc(w_done, 1)
                    if s == AT[f"R{h}"]:
                        drain(i, f"R{h}")
                        wait_from(act, prod_done, stage_value(i, NQ, -NQ) if not isinstance(i, int) else (i - 1) * NQ)
                        act.activation(rT[:, par, h, :], pa[:], ACT.Copy).then_inc(a_drained, 1)
                if s == AT["V1"] + 2:
                    act.wait_ge(v_rest, stage_value(i, 1, 1))
                    act.activation(v3[:, par, 1], xm[:, 2], ACT.Copy).then_inc(v_split, 2)

            def stage_c(i, par, s):
                for k in range(2):
                    if s == C_AT["turn"] + k:
                        act.wait_ge(c_full, stage_value(i, NCF, 1 + k))
                        act.activation(y_tok[:, 2 * k:2 * k + 2, :], pc[:].rearrange("p (t c) -> p t c", t=2),
                                       ACT.Copy).then_inc(c_drained, 1)
                    if s == C_AT["back"] + k:
                        act.wait_ge(c_full, stage_value(i, NCF, 3 + k))
                        for h in range(NH):
                            ins = act.activation(yT[:, h, 2 * k * P:(2 * k + 2) * P], pc[:, h * 2 * P:(h + 1) * 2 * P],
                                                 ACT.Identity, bias=b_col[:, h:h + 1], scale=g_col[:, h:h + 1])
                        ins.then_inc(c_drained, 1)
                    if s == C_AT["x1T"] + k:
                        act.wait_ge(c_full, stage_value(i, NCF, 7 + k))
                        act.activation(yT[:, :, 2 * k * P:(2 * k + 2) * P], pc[:].rearrange("p (h t) -> p h t", h=NH),
                                       ACT.Copy).then_inc(c_drained, 1)
                for which, name in enumerate(("root1", "root2")):
                    if s == C_AT[name]:
                        act.wait_ge(s_dve, stage_value(i, NCH, (2 * TPC, 5 * TPC + 1)[which]))
                        act.activation(rstd[:, which, :], mv[:, which, :, 1], ACT.Sqrt, bias=eps_col[:, 0:1]
                                       ).then_inc(root_done, 1)
                if s == C_AT["ratio"]:
                    act.wait_ge(s_dve, stage_value(i, NCH, GAP_AT))
                    act.activation(ratio[:], gap[:], ACT.Exp).then_inc(ratio_done, 1)

            def set_start(i, par, q):
                wait_from(act, scanned, stage_value(i, NU, QUAD * (q + 1) - NU))
                wait_from(act, prod_done, stage_value(i, NQ, q + 1 - NQ))
                quad = S[:, q // QH, q % QH, :, :]
                act.activation(quad[:, :, 0], quad[:, :, TC], ACT.Copy, scale=keep_now[:, par:par + 1]
                               ).then_inc(start_set, 1)

            def body(i, par, do_a, do_c):
                for p in range(NPAIR):
                    if p % 2 == 0:
                        set_start(i, par, p // 2)
                    if do_a:
                        stage_a(i + 1, 1 - par, 2 * p)
                    if do_c:
                        stage_c(i - 1, 1 - par, 2 * p)
                    if do_a:
                        stage_a(i + 1, 1 - par, 2 * p + 1)
                    if do_c:
                        stage_c(i - 1, 1 - par, 2 * p + 1)

            chunks(act, body, stage_a, stage_c)

        @block.gpsimd
        def _(pool):
            done = [0]

            def const(ins):
                done[0] += 1
                ins.then_inc(s_pool_const, 1)
                pool.wait_ge(s_pool_const, done[0])

            def indicator(t, view, conditions):
                const(pool.memset(t, 1.0))
                for pattern, start, step, comparison in conditions:
                    const(pool.affine_select(out=view, in_=view, pattern=pattern, compare_op=comparison,
                                             fill=0.0, base=start, channel_multiplier=step))

            indicator(to_jh[:], to_jh[:].rearrange("p (j h) -> p j h", h=HPH),
                      [([[-1, HS], [-HS, HPH]], 0, 1, ALU.is_equal)])
            indicator(ident[:], ident[:], [([[-1, P]], 0, 1, ALU.is_equal)])
            indicator(pick_v[:], pick_v[:].rearrange("p j (h i) -> p j h i", h=HPH),
                      [([[-HPH, HS], [-1, HPH], [0, HS]], 0, 1, ALU.is_equal)])
            indicator(sum_head[:], sum_head[:], [([[0, HS], [-HS, HPH]], 0, 1, ALU.is_ge),
                                                 ([[0, HS], [HS, HPH]], HS - 1, -1, ALU.is_ge)])
            sy = sum_y[:].rearrange("p a (b h) -> p a b h", h=HPH)
            indicator(sum_y[:], sy, [([[0, QUAD], [0, QUAD], [-HS, HPH]], 0, 1, ALU.is_ge),
                                     ([[0, QUAD], [0, QUAD], [HS, HPH]], HS - 1, -1, ALU.is_ge),
                                     ([[1, QUAD], [-1, QUAD], [0, HPH]], 0, 0, ALU.is_equal)])
            indicator(before[:], before[:], [([[1, P]], 0, -1, ALU.is_gt)])
            const(pool.memset(ones[:], 1.0))
            const(pool.iota(expert_id[:], pattern=[[1, E]], base=0, channel_multiplier=0,
                            allow_small_or_imprecise_dtypes=True))
            pool.iota(expert_base[:], pattern=[[CAP, E]], base=0, channel_multiplier=0,
                      allow_small_or_imprecise_dtypes=True).then_inc(s_const, N_CONST_POOL)

            def stage_a(i, par, s):
                for f, n in enumerate(MIXES):
                    for h in range(NH):
                        if s == AT[f"m{n}{h}"]:
                            pool.wait_ge(a_drained, stage_value(i, NA, FA[f"m{n}{h}"] + 1))
                            m = xm[:, XM_OF[n], h, :]
                            pool.tensor_tensor(m, m, xT[:, h, 1:TC + 1], ALU.add).then_inc(mixed, 1)

            def multiply(i, par, q):
                half = q // QH
                pool.wait_ge(scanned, stage_value(i, NU, QUAD * (q + 1)))
                wait_from(pool, reduced, stage_value(i, NQ, q - 1))
                pool.tensor_tensor(prod[:, q % 2], S[:, half, q % QH, :, 0:TC],
                                   rT[:, par, half, None, :].to_broadcast([P, QUAD, TC]), ALU.mult
                                   ).then_inc(prod_done, 1)

            def stage_c(i, par, s):
                if s == C_AT["scatter"]:
                    pool.wait_ge(s_dve, stage_value(i, NCH, PUT_AT))
                    if isinstance(i, int) and i == 0:
                        pool.wait_ge(s_fill, 16 * -(-NSLOT // FILL))
                    pool.sem_inc(wait_carrier, 1)
                    for t in range(TPC):
                        for c in range(2):
                            pool.indirect_dma_start(
                                out=xe_dram[:, :],
                                out_offset=bass.IndirectOffsetOnAxis(ap=put_slot[:, t, c:c + 1], axis=0),
                                in_=x1[:, t, :], in_offset=None, bounds_check=NSLOT - 1, oob_is_err=False
                            ).then_inc(scattered, 16)

            def body(i, par, do_a, do_c):
                for p in range(NPAIR):
                    if do_a:
                        stage_a(i + 1, 1 - par, 2 * p)
                    if do_c:
                        stage_c(i - 1, 1 - par, 2 * p)
                    if do_a:
                        stage_a(i + 1, 1 - par, 2 * p + 1)
                    if do_c:
                        stage_c(i - 1, 1 - par, 2 * p + 1)
                    if p % 2 == 1:
                        multiply(i, par, p // 2)

            pool.wait_ge(s_fill, 16 * -(-NSLOT // FILL))
            chunks(pool, body, stage_a, stage_c)
            pool.wait_ge(scattered, 16 * 2 * TPC * NCHUNK)


def experts(nc, xe_dram, ye_dram, w1, b1, w2, b2, ident):
    E, C, F = w1.shape
    CAP = xe_dram.shape[0] // E
    KC = C // P
    FC = F // P
    TILES = -(-CAP // P)
    FULL = CAP // P
    REST = CAP - FULL * P
    HC = (CAP + 1) // 2
    assert 2 * HC == CAP + 1
    TURNS = [(t, min(t + 2, TILES)) for t in range(0, TILES, 2)]
    NTURN = len(TURNS)
    BR = E * FC // P
    assert E % 2 == 0

    def rows_of(t):
        return min(P, CAP - t * P)

    with ExitStack() as ctx:
        def sb(name, shape, dt=F32):
            return ctx.enter_context(nc.sbuf_tensor(name, shape, dt))

        def psum(name, shape):
            return ctx.enter_context(nc.psum_tensor(name, shape, F32))

        def sem(name):
            return ctx.enter_context(nc.semaphore(name))

        b1_rows = sb("b1_rows", [P, BR, P])
        b1T = sb("b1T", [P, E, FC])
        w1_sb = sb("w1_sb", [P, 2, KC, F])
        w2e_sb = sb("w2e_sb", [P, 2, FC, C])
        b2_sb = sb("b2_sb", [P, 2, C])
        xe = sb("xe", [P, 2, TILES, C])
        b1_now = sb("b1_now", [P, 2, FC])
        xeT = sb("xeT", [P, KC, 2 * HC])
        hT = sb("hT", [P, FC, 2 * HC])
        ye = sb("ye", [P, 2, TILES, C])
        turn = psum("turn", [P, 2, 512])
        up = psum("up", [P, 2, 2, 512])
        down = psum("down", [P, 2, 512])

        b1_loaded = sem("b1_loaded")
        b1_turned = sem("b1_turned")
        b1_kept = sem("b1_kept")
        x_loaded = [sem(f"xe_loaded{p}") for p in range(2)]
        w1_loaded = [sem(f"w1_loaded{p}") for p in range(2)]
        w2_loaded = [sem(f"w2_loaded{p}") for p in range(2)]
        y_stored = [sem(f"y_stored{p}") for p in range(2)]
        b1_now_set = sem("b1_now_set")
        turned = sem("turned")
        turn_kept = sem("turn_kept")
        up_done = sem("up_done")
        gelu_done = sem("gelu_done")
        down_done = sem("down_done")
        y_kept = sem("y_kept")

        block = ctx.enter_context(nc.Block())

        @block.sync
        def _(sp):
            sp.dma_start(b1_rows[:], b1.rearrange("e (f p) -> (e f) p", p=P).rearrange("(r q) p -> q r p", q=P)
                         ).then_inc(b1_loaded, 16)

            def load(e, par):
                wait_from(sp, turned, stage_value(e, NTURN, -NTURN))
                at = e * CAP
                sp.dma_start(xe[:, par, 0:FULL, :], xe_dram[bass.ds(at, FULL * P), :]
                             .rearrange("(t p) c -> p t c", p=P)).then_inc(x_loaded[par], 16)
                sp.dma_start(xe[0:REST, par, FULL, :], xe_dram[bass.ds(at + FULL * P, REST), :]
                             ).then_inc(x_loaded[par], 16)
                wait_from(sp, up_done, stage_value(e, FC, -FC))
                sp.dma_start(w1_sb[:, par], w1[bass.ds(e, 1)].rearrange("e (k p) f -> p (e k) f", p=P)
                             ).then_inc(w1_loaded[par], 16)
                wait_from(sp, down_done, stage_value(e, TILES, -TILES))
                sp.dma_start(w2e_sb[:, par], w2[bass.ds(e, 1)].rearrange("e (k p) c -> p (e k) c", p=P)
                             ).then_inc(w2_loaded[par], 16)
                wait_from(sp, y_kept, stage_value(e, TILES, -TILES))
                sp.dma_start(b2_sb[:, par], b2[bass.ds(e, 1)].rearrange("e c -> (e c)").partition_broadcast(P)
                             ).then_inc(w2_loaded[par], 16)

            load(0, 0)
            load(1, 1)
            with sp.Fori(1, E // 2) as n:
                load(2 * n, 0)
                load(2 * n + 1, 1)

        def expert_pairs(eng, body):
            body(0, 0, True)
            body(1, 1, True)
            with eng.Fori(1, E // 2 - 1) as n:
                body(2 * n, 0, True)
                body(2 * n + 1, 1, True)
            body(E - 2, 0, True)
            body(E - 1, 1, False)

        @block.tensor
        def _(pe):
            pe.wait_ge(b1_loaded, 16)
            for r in range(BR):
                last = pe.transpose(up[:, 0, 0, r * P:(r + 1) * P], b1_rows[:, r, :], ident[:])
            last.then_inc(b1_turned, 1)

            def turn_x(e, par):
                pe.wait_ge(x_loaded[par], stage_value(e - par, 16, 32))
                for n, (t0, t1) in enumerate(TURNS):
                    bank = turn[:, (par * NTURN + n) % 2, :]
                    wait_from(pe, turn_kept, stage_value(e, NTURN, n - 1))
                    for k in range(KC):
                        for t in range(t0, t1):
                            m = rows_of(t)
                            at = k * 2 * P + (t - t0) * P
                            last = pe.transpose(bank[:, at:at + m], xe[0:m, par, t, k * P:(k + 1) * P],
                                                ident[0:m, 0:m])
                    last.then_inc(turned, 1)

            def body(e, par, more):
                pe.wait_ge(w1_loaded[par], stage_value(e - par, 8, 16))
                pe.wait_ge(turn_kept, stage_value(e, NTURN, NTURN))
                for f in range(FC):
                    wait_from(pe, gelu_done, stage_value(e, FC, f - 1))
                    for half in range(2):
                        for k in range(KC):
                            last = pe.matmul(up[:, f % 2, half, 0:HC], w1_sb[:, par, k, f * P:(f + 1) * P],
                                             xeT[:, k, half * HC:(half + 1) * HC], start=k == 0, stop=k == KC - 1)
                    last.then_inc(up_done, 1)
                if more:
                    turn_x(e + 1, 1 - par)
                pe.wait_ge(w2_loaded[par], stage_value(e - par, 16, 32))
                pe.wait_ge(gelu_done, stage_value(e, FC, FC))
                for t in range(TILES):
                    m = rows_of(t)
                    wait_from(pe, y_kept, stage_value(e, TILES, t - 1))
                    for f in range(FC):
                        last = pe.matmul(down[0:m, (par * TILES + t) % 2, 0:C], hT[:, f, t * P:t * P + m],
                                         w2e_sb[:, par, f, :], start=f == 0, stop=f == FC - 1)
                    last.then_inc(down_done, 1)

            pe.wait_ge(b1_kept, 1)
            turn_x(0, 0)
            expert_pairs(pe, body)

        @block.scalar
        def _(act):
            act.wait_ge(b1_kept, 2)

            def store(e, par):
                act.wait_ge(y_kept, stage_value(e, TILES, TILES))
                act.dma_start(ye_dram[bass.ds(e * CAP, FULL * P), :].rearrange("(t p) c -> p t c", p=P),
                              ye[:, par, 0:FULL, :]).then_inc(y_stored[par], 16)
                act.dma_start(ye_dram[bass.ds(e * CAP + FULL * P, REST), :], ye[0:REST, par, FULL, :]
                              ).then_inc(y_stored[par], 16)

            def body(e, par, more):
                for f in range(FC):
                    act.wait_ge(up_done, stage_value(e, FC, f + 1))
                    if f == 0:
                        wait_from(act, down_done, stage_value(e, TILES, 0))
                        act.wait_ge(b1_now_set, stage_value(e, 1, 1))
                    act.activation(hT[:, f, :].rearrange("p (a b) -> p a b", a=2), up[:, f % 2, :, 0:HC],
                                   ACT.Gelu, bias=b1_now[:, par, f:f + 1]).then_inc(gelu_done, 1)
                    if f == FC // 2 and not (isinstance(e, int) and e == 0):
                        store(e - 1, 1 - par)

            expert_pairs(act, body)
            store(E - 1, 1)
            for p in range(2):
                act.wait_ge(y_stored[p], 16 * E)

        @block.vector
        def _(dve):
            nc.vector.memset(xeT[:, :, CAP:2 * HC], 0.0).then_inc(b1_kept, 1)
            dve.wait_ge(b1_turned, 1)
            nc.vector.tensor_copy(b1T[:].rearrange("p e f -> p (e f)"), up[:, 0, 0, 0:BR * P]).then_inc(b1_kept, 1)
            dve.wait_ge(b1_kept, 2)

            def keep_turned(e, par):
                wait_from(dve, up_done, stage_value(e, FC, 0))
                for n, (t0, t1) in enumerate(TURNS):
                    dve.wait_ge(turned, stage_value(e, NTURN, n + 1))
                    bank = turn[:, (par * NTURN + n) % 2, :].rearrange("p (k t) -> p k t", k=KC)
                    cols = min(t1 * P, CAP) - t0 * P
                    dve.tensor_copy(xeT[:, :, t0 * P:t0 * P + cols], bank[:, :, 0:cols]).then_inc(turn_kept, 1)

            def body(e, par, more):
                wait_from(dve, gelu_done, stage_value(e, FC, -FC))
                dve.tensor_scalar(b1_now[:, par, :], b1T[:, bass.ds(e, 1), :].rearrange("p e f -> p (e f)"),
                                  1.0, None, ALU.mult).then_inc(b1_now_set, 1)
                if more:
                    keep_turned(e + 1, 1 - par)
                dve.wait_ge(w2_loaded[par], stage_value(e - par, 16, 32))
                wait_from(dve, y_stored[par], stage_value(e - par, 16, 0))
                for t in range(TILES):
                    m = rows_of(t)
                    dve.wait_ge(down_done, stage_value(e, TILES, t + 1))
                    dve.tensor_tensor(ye[0:m, par, t, :], down[0:m, (par * TILES + t) % 2, 0:C], b2_sb[0:m, par, :],
                                      ALU.add).then_inc(y_kept, 1)

            keep_turned(0, 0)
            expert_pairs(dve, body)


def combine(nc, x1_dram, ye_dram, out_rows, slot_of, weight_of):
    NTOK, C = x1_dram.shape
    GT = 4
    GROUPS = NTOK // (GT * P)
    assert GROUPS % 2 == 0

    with ExitStack() as ctx:
        def sb(name, shape, dt=F32):
            return ctx.enter_context(nc.sbuf_tensor(name, shape, dt))

        def sem(name):
            return ctx.enter_context(nc.semaphore(name))

        place = sb("place", [P, 2, GT, 2], U32)
        weight = sb("weight", [P, 2, GT, 2])
        rows = sb("rows", [P, 2, GT, 2, C])
        acc = sb("acc", [P, 2, GT, C])
        stats = sb("c_stats", [P, 2, GT, 6])
        mv = sb("c_mv", [P, 2, GT, 2])
        rstd = sb("c_rstd", [P, 2, GT])
        eps_col = sb("c_eps", [P, 1])

        eps_set = sem("eps_set")
        wait_carrier = sem("c_wait_carrier")
        picked = sem("picked")
        gathered = [sem(f"gathered{p}") for p in range(2)]
        x1_loaded = [sem(f"x1_loaded{p}") for p in range(2)]
        stored = [sem(f"stored{p}") for p in range(2)]
        step = sem("c_step")
        rooted = sem("rooted")

        ACC_AT = 2 * GT
        STAT_AT = 4 * GT
        OUT_AT = 5 * GT + 1
        NSTEP = OUT_AT

        def groups(eng, body):
            body(0, 0)
            body(1, 1)
            with eng.Fori(1, GROUPS // 2) as n:
                body(2 * n, 0)
                body(2 * n + 1, 1)

        block = ctx.enter_context(nc.Block())

        @block.gpsimd
        def _(pool):
            def body(g, par):
                pool.wait_ge(picked, stage_value(g, 2, 2))
                wait_from(pool, step, stage_value(g, NSTEP, -NSTEP))
                pool.sem_inc(wait_carrier, 1)
                for t in range(GT):
                    for c in range(2):
                        pool.indirect_dma_start(
                            out=rows[:, par, t, c, :], out_offset=None, in_=ye_dram[:, :],
                            in_offset=bass.IndirectOffsetOnAxis(ap=place[:, par, t, c:c + 1], axis=0)
                        ).then_inc(gathered[par], 16)

            groups(pool, body)

        @block.sync
        def _(sp):
            def load(g, par):
                wait_from(sp, stored[par], stage_value(g - par, 8, 0))
                sp.dma_start(acc[:, par], x1_dram[bass.ds(g * (GT * P), GT * P), :]
                             .rearrange("(t p) c -> p t c", p=P)).then_inc(x1_loaded[par], 16)

            def store(g, par):
                sp.wait_ge(step, stage_value(g, NSTEP, OUT_AT))
                sp.dma_start(out_rows[bass.ds(g * (GT * P), GT * P), :].rearrange("(t p) c -> p t c", p=P),
                             acc[:, par]).then_inc(stored[par], 16)

            load(0, 0)
            load(1, 1)
            store(0, 0)
            with sp.Fori(1, GROUPS // 2) as n:
                load(2 * n, 0)
                store(2 * n - 1, 1)
                load(2 * n + 1, 1)
                store(2 * n, 0)
            store(GROUPS - 1, 1)
            for p in range(2):
                sp.wait_ge(stored[p], 8 * GROUPS)

        @block.scalar
        def _(act):
            act.wait_ge(eps_set, 1)

            def body(g, par):
                act.wait_ge(step, stage_value(g, NSTEP, STAT_AT))
                act.activation(rstd[:, par, :], mv[:, par, :, 1], ACT.Sqrt, bias=eps_col[:, 0:1]
                               ).then_inc(rooted, 1)

            groups(act, body)

        @block.vector
        def _(dve):
            nc.vector.memset(eps_col[:], LN_EPS).then_inc(eps_set, 1)

            def pick(g, par):
                wait_from(dve, gathered[par], stage_value(g - par, 16 * GT, 0))
                dve.tensor_scalar(place[:, par], slot_of[:, bass.ds(g * GT, GT), :], 0, None, ALU.bitwise_or
                                  ).then_inc(picked, 1)
                dve.tensor_scalar(weight[:, par], weight_of[:, bass.ds(g * GT, GT), :], 1.0, None, ALU.mult
                                  ).then_inc(picked, 1)

            def body(g, par, more=True):
                if more:
                    pick(g + 1, 1 - par)
                dve.wait_ge(x1_loaded[par], stage_value(g - par, 8, 16))
                dve.wait_ge(gathered[par], stage_value(g - par, 16 * GT, 32 * GT))
                dve.wait_ge(picked, stage_value(g, 2, 2))
                for c in range(2):
                    if c:
                        dve.wait_ge(step, stage_value(g, NSTEP, GT))
                    for t in range(GT):
                        dve.scalar_tensor_tensor(acc[:, par, t, :], rows[:, par, t, c, :], weight[:, par, t, c:c + 1],
                                                 acc[:, par, t, :], ALU.mult, ALU.add).then_inc(step, 1)
                dve.wait_ge(step, stage_value(g, NSTEP, ACC_AT))
                for t in range(GT):
                    dve.bn_stats(stats[:, par, t, :], acc[:, par, t, :]).then_inc(step, 1)
                dve.wait_ge(step, stage_value(g, NSTEP, 3 * GT))
                dve.sem_inc(wait_carrier, 1)
                for t in range(GT):
                    dve.bn_aggr(mv[:, par, t, :], stats[:, par, t, :]).then_inc(step, 1)
                dve.wait_ge(rooted, stage_value(g, 1, 1))
                dve.reciprocal(rstd[:, par, :], rstd[:, par, :]).then_inc(step, 1)
                dve.wait_ge(step, stage_value(g, NSTEP, STAT_AT + 1))
                for t in range(GT):
                    dve.tensor_scalar(acc[:, par, t, :], acc[:, par, t, :], mv[:, par, t, 0:1], rstd[:, par, t:t + 1],
                                      ALU.subtract, ALU.mult).then_inc(step, 1)

            pick(0, 0)
            body(0, 0)
            body(1, 1)
            with dve.Fori(1, GROUPS // 2 - 1) as n:
                body(2 * n, 0)
                body(2 * n + 1, 1)
            body(GROUPS - 2, 0)
            body(GROUPS - 1, 1, False)


_INS = ["L0_attn_x", "L0_attn_time_maa_x", "L0_attn_time_maa_w", "L0_attn_time_maa_k", "L0_attn_time_maa_v",
        "L0_attn_time_maa_r", "L0_attn_time_maa_w1", "L0_attn_time_maa_w2", "L0_attn_time_decay",
        "L0_attn_time_decay_w1", "L0_attn_time_decay_w2", "L0_attn_time_faaaa", "L0_attn_W_r", "L0_attn_W_k",
        "L0_attn_W_v", "L0_attn_W_o", "L0_attn_ln_g", "L0_attn_ln_b", "L0_ffn_gate_w", "L0_ffn_gate_b",
        "L0_ffn_w1", "L0_ffn_b1", "L0_ffn_w2", "L0_ffn_b2"]


def kernel(**inputs):
    import numpy as _np
    import concourse.bacc as _bacc
    from concourse import mybir as _mybir
    from concourse.bass_utils import run_bass_kernel_spmd as _run

    nc = _bacc.Bacc("TRN2", target_bir_lowering=False, num_devices=1)
    arrays, args = {}, []
    for name in _INS:
        a = _np.ascontiguousarray(inputs[name])
        arrays[f"in_{name}_dram"] = a
        args.append(nc.dram_tensor(f"in_{name}_dram", a.shape, _mybir.dt.from_np(a.dtype), kind="ExternalInput").ap())
    shape = arrays["in_L0_attn_x_dram"].shape
    out = nc.dram_tensor("out_0_dram", shape, _mybir.dt.float32, kind="ExternalOutput").ap()
    rwkv_moe(nc, *args, out)
    r = _run(nc, [arrays], core_ids=[0])
    return r.results[0]["out_0_dram"]
```

```python
from contextlib import ExitStack

import concourse.bass as bass
from concourse import mybir

F32 = mybir.dt.float32
BF16 = mybir.dt.bfloat16
F32R = mybir.dt.float32r
U32 = mybir.dt.uint32
ALU = mybir.AluOpType
ACT = mybir.ActivationFunctionType
AX = mybir.AxisListType

P = 128
BATCH = 2
LN_EPS = 1e-5


def stage_value(index, per_stage, within):
    return index * per_stage + within


def wait_from(eng, sem, value):
    if not isinstance(value, int) or value > 0:
        eng.wait_ge(sem, value)


def rwkv_moe(nc, x, maa_x, maa_w, maa_k, maa_v, maa_r, maa_w1, maa_w2, decay, decay_w1, decay_w2,
             faaaa, W_r, W_k, W_v, W_o, ln_g, ln_b, gate_w, gate_b, w1, b1, w2, b2, out):
    B, T, C = x.shape
    E = gate_w.shape[1]
    NTOK = B * T
    NT = NTOK // P
    NSLOT = E * expert_slots(NTOK, E)
    assert B == BATCH

    x_rows = x.rearrange("b t c -> (b t) c")
    out_rows = out.rearrange("b t c -> (b t) c")
    x1_dram = nc.dram_tensor("x1_rows", (NTOK, C), F32, kind="Internal").ap()
    xe_dram = nc.dram_tensor("expert_in_rows", (NSLOT, C), F32, kind="Internal").ap()
    ye_dram = nc.dram_tensor("expert_out_rows", (NSLOT, C), F32, kind="Internal").ap()

    whole = ExitStack()
    with whole:
        def keep_sb(name, shape, dt):
            return whole.enter_context(nc.sbuf_tensor(name, shape, dt))

        ident = keep_sb("ident", [P, P], F32)
        slot_of = keep_sb("slot_of", [P, NT, 2], U32)
        weight_of = keep_sb("weight_of", [P, NT, 2], F32)

        time_mix(nc, x_rows, x1_dram, xe_dram, maa_x, maa_w, maa_k, maa_v, maa_r, maa_w1, maa_w2, decay,
                 decay_w1, decay_w2, faaaa, W_r, W_k, W_v, W_o, ln_g, ln_b, gate_w, gate_b, ident,
                 slot_of, weight_of)
        experts(nc, xe_dram, ye_dram, w1, b1, w2, b2, ident)
        combine(nc, x1_dram, ye_dram, out_rows, slot_of, weight_of)


def expert_slots(tokens, n_experts):
    return -(-tokens * 2 * 12 // (n_experts * 10))


def time_mix(nc, x_rows, x1_dram, xe_dram, maa_x, maa_w, maa_k, maa_v, maa_r, maa_w1, maa_w2, decay,
             decay_w1, decay_w2, faaaa, W_r, W_k, W_v, W_o, ln_g, ln_b, gate_w, gate_b, ident,
             slot_of, weight_of):
    NTOK, C = x_rows.shape
    H, HS = faaaa.shape
    MIX, DMIX, _ = maa_w2.shape
    DDEC = decay_w1.shape[1]
    E = gate_w.shape[1]
    NH = C // P
    HPH = P // HS
    TC = 512
    NCHUNK = NTOK // TC
    CPB = NCHUNK // BATCH
    TPC = TC // P
    NU = NH * HS
    QUAD = 4
    NQ = NU // QUAD
    QH = NQ // NH
    NPAIR = NU // 2
    LAG = 4
    RING = 4
    JG = HS // 2
    SLOTS = 2 * NPAIR
    CAP = expert_slots(NTOK, E)
    NSLOT = E * CAP
    SKIP = 1 << 20
    assert NCHUNK % 2 == 0 and MIX * DMIX == P and NSLOT < SKIP

    with ExitStack() as ctx:
        def sb(name, shape, dt=F32):
            return ctx.enter_context(nc.sbuf_tensor(name, shape, dt))

        def psum(name, shape):
            return ctx.enter_context(nc.psum_tensor(name, shape, F32))

        def sem(name):
            return ctx.enter_context(nc.semaphore(name))

        mu_x = sb("mu_x", [P, NH])
        mu = sb("mu", [P, MIX, NH])
        u_col = sb("u_col", [P, NH])
        decay_col = sb("decay_col", [P, NH])
        g_col = sb("g_col", [P, NH])
        b_col = sb("b_col", [P, NH])
        eps_col = sb("eps_col", [P, 1])
        w1_sb = sb("maa_w1_sb", [P, NH, P])
        w2_sb = sb("maa_w2_sb", [3 * DMIX, MIX, C], F32R)
        dw1_sb = sb("dw1_sb", [P, NH, DDEC])
        dw2_sb = sb("dw2_sb", [DDEC, C])
        wr_sb = sb("wr_sb", [P, NH, C])
        wk_sb = sb("wk_sb", [P, NH, C])
        wv_sb = sb("wv_sb", [P, NH, C])
        wo_sb = sb("wo_sb", [P, NH, C])
        gate_sb = sb("gate_sb", [P, NH, E])
        gate_bias = sb("gate_bias", [P, E])
        pick_v = sb("pick_v", [P, JG, P], F32R)
        sum_y = sb("sum_y", [P, QUAD, 32])
        sum_head = sb("sum_head", [P, HS, HPH])
        before = sb("before", [P, P], BF16)
        ones = sb("ones", [P, P], BF16)
        expert_id = sb("expert_id", [P, E])
        expert_base = sb("expert_base", [P, E])
        keep = sb("keep", [P, NCHUNK])
        keep_now = sb("keep_now", [P, 2])
        x_tok = sb("x_tok", [P, TPC, C])
        xT = sb("xT", [P, NH, TC + 1])
        xx = sb("xx", [P, NH, TC])
        xm = sb("xm", [P, 3, NH, TC])
        hid = sb("hid", [P, TC])
        hid_parts = sb("hid_parts", [P, 2, TC], F32R)
        hid_stack = sb("hid_stack", [3 * DMIX, MIX, TC], F32R)
        hid_w = sb("hid_w", [DDEC, TC])
        to_jh = sb("to_jh", [P, P])
        v_full = sb("v_full", [P, NH, TC])
        wT = sb("wT", [P, 2, NH, TC])
        kT = sb("kT", [P, 2, NH, TC])
        rT = sb("rT", [P, 2, NH, TC])
        uT = sb("uT", [P, 2, NH, TC])
        v_parts = sb("v_parts", [P, 2, NH, TC], F32R)
        v_stack = sb("v_stack", [P, 2, NH, 2, TC], F32R)
        S = sb("S", [P, RING, QUAD, TC + 1])
        carry = sb("carry", [P, NQ, QUAD])
        prod = sb("prod", [P, 2, QUAD, TC])
        y_sum = sb("y_sum", [P, NH, TC])
        yT = sb("yT", [P, NH, TC])
        y_tok = sb("y_tok", [P, TPC, C])
        x_res = sb("x_res", [P, TPC, C])
        x1 = sb("x1", [P, TPC, C])
        stats = sb("stats", [P, 2, TPC, 6])
        mv = sb("mv", [P, 2, TPC, 2])
        rstd = sb("rstd", [P, 2, TPC])
        logits = sb("logits", [P, TPC, E])
        top = sb("top", [P, TPC, 8])
        top_i = sb("top_i", [P, TPC, 8], U32)
        top_f = sb("top_f", [P, TPC, 2])
        onehot = sb("onehot", [P, 2, TPC, E])
        hits = sb("hits", [P, TPC, E], BF16)
        seen = sb("seen", [P, E], BF16)
        scratch = sb("scratch", [P, 2, TPC, E])
        pos = sb("pos", [P, 2, TPC])
        base = sb("base", [P, 2, TPC])
        valid = sb("valid", [P, 2, TPC])
        slot_f = sb("slot_f", [P, 2, TPC])
        put_f = sb("put_f", [P, 2, TPC])
        put_slot = sb("put_slot", [P, TPC, 2], U32)
        gap = sb("gap", [P, TPC])
        ratio = sb("ratio", [P, TPC])
        share = sb("share", [P, 2, TPC])

        vb = psum("vb", [P, 2, 2, TC])
        ypsum = psum("ypsum", [P, TC])
        pa = psum("pa", [P, 2, TC])
        pc = psum("pc", [P, TC])

        s_const = sem("s_const")
        pick_set = sem("pick_set")
        w2_set = sem("w2_set")
        v_act = sem("v_act")
        hid_stacked = sem("hid_stacked")
        hid_split = sem("hid_split")
        v_stacked = sem("v_stacked")
        s_perm_kept = sem("s_perm_kept")
        s_perm = sem("s_perm")
        s_pool_const = sem("s_pool_const")
        s_w = sem("s_w")
        s_vperm = sem("s_vperm")
        s_zero = sem("s_zero")
        s_fill = sem("s_fill")
        x_loaded = sem("x_loaded")
        a_full = sem("a_full")
        a_drained = [sem(f"a_drained{b}") for b in range(2)]
        x_moved = sem("x_moved")
        keep_set = sem("keep_set")
        carried = sem("carried")
        wait_carrier = sem("wait_carrier")
        xx_done = sem("xx_done")
        xxx_done = sem("xxx_done")
        mix_psum_read = sem("mix_psum_read")
        mixed = sem("mixed")
        rate_done = sem("rate_done")
        w_done = sem("w_done")
        ruk_done = sem("ruk_done")
        u_done = sem("u_done")
        vb_full = sem("vb_full")
        kv_done = sem("kv_done")
        scanned = sem("scanned")
        start_set = sem("start_set")
        prod_done = sem("prod_done")
        reduced = sem("reduced")
        y_summed = sem("y_summed")
        c_full = sem("c_full")
        c_drained = sem("c_drained")
        res_loaded = sem("res_loaded")
        x1_stored = sem("x1_stored")
        s_dve = sem("s_dve")
        root_done = sem("root_done")
        ratio_done = sem("ratio_done")
        scattered = sem("scattered")

        pick_raw = xm[:, 2].rearrange("p h t -> p (h t)").rearrange("p (j m) -> p j m", m=P)
        zeros = y_tok[:].rearrange("p q c -> p (q c)")
        w2_raw = x1[0:3 * DMIX]
        wo_raw = xm[:, 1]

        def per_chan(v):
            return v.rearrange("(h p) -> p h", p=P)

        loads = [
            (mu_x[:], per_chan(maa_x[0, 0])),
            (mu[:, 0, :], per_chan(maa_w[0, 0])),
            (mu[:, 1, :], per_chan(maa_k[0, 0])),
            (mu[:, 2, :], per_chan(maa_v[0, 0])),
            (mu[:, 3, :], per_chan(maa_r[0, 0])),
            (decay_col[:], per_chan(decay[0, 0])),
            (u_col[:], per_chan(faaaa.rearrange("h i -> (h i)"))),
            (w1_sb[:], maa_w1.rearrange("(h p) n -> p h n", p=P)),
            (dw1_sb[:], decay_w1.rearrange("(h p) n -> p h n", p=P)),
            (dw2_sb[:], decay_w2),
            (wr_sb[:], W_r.rearrange("(h p) n -> p h n", p=P)),
            (wk_sb[:], W_k.rearrange("(h p) n -> p h n", p=P)),
            (xm[:, 0, :, 0:C], W_v.rearrange("(h p) n -> p h n", p=P)),
            (gate_sb[:], gate_w.rearrange("(h p) n -> p h n", p=P)),
            (gate_bias[:], gate_b.partition_broadcast(P)),
            (wo_raw[:, :, 0:C], W_o.rearrange("(h p) n -> p h n", p=P)),
            (wo_raw[:, :, C], per_chan(ln_g)),
            (wo_raw[:, :, C + 1], per_chan(ln_b)),
        ]
        FILL = 4 * P
        assert NSLOT % 4 == 0
        AT = {"x0": 0, "x1": 1, "hid": 4, "mw0": 9, "mw1": 10, "mk0": 11, "mk1": 12, "mv0": 13, "mv1": 14,
              "dw": 15, "K0": 16, "K1": 17, "V0": 18, "V1": 19, "mr0": 20, "mr1": 21, "e0": 23, "e1": 24,
              "R0": 25, "R1": 26, "B0": 29, "B1": 30}
        FA = {name: k for k, name in enumerate(AT)}
        NA = len(FA)
        NAB = NA // 2
        assert NA % 2 == 0
        MIXES = ["w", "k", "v", "r"]
        XM_OF = {"w": 0, "k": 1, "v": 2, "r": 0}
        C_AT = {"turn": 7, "stat1": 10, "root1": 11, "norm1": 12, "back": 14, "wo0": 17, "z0": 18, "wo1": 19,
                "z1": 20, "stat2": 21, "root2": 22, "norm2": 23, "x1T": 25, "gate": 27, "top": 28, "ratio": 29,
                "count": 30, "place": 31, "scatter": 31}
        NCF = 10
        LN1_AT = 3 * TPC + 1
        X1_AT = 6 * TPC + 2
        GAP_AT = X1_AT + 2 * TPC + 1
        HITS_AT = GAP_AT + 4
        PUT_AT = HITS_AT + TPC + 11
        NCH = PUT_AT + 5
        N_CONST_POOL = 1
        N_CONST = N_CONST_POOL + 5 + NCHUNK // CPB

        def pa_of(name):
            return pa[:, FA[name] % 2, :]

        def drained_sem(name):
            return a_drained[FA[name] % 2]

        def wait_drained(eng, i, name):
            wait_from(eng, drained_sem(name), stage_value(i, NAB, FA[name] // 2 + 1))

        block = ctx.enter_context(nc.Block())

        @block.sync
        def _(sp):
            sp.dma_start(x_tok[:], x_rows[0:TC, :].rearrange("(q p) c -> p q c", p=P)).then_inc(x_loaded, 16)
            for to, of in loads:
                sp.dma_start(to, of, allow_slow_non_contiguous=True).then_inc(s_w, 16)
            for part in range(3):
                sp.dma_start(x1[part * DMIX:(part + 1) * DMIX], maa_w2.rearrange("f d c -> d f c")
                             ).then_inc(s_w, 16)
            sp.wait_ge(s_zero, 1)
            for row in range(0, NSLOT, FILL):
                n = min(FILL, NSLOT - row)
                rows = xe_dram[row:row + n, :]
                sp.dma_start(rows.rearrange("(p q) c -> p (q c)", q=4), zeros[0:n // 4]).then_inc(s_fill, 16)

            def stack_hidden(i):
                sp.wait_ge(hid_split, stage_value(i, 2, 2))
                for f in range(MIX):
                    for row, part in enumerate((0, 1, 0)):
                        sp.dma_start(hid_stack[row * DMIX:(row + 1) * DMIX, f, :].bitcast(F32),
                                     hid_parts[f * DMIX:(f + 1) * DMIX, part, :].bitcast(F32)
                                     ).then_inc(hid_stacked, 16)

            def stack_v(i, par):
                wait_drained(sp, i, "V1")
                for part in range(2):
                    for g in range(2):
                        sp.dma_start(v_stack[part * (P // 2):(part + 1) * (P // 2), par, :, g, :].bitcast(F32),
                                     v_parts[g * (P // 2):(g + 1) * (P // 2), part, :, :].bitcast(F32)
                                     ).then_inc(v_stacked, 16)

            def chunk_io(i, par, do_a, do_c, more_x=True):
                if do_c:
                    wait_from(sp, c_drained, stage_value(i - 1, NCF, 0) if isinstance(i, int)
                              else stage_value(i, NCF, -NCF))
                    sp.dma_start(x_res[:], x_rows[bass.ds(i * TC - TC, TC), :].rearrange("(q p) c -> p q c", p=P)
                                 ).then_inc(res_loaded, 16)
                if do_a:
                    stack_hidden(i + 1)
                    if more_x:
                        sp.dma_start(x_tok[:], x_rows[bass.ds(i * TC + 2 * TC, TC), :]
                                     .rearrange("(q p) c -> p q c", p=P)).then_inc(x_loaded, 16)
                    stack_v(i + 1, 1 - par)
                if do_c:
                    store_x1(i - 1)

            def store_x1(c):
                sp.wait_ge(s_dve, stage_value(c, NCH, X1_AT))
                sp.dma_start(x1_dram[bass.ds(c * TC, TC), :].rearrange("(q p) c -> p q c", p=P), x1[:]
                             ).then_inc(x1_stored, 16)

            stack_hidden(0)
            sp.dma_start(x_tok[:], x_rows[TC:2 * TC, :].rearrange("(q p) c -> p q c", p=P)).then_inc(x_loaded, 16)
            stack_v(0, 0)
            chunk_io(0, 0, True, False)
            chunk_io(1, 1, True, True)
            chunk_io(2, 0, True, True)
            with sp.Fori(1, NCHUNK // 2 - 2) as n:
                chunk_io(2 * n + 1, 1, True, True)
                chunk_io(2 * n + 2, 0, True, True)
            chunk_io(NCHUNK - 3, 1, True, True)
            chunk_io(NCHUNK - 2, 0, True, True, False)
            chunk_io(NCHUNK - 1, 1, False, True)
            chunk_io_last = NCHUNK
            sp.wait_ge(c_drained, stage_value(NCHUNK - 1, NCF, 0))
            sp.dma_start(x_res[:], x_rows[(chunk_io_last - 1) * TC:chunk_io_last * TC, :]
                         .rearrange("(q p) c -> p q c", p=P)).then_inc(res_loaded, 16)
            store_x1(NCHUNK - 1)
            sp.wait_ge(x1_stored, 16 * NCHUNK)

        def chunks(eng, body, stage_a, stage_c):
            for s in range(SLOTS):
                stage_a(0, 0, s)
            body(0, 0, True, False)
            body(1, 1, True, True)
            body(2, 0, True, True)
            with eng.Fori(1, NCHUNK // 2 - 1) as n:
                body(2 * n + 1, 1, True, True)
                body(2 * n + 2, 0, True, True)
            body(NCHUNK - 1, 1, False, True)
            for s in range(SLOTS + 1):
                stage_c(NCHUNK - 1, 1, s)

        @block.tensor
        def _(pe):
            pe.wait_ge(s_const, N_CONST)
            pe.wait_ge(s_w, 16 * (len(loads) + 3))
            for half, bank in enumerate((pa[:, 0, :], pc)):
                pe.matmul(bank[:, 0:C + 2], to_jh[:], wo_raw[:, half, 0:C + 2], start=True, stop=True
                          ).then_inc(s_perm, 1)
            pe.wait_ge(s_perm_kept, 3 * NH)
            pe.wait_ge(s_vperm, 1)
            pe.wait_ge(w2_set, 2)
            pe.wait_ge(pick_set, 1)

            def a_fill(i, name):
                wait_from(pe, drained_sem(name), stage_value(i, NAB, FA[name] // 2))

            def stage_a(i, par, s):
                if s == AT["x0"]:
                    pe.wait_ge(x_loaded, stage_value(i, 16, 16))
                for h in range(NH):
                    if s == AT[f"x{h}"]:
                        a_fill(i, f"x{h}")
                        for q in range(TPC):
                            last = pe.transpose(pa_of(f"x{h}")[:, q * P:(q + 1) * P], x_tok[:, q, h * P:(h + 1) * P], ident[:])
                        last.then_inc(a_full, 1)
                if s == AT["hid"]:
                    a_fill(i, "hid")
                    pe.wait_ge(xxx_done, stage_value(i, NH, NH))
                    for h in range(NH):
                        last = pe.matmul(pa_of("hid"), w1_sb[:, h, :], xm[:, 2, h, :], start=h == 0, stop=h == NH - 1)
                    last.then_inc(a_full, 1)
                for f, n in enumerate(MIXES):
                    for h in range(NH):
                        if s == AT[f"m{n}{h}"]:
                            a_fill(i, f"m{n}{h}")
                            pe.wait_ge(hid_stacked, stage_value(i, 16 * 3 * MIX, 16 * 3 * MIX))
                            pe.matmul(pa_of(f"m{n}{h}"), w2_sb[:, f, h * P:(h + 1) * P], hid_stack[:, f, :], start=True, stop=True
                                      ).then_inc(a_full, 1)
                if s == AT["dw"]:
                    a_fill(i, "dw")
                    pe.wait_ge(mixed, stage_value(i, MIX * NH, NH))
                    for h in range(NH):
                        last = pe.matmul(pa_of("dw")[0:DDEC, :], dw1_sb[:, h, :], xm[:, XM_OF["w"], h, :],
                                         start=h == 0, stop=h == NH - 1)
                    last.then_inc(a_full, 1)
                for n, w_sb, order in (("K", wk_sb, 1), ("V", wv_sb, 2), ("R", wr_sb, 3)):
                    for h in range(NH):
                        if s == AT[f"{n}{h}"]:
                            a_fill(i, f"{n}{h}")
                            pe.wait_ge(mixed, stage_value(i, MIX * NH, (order + 1) * NH))
                            for g in range(NH):
                                last = pe.matmul(pa_of(f"{n}{h}"), w_sb[:, g, h * P:(h + 1) * P],
                                                 xm[:, XM_OF[n.lower()], g, :], start=g == 0, stop=g == NH - 1)
                            last.then_inc(a_full, 1)
                for h in range(NH):
                    if s == AT[f"e{h}"]:
                        a_fill(i, f"e{h}")
                        pe.matmul(pa_of(f"e{h}"), dw2_sb[:, h * P:(h + 1) * P], hid_w[:], start=True, stop=True
                                  ).then_inc(a_full, 1)
                    if s == AT[f"B{h}"]:
                        a_fill(i, f"B{h}")
                        pe.wait_ge(ruk_done, stage_value(i, NH, h + 1))
                        pe.matmul(pa_of(f"B{h}"), sum_head[:].rearrange("p j h -> p (j h)"), xx[:, h, :],
                                  start=True, stop=True).then_inc(a_full, 1)

            def c_fill(i, k):
                wait_from(pe, c_drained, stage_value(i, NCF, k))

            def stage_c(i, par, s):
                for k in range(2):
                    if s == C_AT["turn"] + k:
                        c_fill(i, k)
                        pe.wait_ge(y_summed, stage_value(i, NH, NH))
                        for t in range(2):
                            for h in range(NH):
                                last = pe.transpose(pc[:, t * C + h * P:t * C + (h + 1) * P],
                                                    y_sum[:, h, (2 * k + t) * P:(2 * k + t + 1) * P], ident[:])
                        last.then_inc(c_full, 1)
                    if s == C_AT["back"] + k:
                        c_fill(i, 2 + k)
                        pe.wait_ge(s_dve, stage_value(i, NCH, LN1_AT))
                        for h in range(NH):
                            for t in range(2):
                                last = pe.transpose(pc[:, h * 2 * P + t * P:h * 2 * P + (t + 1) * P],
                                                    y_tok[:, 2 * k + t, h * P:(h + 1) * P], ident[:])
                        last.then_inc(c_full, 1)
                    if s == C_AT[f"wo{k}"]:
                        c_fill(i, 4 + k)
                        for t in range(2):
                            for h in range(NH):
                                last = pe.matmul(pc[:, t * C:(t + 1) * C], yT[:, h, (2 * k + t) * P:(2 * k + t + 1) * P],
                                                 wo_sb[:, h, :], start=h == 0, stop=h == NH - 1)
                        last.then_inc(c_full, 1)
                    if s == C_AT["x1T"] + k:
                        c_fill(i, 6 + k)
                        pe.wait_ge(s_dve, stage_value(i, NCH, X1_AT))
                        for h in range(NH):
                            for t in range(2):
                                last = pe.transpose(pc[:, h * 2 * P + t * P:h * 2 * P + (t + 1) * P],
                                                    x1[:, 2 * k + t, h * P:(h + 1) * P], ident[:])
                        last.then_inc(c_full, 1)
                if s == C_AT["gate"]:
                    c_fill(i, 8)
                    for t in range(TPC):
                        for h in range(NH):
                            last = pe.matmul(pc[:, t * E:(t + 1) * E], yT[:, h, t * P:(t + 1) * P],
                                             gate_sb[:, h, :], start=h == 0, stop=h == NH - 1)
                    last.then_inc(c_full, 1)
                if s == C_AT["count"]:
                    c_fill(i, 9)
                    pe.wait_ge(s_dve, stage_value(i, NCH, HITS_AT))
                    for t in range(TPC):
                        pe.matmul(pc[:, t * E:(t + 1) * E], ones[:], seen[:], start=True, stop=False)
                        for b in range(t):
                            pe.matmul(pc[:, t * E:(t + 1) * E], ones[:], hits[:, b, :], start=False, stop=False)
                        last = pe.matmul(pc[:, t * E:(t + 1) * E], before[:], hits[:, t, :], start=False, stop=True)
                    last.then_inc(c_full, 1)

            def spread_v(i, par, p):
                half, jj, g0 = p // (NPAIR // NH), (p % (NPAIR // NH)) // 2, 2 * (p % 2)
                wait_from(pe, scanned, stage_value(i, NU, 2 * p - 2))
                if p == 0:
                    pe.wait_ge(v_stacked, stage_value(i, 16 * 4, 16 * 4))
                for g in range(2):
                    j = (g0 + g) * QH + jj
                    pe.matmul(vb[:, p % 2, g, :], pick_v[:, j % JG, :], v_stack[:, par, half, j // JG, :],
                              start=True, stop=True).then_inc(vb_full, 1)

            def reduce_y(i, q):
                half, jj = q // QH, q % QH
                pe.wait_ge(prod_done, stage_value(i, NQ, q + 1))
                if jj == 0:
                    wait_from(pe, y_summed, stage_value(i, NH, half))
                for g in range(QUAD):
                    last = pe.matmul(ypsum[32 * g:32 * g + 32, :], sum_y[:, jj, :], prod[:, q % 2, g, :],
                                     start=jj == 0, stop=jj == QH - 1)
                last.then_inc(reduced, 1)

            def body(i, par, do_a, do_c):
                for p in range(NPAIR):
                    if do_a:
                        stage_a(i + 1, 1 - par, 2 * p)
                    spread_v(i, par, p)
                    if p in (LAG - 4, LAG - 2) and do_c:
                        reduce_y(i - 1, NQ + (p - LAG) // 2)
                    if p >= LAG and p % 2 == 0:
                        reduce_y(i, (p - LAG) // 2)
                    if do_c:
                        stage_c(i - 1, 1 - par, 2 * p)
                    if do_a:
                        stage_a(i + 1, 1 - par, 2 * p + 1)
                    if do_c:
                        stage_c(i - 1, 1 - par, 2 * p + 1)

            def last_c(i, par, s):
                if s == 0:
                    for q in (NQ - 2, NQ - 1):
                        reduce_y(i, q)
                stage_c(i, par, s)

            chunks(pe, body, stage_a, last_c)

        @block.vector
        def _(dve):
            nc.vector.memset(zeros, 0.0).then_inc(s_zero, 1)
            nc.vector.memset(seen[:], 0.0).then_inc(s_const, 1)
            nc.vector.memset(carry[:], 0.0).then_inc(s_const, 1)
            nc.vector.memset(xT[:], 0.0).then_inc(s_const, 1)
            nc.vector.memset(eps_col[:], LN_EPS).then_inc(s_const, 1)
            nc.vector.memset(keep[:], 1.0).then_inc(s_const, 1)
            dve.wait_ge(s_const, N_CONST_POOL + 5)
            for b in range(NCHUNK // CPB):
                nc.vector.memset(keep[:, b * CPB:b * CPB + 1], 0.0).then_inc(s_const, 1)
            dve.wait_ge(s_w, 16 * (len(loads) + 3))
            for g in range(NH):
                last = nc.vector.tensor_copy(
                    wv_sb[:, g, :].rearrange("p (a j h) -> p a j h", a=NH, j=HS),
                    xm[:, 0, g, 0:C].rearrange("p (a h j) -> p a j h", a=NH, j=HS))
            last.then_inc(s_vperm, 1)
            dve.wait_ge(s_perm, NH)
            for half, bank in enumerate((pa[:, 0, :], pc)):
                nc.vector.tensor_copy(wo_sb[:, half, :], bank[:, 0:C]).then_inc(s_perm_kept, 1)
                nc.vector.tensor_copy(g_col[:, half:half + 1], bank[:, C:C + 1]).then_inc(s_perm_kept, 1)
                nc.vector.tensor_copy(b_col[:, half:half + 1], bank[:, C + 1:C + 2]).then_inc(s_perm_kept, 1)
            dve.wait_ge(s_perm_kept, 3 * NH)
            dve.wait_ge(s_vperm, 1)
            nc.vector.tensor_copy(w2_sb[:], w2_raw).then_inc(w2_set, 1)
            dve.wait_ge(w2_set, 1)
            low = slice(2 * DMIX, 3 * DMIX)
            nc.vector.tensor_tensor(w2_sb[low], x1[low], w2_sb[low].bitcast(F32), ALU.subtract
                                    ).then_inc(w2_set, 1)
            nc.vector.tensor_copy(pick_v[:], pick_raw).then_inc(pick_set, 1)
            dve.wait_ge(pick_set, 1)
            dve.wait_ge(s_const, N_CONST)

            def stage_a(i, par, s):
                if s == 0:
                    dve.tensor_scalar(keep_now[:, par:par + 1], keep[:, bass.ds(i, 1)], 1.0, None, ALU.mult
                                      ).then_inc(keep_set, 1)
                if s == AT["x1"] + 1:
                    wait_drained(dve, i, "x1")
                    wait_from(dve, a_full, stage_value(i, NA, 0))
                    dve.tensor_tensor(xx[:], xT[:, :, 0:TC], xT[:, :, 1:TC + 1], ALU.subtract).then_inc(xx_done, 1)
                    dve.wait_ge(xx_done, stage_value(i, 1, 1))
                    for h in range(NH):
                        dve.scalar_tensor_tensor(xm[:, 2, h, :], xx[:, h, :], mu_x[:, h:h + 1], xT[:, h, 1:TC + 1],
                                                 ALU.mult, ALU.add).then_inc(xxx_done, 1)
                for f, n in enumerate(MIXES):
                    for h in range(NH):
                        if s == AT[f"m{n}{h}"] + 1:
                            dve.wait_ge(a_full, stage_value(i, NA, FA[f"m{n}{h}"] + 1))
                            if n == "v":
                                dve.wait_ge(a_full, stage_value(i, NA, FA["hid"] + 1))
                            if n == "r":
                                dve.wait_ge(a_full, stage_value(i, NA, FA["dw"] + 1))
                            dve.scalar_tensor_tensor(xm[:, XM_OF[n], h, :], pa_of(f"m{n}{h}"), mu[:, f, h:h + 1],
                                                     xx[:, h, :], ALU.add, ALU.mult
                                                     ).then_inc(drained_sem(f"m{n}{h}"), 1)
                if s == AT["hid"] + 2:
                    dve.wait_ge(hid_split, stage_value(i, 2, 1))
                    dve.tensor_tensor(hid_parts[:, 1, :], hid[:], hid_parts[:, 0, :].bitcast(F32), ALU.subtract
                                      ).then_inc(hid_split, 1)
                for h in range(NH):
                    if s == AT[f"V{h}"] + 1:
                        dve.wait_ge(v_act, stage_value(i, 2 * NH, 2 * h + 2))
                        dve.tensor_tensor(v_parts[:, 1, h, :], pa_of(f"V{h}"), v_parts[:, 0, h, :].bitcast(F32),
                                          ALU.subtract).then_inc(drained_sem(f"V{h}"), 1)
                if s == AT["B0"] - 1:
                    wait_drained(dve, i, "R1")
                    for h in range(NH):
                        dve.scalar_tensor_tensor(xx[:, h, :], rT[:, par, h, :], u_col[:, h:h + 1], kT[:, par, h, :],
                                                 ALU.mult, ALU.mult).then_inc(ruk_done, 1)
                for h in range(NH):
                    if s == AT[f"B{h}"] + 1:
                        dve.wait_ge(a_full, stage_value(i, NA, FA[f"B{h}"] + 1))
                        dve.tensor_tensor(uT[:, par, h, :], pa_of(f"B{h}"), v_full[:, h, :], ALU.mult
                                          ).then_inc(drained_sem(f"B{h}"), 1)

            def chain(i, k):
                dve.wait_ge(s_dve, stage_value(i, NCH, k))

            def root(i, k, which):
                dve.wait_ge(root_done, stage_value(i, 2, which + 1))
                dve.reciprocal(rstd[:, which, :], rstd[:, which, :]).then_inc(s_dve, 1)

            def statistics(src, which, first):
                for t in range(TPC):
                    dve.bn_stats(stats[:, which, t, :], src[:, t, :]).then_inc(s_dve, 1)
                return first + TPC

            def stage_c(i, par, s):
                if s == C_AT["stat1"]:
                    dve.wait_ge(c_drained, stage_value(i, NCF, 2))
                    k = statistics(y_tok, 0, 0)
                    chain(i, k)
                    dve.sem_inc(wait_carrier, 1)
                    for t in range(TPC):
                        dve.bn_aggr(mv[:, 0, t, :], stats[:, 0, t, :]).then_inc(s_dve, 1)
                if s == C_AT["norm1"]:
                    root(i, 0, 0)
                    chain(i, 2 * TPC + 1)
                    for t in range(TPC):
                        dve.tensor_scalar(y_tok[:, t, :], y_tok[:, t, :], mv[:, 0, t, 0:1], rstd[:, 0, t:t + 1],
                                          ALU.subtract, ALU.mult).then_inc(s_dve, 1)
                for k in range(2):
                    if s == C_AT[f"z{k}"]:
                        dve.wait_ge(c_full, stage_value(i, NCF, 5 + k))
                        if k == 0:
                            dve.wait_ge(res_loaded, stage_value(i, 16, 16))
                            wait_from(dve, x1_stored, stage_value(i, 16, 0))
                            wait_from(dve, scattered, stage_value(i, 16 * 2 * TPC, 0))
                        dve.tensor_tensor(x1[:, 2 * k:2 * k + 2, :], pc[:].rearrange("p (t c) -> p t c", t=2),
                                          x_res[:, 2 * k:2 * k + 2, :], ALU.add).then_inc(c_drained, 1)
                if s == C_AT["stat2"]:
                    dve.wait_ge(c_drained, stage_value(i, NCF, 6))
                    statistics(x1, 1, 0)
                    chain(i, 4 * TPC + 1)
                    dve.sem_inc(wait_carrier, 1)
                    for t in range(TPC):
                        dve.bn_aggr(mv[:, 1, t, :], stats[:, 1, t, :]).then_inc(s_dve, 1)
                if s == C_AT["norm2"]:
                    root(i, 0, 1)
                    chain(i, 5 * TPC + 2)
                    for t in range(TPC):
                        dve.tensor_scalar(x1[:, t, :], x1[:, t, :], mv[:, 1, t, 0:1], rstd[:, 1, t:t + 1],
                                          ALU.subtract, ALU.mult).then_inc(s_dve, 1)
                if s == C_AT["top"]:
                    dve.wait_ge(c_full, stage_value(i, NCF, 9))
                    dve.tensor_tensor(logits[:], pc[:, 0:TPC * E].rearrange("p (t e) -> p t e", t=TPC),
                                      gate_bias[:, None, :].to_broadcast([P, TPC, E]), ALU.add
                                      ).then_inc(c_drained, 1)
                if s == C_AT["top"]:
                    dve.wait_ge(c_drained, stage_value(i, NCF, 9))
                    dve.sem_inc(wait_carrier, 1)
                    for t in range(TPC):
                        dve.max(top[:, t, :], logits[:, t, :]).then_inc(s_dve, 1)
                    chain(i, X1_AT + TPC)
                    dve.sem_inc(wait_carrier, 1)
                    for t in range(TPC):
                        dve.max_index(top_i[:, t, :], top[:, t, :], logits[:, t, :]).then_inc(s_dve, 1)
                    dve.tensor_tensor(gap[:], top[:, :, 1], top[:, :, 0], ALU.subtract).then_inc(s_dve, 1)
                    chain(i, GAP_AT)
                    dve.tensor_copy(top_f[:], top_i[:, :, 0:2]).then_inc(s_dve, 1)
                    chain(i, GAP_AT + 1)
                    for c in range(2):
                        dve.tensor_tensor(onehot[:, c], expert_id[:, None, :].to_broadcast([P, TPC, E]),
                                          top_f[:, :, c:c + 1].to_broadcast([P, TPC, E]), ALU.is_equal
                                          ).then_inc(s_dve, 1)
                    chain(i, GAP_AT + 3)
                    dve.tensor_tensor(hits[:], onehot[:, 0], onehot[:, 1], ALU.add).then_inc(s_dve, 1)
                if s == C_AT["place"]:
                    dve.wait_ge(c_full, stage_value(i, NCF, 10))
                    for c in range(2):
                        ins = dve.tensor_tensor(scratch[:, c], pc[:, 0:TPC * E].rearrange("p (t e) -> p t e", t=TPC),
                                                onehot[:, c], ALU.mult)
                        ins.then_inc(s_dve, 1)
                    chain(i, HITS_AT + 2)
                    dve.tensor_reduce(pos[:], scratch[:], AX.X, ALU.add).then_inc(c_drained, 1)
                    dve.wait_ge(c_drained, stage_value(i, NCF, 10))
                    for c in range(2):
                        dve.tensor_tensor(scratch[:, c], expert_base[:, None, :].to_broadcast([P, TPC, E]),
                                          onehot[:, c], ALU.mult).then_inc(s_dve, 1)
                    chain(i, HITS_AT + 4)
                    dve.tensor_reduce(base[:], scratch[:], AX.X, ALU.add).then_inc(s_dve, 1)
                    for t in range(TPC):
                        dve.tensor_tensor(seen[:], seen[:], hits[:, t, :], ALU.add).then_inc(s_dve, 1)
                        chain(i, HITS_AT + 6 + t)
                    k = HITS_AT + 5 + TPC
                    dve.tensor_scalar(valid[:], pos[:], float(CAP), None, ALU.is_lt).then_inc(s_dve, 1)
                    dve.tensor_scalar(slot_f[:], pos[:], float(CAP - 1), None, ALU.min).then_inc(s_dve, 1)
                    dve.tensor_scalar(put_f[:], pos[:], float(CAP), float(SKIP), ALU.is_ge, ALU.mult
                                      ).then_inc(s_dve, 1)
                    chain(i, k + 3)
                    dve.tensor_tensor(slot_f[:], slot_f[:], base[:], ALU.add).then_inc(s_dve, 1)
                    chain(i, k + 4)
                    dve.tensor_tensor(put_f[:], put_f[:], slot_f[:], ALU.add).then_inc(s_dve, 1)
                    chain(i, k + 5)
                    wait_from(dve, scattered, stage_value(i, 16 * 2 * TPC, 0))
                    dve.tensor_copy(put_slot[:], put_f[:].rearrange("p c t -> p t c")).then_inc(s_dve, 1)
                    dve.tensor_scalar(slot_of[:, bass.ds(i * TPC, TPC), :], slot_f[:].rearrange("p c t -> p t c"),
                                      1.0, None, ALU.mult).then_inc(s_dve, 1)
                    dve.wait_ge(ratio_done, stage_value(i, 1, 1))
                    dve.tensor_scalar(share[:, 1, :], ratio[:], 1.0, None, ALU.add).then_inc(s_dve, 1)
                    chain(i, k + 8)
                    dve.reciprocal(share[:, 0, :], share[:, 1, :]).then_inc(s_dve, 1)
                    chain(i, k + 9)
                    dve.tensor_tensor(share[:, 1, :], share[:, 0, :], ratio[:], ALU.mult).then_inc(s_dve, 1)
                    chain(i, k + 10)
                    dve.tensor_tensor(weight_of[:, bass.ds(i * TPC, TPC), :], share[:].rearrange("p c t -> p t c"),
                                      valid[:].rearrange("p c t -> p t c"), ALU.mult).then_inc(s_dve, 1)

            def sum_y_half(i, par, half):
                dve.wait_ge(reduced, stage_value(i, NQ, (half + 1) * QH))
                dve.tensor_tensor(y_sum[:, half, :], ypsum[:], uT[:, par, half, :], ALU.add
                                  ).then_inc(y_summed, 1)

            def body(i, par, do_a, do_c):
                for p in range(NPAIR):
                    half = p // (NPAIR // NH)
                    q = p // 2
                    if do_a:
                        stage_a(i + 1, 1 - par, 2 * p)
                    if p == 0:
                        wait_drained(dve, i, "R1")
                        dve.wait_ge(w_done, stage_value(i, NH, NH))
                    for g in range(2):
                        dve.wait_ge(vb_full, stage_value(i, NU, 2 * p + g + 1))
                        dve.tensor_tensor(vb[:, p % 2, g, :], vb[:, p % 2, g, :], kT[:, par, half, :], ALU.mult
                                          ).then_inc(kv_done, 1)
                    if p % 2 == 0:
                        dve.wait_ge(start_set, stage_value(i, NQ, q + 1))
                    for g in range(2):
                        line = S[:, q % RING, 2 * (p % 2) + g, :]
                        dve.wait_ge(kv_done, stage_value(i, NU, 2 * p + g + 1))
                        dve.tensor_tensor_scan(line[:, 1:TC + 1], wT[:, par, half, :], vb[:, p % 2, g, :],
                                               line[:, 0:1], ALU.mult, ALU.add).then_inc(scanned, 1)
                    if p == LAG - 1 and do_c:
                        sum_y_half(i - 1, 1 - par, 1)
                    if do_c:
                        stage_c(i - 1, 1 - par, 2 * p)
                    if do_a:
                        stage_a(i + 1, 1 - par, 2 * p + 1)
                    if do_c:
                        stage_c(i - 1, 1 - par, 2 * p + 1)
                    if p == LAG + 2 * QH - 1:
                        sum_y_half(i, par, 0)

            def last_c(i, par, s):
                if s == 0:
                    sum_y_half(i, par, 1)
                stage_c(i, par, s)

            chunks(dve, body, stage_a, last_c)

        @block.scalar
        def _(act):
            act.wait_ge(s_w, 16 * (len(loads) + 3))
            act.wait_ge(s_perm_kept, 3 * NH)
            act.wait_ge(s_const, N_CONST)

            def drain(i, name):
                act.wait_ge(a_full, stage_value(i, NA, FA[name] + 1))

            def stage_a(i, par, s):
                if isinstance(i, int) and i == 0 and s == SLOTS - 1:
                    set_start(0, 0, 0)
                if s == 0:
                    wait_from(act, mixed, stage_value(i, MIX * NH, 0))
                    wait_from(act, drained_sem("x1"), stage_value(i, NAB, FA["x1"] // 2 + 1 - NAB))
                    act.wait_ge(keep_set, stage_value(i, 1, 1))
                    act.activation(xT[:, :, 0], xT[:, :, TC], ACT.Copy, scale=keep_now[:, par:par + 1]
                                   ).then_inc(x_moved, 1)
                    act.wait_ge(x_moved, stage_value(i, 1, 1))
                for h in range(NH):
                    if s == AT[f"x{h}"]:
                        drain(i, f"x{h}")
                        act.activation(xT[:, h, 1:TC + 1], pa_of(f"x{h}"), ACT.Copy).then_inc(drained_sem(f"x{h}"), 1)
                if s == AT["hid"]:
                    drain(i, "hid")
                    wait_from(act, hid_stacked, stage_value(i, 16 * 3 * MIX, 0))
                    act.activation(hid[:], pa_of("hid"), ACT.Tanh).then_inc(drained_sem("hid"), 1)
                    wait_drained(act, i, "hid")
                    act.activation(hid_parts[:, 0, :], hid[:], ACT.Copy).then_inc(hid_split, 1)
                if s == AT["dw"]:
                    drain(i, "dw")
                    act.activation(hid_w[:], pa_of("dw")[0:DDEC, :], ACT.Tanh).then_inc(drained_sem("dw"), 1)
                for h in range(NH):
                    if s == AT[f"K{h}"]:
                        drain(i, f"K{h}")
                        wait_from(act, scanned, stage_value(i, NU, -NU) if not isinstance(i, int) else (i - 1) * NU)
                        act.activation(kT[:, par, h, :], pa_of(f"K{h}"), ACT.Copy).then_inc(drained_sem(f"K{h}"), 1)
                    if s == AT[f"V{h}"]:
                        drain(i, f"V{h}")
                        wait_from(act, v_stacked, stage_value(i, 16 * 4, 0))
                        act.activation(v_parts[:, 0, h, :], pa_of(f"V{h}"), ACT.Copy).then_inc(v_act, 1)
                        act.activation(v_full[:, h, :], pa_of(f"V{h}"), ACT.Copy).then_inc(v_act, 1)
                    if s == AT[f"e{h}"]:
                        drain(i, f"e{h}")
                        wait_from(act, w_done, stage_value(i, NH, h))
                        act.activation(hid[:], pa_of(f"e{h}"), ACT.Exp, bias=decay_col[:, h:h + 1]
                                       ).then_inc(drained_sem(f"e{h}"), 1)
                        wait_drained(act, i, f"e{h}")
                        act.activation(wT[:, par, h, :], hid[:], ACT.Exp, scale=-1.0).then_inc(w_done, 1)
                    if s == AT[f"R{h}"]:
                        drain(i, f"R{h}")
                        wait_from(act, prod_done, stage_value(i, NQ, -NQ) if not isinstance(i, int) else (i - 1) * NQ)
                        act.activation(rT[:, par, h, :], pa_of(f"R{h}"), ACT.Copy).then_inc(drained_sem(f"R{h}"), 1)

            def stage_c(i, par, s):
                for k in range(2):
                    if s == C_AT["turn"] + k:
                        act.wait_ge(c_full, stage_value(i, NCF, 1 + k))
                        if isinstance(i, int) and i == 0:
                            act.wait_ge(s_fill, 16 * -(-NSLOT // FILL))
                        act.activation(y_tok[:, 2 * k:2 * k + 2, :], pc[:].rearrange("p (t c) -> p t c", t=2),
                                       ACT.Copy).then_inc(c_drained, 1)
                    if s == C_AT["back"] + k:
                        act.wait_ge(c_full, stage_value(i, NCF, 3 + k))
                        for h in range(NH):
                            ins = act.activation(yT[:, h, 2 * k * P:(2 * k + 2) * P], pc[:, h * 2 * P:(h + 1) * 2 * P],
                                                 ACT.Identity, bias=b_col[:, h:h + 1], scale=g_col[:, h:h + 1])
                        ins.then_inc(c_drained, 1)
                    if s == C_AT["x1T"] + k:
                        act.wait_ge(c_full, stage_value(i, NCF, 7 + k))
                        act.activation(yT[:, :, 2 * k * P:(2 * k + 2) * P], pc[:].rearrange("p (h t) -> p h t", h=NH),
                                       ACT.Copy).then_inc(c_drained, 1)
                for which, name in enumerate(("root1", "root2")):
                    if s == C_AT[name]:
                        act.wait_ge(s_dve, stage_value(i, NCH, (2 * TPC, 5 * TPC + 1)[which]))
                        act.activation(rstd[:, which, :], mv[:, which, :, 1], ACT.Sqrt, bias=eps_col[:, 0:1]
                                       ).then_inc(root_done, 1)
                if s == C_AT["ratio"]:
                    act.wait_ge(s_dve, stage_value(i, NCH, GAP_AT))
                    act.activation(ratio[:], gap[:], ACT.Exp).then_inc(ratio_done, 1)

            def set_start(i, par, q):
                wait_from(act, prod_done, stage_value(i, NQ, q + 1 - RING))
                wait_from(act, carried, stage_value(i, NQ, q + 1 - NQ))
                if q == 0:
                    act.wait_ge(keep_set, stage_value(i, 1, 1))
                act.activation(S[:, q % RING, :, 0], carry[:, q, :], ACT.Copy, scale=keep_now[:, par:par + 1]
                               ).then_inc(start_set, 1)

            def save_last(i, q):
                act.wait_ge(scanned, stage_value(i, NU, QUAD * (q + 1)))
                act.wait_ge(start_set, stage_value(i, NQ, q + 1))
                act.activation(carry[:, q, :], S[:, q % RING, :, TC], ACT.Copy).then_inc(carried, 1)

            def body(i, par, do_a, do_c):
                for p in range(NPAIR):
                    q = p // 2
                    if p % 2 == 0 and q + 1 < NQ:
                        set_start(i, par, q + 1)
                    if p % 2 == 0 and q >= 1:
                        save_last(i, q - 1)
                    if do_a:
                        stage_a(i + 1, 1 - par, 2 * p)
                    if p == NPAIR - 2 and do_a:
                        set_start(i + 1, 1 - par, 0)
                    if do_c:
                        stage_c(i - 1, 1 - par, 2 * p)
                    if do_a:
                        stage_a(i + 1, 1 - par, 2 * p + 1)
                    if do_c:
                        stage_c(i - 1, 1 - par, 2 * p + 1)
                    if p == NPAIR - 1:
                        save_last(i, q)

            chunks(act, body, stage_a, stage_c)

        @block.gpsimd
        def _(pool):
            done = [0]

            def const(ins):
                done[0] += 1
                ins.then_inc(s_pool_const, 1)
                pool.wait_ge(s_pool_const, done[0])

            def indicator(t, view, conditions):
                const(pool.memset(t, 1.0))
                for pattern, start, step, comparison in conditions:
                    const(pool.affine_select(out=view, in_=view, pattern=pattern, compare_op=comparison,
                                             fill=0.0, base=start, channel_multiplier=step))

            indicator(to_jh[:], to_jh[:].rearrange("p (j h) -> p j h", h=HPH),
                      [([[-1, HS], [-HS, HPH]], 0, 1, ALU.is_equal)])
            indicator(ident[:], ident[:], [([[-1, P]], 0, 1, ALU.is_equal)])
            for part in range(2):
                rows = pick_raw[part * (P // 2):(part + 1) * (P // 2)]
                indicator(rows, rows.rearrange("p j (h i) -> p j h i", h=HPH),
                          [([[-HPH, JG], [-1, HPH], [0, HS]], 0, 1, ALU.is_equal)])
            indicator(sum_head[:], sum_head[:], [([[0, HS], [-HS, HPH]], 0, 1, ALU.is_ge),
                                                 ([[0, HS], [HS, HPH]], HS - 1, -1, ALU.is_ge)])
            sy = sum_y[:].rearrange("p a (b h) -> p a b h", h=HPH)
            indicator(sum_y[:], sy, [([[0, QUAD], [0, QUAD], [-HS, HPH]], 0, 1, ALU.is_ge),
                                     ([[0, QUAD], [0, QUAD], [HS, HPH]], HS - 1, -1, ALU.is_ge),
                                     ([[1, QUAD], [-1, QUAD], [0, HPH]], 0, 0, ALU.is_equal)])
            indicator(before[:], before[:], [([[1, P]], 0, -1, ALU.is_gt)])
            const(pool.memset(ones[:], 1.0))
            const(pool.iota(expert_id[:], pattern=[[1, E]], base=0, channel_multiplier=0,
                            allow_small_or_imprecise_dtypes=True))
            pool.iota(expert_base[:], pattern=[[CAP, E]], base=0, channel_multiplier=0,
                      allow_small_or_imprecise_dtypes=True).then_inc(s_const, N_CONST_POOL)

            def stage_a(i, par, s):
                for f, n in enumerate(MIXES):
                    for h in range(NH):
                        if s == AT[f"m{n}{h}"] + 1:
                            wait_drained(pool, i, f"m{n}{h}")
                            m = xm[:, XM_OF[n], h, :]
                            pool.tensor_tensor(m, m, xT[:, h, 1:TC + 1], ALU.add).then_inc(mixed, 1)

            def multiply(i, par, q):
                half = q // QH
                pool.wait_ge(scanned, stage_value(i, NU, QUAD * (q + 1)))
                wait_from(pool, reduced, stage_value(i, NQ, q - 1))
                pool.tensor_tensor(prod[:, q % 2], S[:, q % RING, :, 0:TC],
                                   rT[:, par, half, None, :].to_broadcast([P, QUAD, TC]), ALU.mult
                                   ).then_inc(prod_done, 1)

            def stage_c(i, par, s):
                if s == C_AT["scatter"]:
                    pool.wait_ge(s_dve, stage_value(i, NCH, PUT_AT))
                    if isinstance(i, int) and i == 0:
                        pool.wait_ge(s_fill, 16 * -(-NSLOT // FILL))
                    pool.sem_inc(wait_carrier, 1)
                    for t in range(TPC):
                        for c in range(2):
                            pool.indirect_dma_start(
                                out=xe_dram[:, :],
                                out_offset=bass.IndirectOffsetOnAxis(ap=put_slot[:, t, c:c + 1], axis=0),
                                in_=x1[:, t, :], in_offset=None, bounds_check=NSLOT - 1, oob_is_err=False
                            ).then_inc(scattered, 16)

            def body(i, par, do_a, do_c):
                for p in range(NPAIR):
                    if do_a:
                        stage_a(i + 1, 1 - par, 2 * p)
                    if do_c:
                        stage_c(i - 1, 1 - par, 2 * p)
                    if do_a:
                        stage_a(i + 1, 1 - par, 2 * p + 1)
                    if do_c:
                        stage_c(i - 1, 1 - par, 2 * p + 1)
                    if p % 2 == 1:
                        multiply(i, par, p // 2)

            pool.wait_ge(s_fill, 16 * -(-NSLOT // FILL))
            chunks(pool, body, stage_a, stage_c)
            pool.wait_ge(scattered, 16 * 2 * TPC * NCHUNK)


def experts(nc, xe_dram, ye_dram, w1, b1, w2, b2, ident):
    E, C, F = w1.shape
    CAP = xe_dram.shape[0] // E
    KC = C // P
    FC = F // P
    TILES = -(-CAP // P)
    FULL = CAP // P
    REST = CAP - FULL * P
    HC = (CAP + 1) // 2
    assert 2 * HC == CAP + 1
    TURNS = [(t, min(t + 2, TILES)) for t in range(0, TILES, 2)]
    NTURN = len(TURNS)
    TURN_AT = [2 * n + 1 for n in range(NTURN)]
    BR = E * FC // P
    HALF_F = FC // 2
    assert E % 2 == 0 and KC == 2 and TILES >= 4

    def rows_of(t):
        return min(P, CAP - t * P)

    with ExitStack() as ctx:
        def sb(name, shape, dt=F32):
            return ctx.enter_context(nc.sbuf_tensor(name, shape, dt))

        def psum(name, shape):
            return ctx.enter_context(nc.psum_tensor(name, shape, F32))

        def sem(name):
            return ctx.enter_context(nc.semaphore(name))

        b1_rows = sb("b1_rows", [P, BR, P])
        b1T = sb("b1T", [P, E, FC])
        w1_raw = sb("w1_raw", [P, KC, F])
        w2_raw = sb("w2_raw", [P, FC, C])
        w1_parts = sb("w1_parts", [P, 2, 2, KC, F], F32R)
        w2_parts = sb("w2_parts", [P, 2, 2, FC, C], F32R)
        b2_sb = sb("b2_sb", [P, 2, C])
        xe = sb("xe", [P, 2, TILES, C])
        b1_now = sb("b1_now", [P, 2, FC])
        x_parts = sb("x_parts", [P, 2, 2, KC, 2 * HC], F32R)
        h_full = sb("h_full", [P, 2, 2 * HC])
        h_parts = sb("h_parts", [P, 2, FC, 2 * HC], F32R)
        ye = sb("ye", [P, 2, TILES, C])
        turn = psum("turn", [P, 2, 512])
        up = psum("up", [P, 2, 2, 512])
        down = psum("down", [P, 2, 512])

        b1_loaded = sem("b1_loaded")
        b1_turned = sem("b1_turned")
        b1_kept = sem("b1_kept")
        x_loaded = [sem(f"xe_loaded{p}") for p in range(2)]
        w1_loaded = sem("w1_loaded")
        w2_loaded = sem("w2_loaded")
        b2_loaded = [sem(f"b2_loaded{p}") for p in range(2)]
        w1_high = sem("w1_high")
        w2_high = sem("w2_high")
        w1_low = sem("w1_low")
        w2_low = sem("w2_low")
        x_high = sem("x_high")
        h_low = sem("h_low")
        y_stored = [sem(f"y_stored{p}") for p in range(2)]
        b1_now_set = sem("b1_now_set")
        turned = sem("turned")
        turn_kept = sem("turn_kept")
        up_done = sem("up_done")
        gelu_done = sem("gelu_done")
        down_done = sem("down_done")
        y_kept = sem("y_kept")

        block = ctx.enter_context(nc.Block())

        @block.sync
        def _(sp):
            sp.dma_start(b1_rows[:], b1.rearrange("e (f p) -> (e f) p", p=P).rearrange("(r q) p -> q r p", q=P)
                         ).then_inc(b1_loaded, 16)

            def load(e, par):
                wait_from(sp, turned, stage_value(e, NTURN, -NTURN))
                at = e * CAP
                sp.dma_start(xe[:, par, 0:FULL, :], xe_dram[bass.ds(at, FULL * P), :]
                             .rearrange("(t p) c -> p t c", p=P)).then_inc(x_loaded[par], 16)
                sp.dma_start(xe[0:REST, par, FULL, :], xe_dram[bass.ds(at + FULL * P, REST), :]
                             ).then_inc(x_loaded[par], 16)
                wait_from(sp, y_kept, stage_value(e, TILES, -TILES))
                sp.dma_start(b2_sb[:, par], b2[bass.ds(e, 1)].rearrange("e c -> (e c)").partition_broadcast(P)
                             ).then_inc(b2_loaded[par], 16)
                wait_from(sp, w1_low, stage_value(e, KC, 0))
                sp.dma_start(w1_raw[:], w1[bass.ds(e, 1)].rearrange("e (k p) f -> p (e k) f", p=P)
                             ).then_inc(w1_loaded, 16)
                wait_from(sp, w2_low, stage_value(e, 2, 0))
                sp.dma_start(w2_raw[:], w2[bass.ds(e, 1)].rearrange("e (k p) c -> p (e k) c", p=P)
                             ).then_inc(w2_loaded, 16)

            load(0, 0)
            load(1, 1)
            with sp.Fori(1, E // 2) as n:
                load(2 * n, 0)
                load(2 * n + 1, 1)

        def expert_pairs(eng, body):
            body(0, 0, True)
            body(1, 1, True)
            with eng.Fori(1, E // 2 - 1) as n:
                body(2 * n, 0, True)
                body(2 * n + 1, 1, True)
            body(E - 2, 0, True)
            body(E - 1, 1, False)

        @block.tensor
        def _(pe):
            pe.wait_ge(b1_loaded, 16)
            for r in range(BR):
                last = pe.transpose(up[:, 0, 0, r * P:(r + 1) * P], b1_rows[:, r, :], ident[:])
            last.then_inc(b1_turned, 1)

            def turn_x(e, par, n):
                if n == 0:
                    pe.wait_ge(x_loaded[par], stage_value(e - par, 16, 32))
                t0, t1 = TURNS[n]
                bank = turn[:, (par * NTURN + n) % 2, :]
                wait_from(pe, turn_kept, stage_value(e, NTURN, n - 1))
                for k in range(KC):
                    for t in range(t0, t1):
                        m = rows_of(t)
                        at = k * 2 * P + (t - t0) * P
                        last = pe.transpose(bank[:, at:at + m], xe[0:m, par, t, k * P:(k + 1) * P],
                                            ident[0:m, 0:m])
                last.then_inc(turned, 1)

            PARTS = ((0, 0), (0, 1), (1, 0))

            def body(e, par, more):
                pe.wait_ge(w1_low, stage_value(e, KC, KC))
                pe.wait_ge(turn_kept, stage_value(e, NTURN, NTURN))
                for f in range(FC):
                    wait_from(pe, gelu_done, stage_value(e, 2 * FC, 2 * (f - 1)))
                    for half in range(2):
                        for k in range(KC):
                            for n, (wp, xp) in enumerate(PARTS):
                                last = pe.matmul(up[:, f % 2, half, 0:HC],
                                                 w1_parts[:, par, wp, k, f * P:(f + 1) * P],
                                                 x_parts[:, par, xp, k, half * HC:(half + 1) * HC],
                                                 start=(k, n) == (0, 0), stop=(k, n) == (KC - 1, 2))
                    last.then_inc(up_done, 1)
                    if more and f in TURN_AT:
                        turn_x(e + 1, 1 - par, TURN_AT.index(f))
                pe.wait_ge(w2_low, stage_value(e, 2, 2))
                for t in range(TILES):
                    m = rows_of(t)
                    wait_from(pe, y_kept, stage_value(e, TILES, t - 1))
                    for f in range(FC):
                        if t == 0:
                            pe.wait_ge(h_low, stage_value(e, FC, f + 1))
                        for n, (wp, hp) in enumerate(PARTS):
                            last = pe.matmul(down[0:m, (par * TILES + t) % 2, 0:C],
                                             h_parts[:, hp, f, t * P:t * P + m], w2_parts[:, par, wp, f, :],
                                             start=(f, n) == (0, 0), stop=(f, n) == (FC - 1, 2))
                    last.then_inc(down_done, 1)

            pe.wait_ge(b1_kept, 1)
            for n in range(NTURN):
                turn_x(0, 0, n)
            expert_pairs(pe, body)

        @block.scalar
        def _(act):
            act.wait_ge(b1_kept, 2)

            def store(e, par):
                act.wait_ge(y_kept, stage_value(e, TILES, TILES))
                act.dma_start(ye_dram[bass.ds(e * CAP, FULL * P), :].rearrange("(t p) c -> p t c", p=P),
                              ye[:, par, 0:FULL, :]).then_inc(y_stored[par], 16)
                act.dma_start(ye_dram[bass.ds(e * CAP + FULL * P, REST), :], ye[0:REST, par, FULL, :]
                              ).then_inc(y_stored[par], 16)

            def high_parts(e, par):
                act.wait_ge(w1_loaded, stage_value(e, 16, 16))
                for k in range(KC):
                    act.activation(w1_parts[:, par, 0, k, :], w1_raw[:, k, :], ACT.Copy).then_inc(w1_high, 1)
                act.wait_ge(w2_loaded, stage_value(e, 16, 16))
                for k in range(2):
                    act.activation(w2_parts[:, par, 0, HALF_F * k:HALF_F * (k + 1), :],
                                   w2_raw[:, HALF_F * k:HALF_F * (k + 1), :], ACT.Copy).then_inc(w2_high, 1)

            def body(e, par, more):
                for f in range(FC):
                    act.wait_ge(up_done, stage_value(e, FC, f + 1))
                    if f == 0:
                        wait_from(act, down_done, stage_value(e, TILES, 0))
                        act.wait_ge(b1_now_set, stage_value(e, 1, 1))
                    wait_from(act, h_low, stage_value(e, FC, f - 1))
                    for out in (h_full[:, f % 2, :], h_parts[:, 0, f, :]):
                        act.activation(out.rearrange("p (a b) -> p a b", a=2), up[:, f % 2, :, 0:HC],
                                       ACT.Gelu, bias=b1_now[:, par, f:f + 1]).then_inc(gelu_done, 1)
                    if f == FC // 2 and not (isinstance(e, int) and e == 0):
                        store(e - 1, 1 - par)
                if more:
                    high_parts(e + 1, 1 - par)

            high_parts(0, 0)
            expert_pairs(act, body)
            store(E - 1, 1)
            for p in range(2):
                act.wait_ge(y_stored[p], 16 * E)

        @block.vector
        def _(dve):
            nc.vector.memset(x_parts[:, :, :, :, CAP:2 * HC].bitcast(F32), 0.0).then_inc(b1_kept, 1)
            dve.wait_ge(b1_turned, 1)
            nc.vector.tensor_copy(b1T[:].rearrange("p e f -> p (e f)"), up[:, 0, 0, 0:BR * P]).then_inc(b1_kept, 1)
            dve.wait_ge(b1_kept, 2)

            def keep_turned(e, par, n):
                t0, t1 = TURNS[n]
                dve.wait_ge(turned, stage_value(e, NTURN, n + 1))
                bank = turn[:, (par * NTURN + n) % 2, :].rearrange("p (k t) -> p k t", k=KC)
                cols = min(t1 * P, CAP) - t0 * P
                high, low = (x_parts[:, par, part, :, t0 * P:t0 * P + cols] for part in range(2))
                dve.tensor_copy(high, bank[:, :, 0:cols]).then_inc(x_high, 1)
                dve.wait_ge(x_high, stage_value(e, NTURN, n + 1))
                dve.tensor_tensor(low, bank[:, :, 0:cols], high.bitcast(F32), ALU.subtract).then_inc(turn_kept, 1)

            def low_w1(e, par, k):
                dve.wait_ge(w1_high, stage_value(e, KC, k + 1))
                dve.tensor_tensor(w1_parts[:, par, 1, k, :], w1_raw[:, k, :], w1_parts[:, par, 0, k, :].bitcast(F32),
                                  ALU.subtract).then_inc(w1_low, 1)

            def low_w2(e, par, k):
                rows = slice(HALF_F * k, HALF_F * (k + 1))
                dve.wait_ge(w2_high, stage_value(e, 2, k + 1))
                dve.tensor_tensor(w2_parts[:, par, 1, rows, :], w2_raw[:, rows, :],
                                  w2_parts[:, par, 0, rows, :].bitcast(F32), ALU.subtract).then_inc(w2_low, 1)

            def body(e, par, more):
                wait_from(dve, gelu_done, stage_value(e, 2 * FC, -2 * FC))
                dve.tensor_scalar(b1_now[:, par, :], b1T[:, bass.ds(e, 1), :].rearrange("p e f -> p (e f)"),
                                  1.0, None, ALU.mult).then_inc(b1_now_set, 1)
                for f in range(FC):
                    dve.wait_ge(gelu_done, stage_value(e, 2 * FC, 2 * (f + 1)))
                    dve.tensor_tensor(h_parts[:, 1, f, :], h_full[:, f % 2, :], h_parts[:, 0, f, :].bitcast(F32),
                                      ALU.subtract).then_inc(h_low, 1)
                    if more and f in TURN_AT:
                        keep_turned(e + 1, 1 - par, TURN_AT.index(f))
                dve.wait_ge(b2_loaded[par], stage_value(e - par, 8, 16))
                wait_from(dve, y_stored[par], stage_value(e - par, 16, 0))
                for t in range(TILES):
                    m = rows_of(t)
                    dve.wait_ge(down_done, stage_value(e, TILES, t + 1))
                    dve.tensor_tensor(ye[0:m, par, t, :], down[0:m, (par * TILES + t) % 2, 0:C], b2_sb[0:m, par, :],
                                      ALU.add).then_inc(y_kept, 1)
                    if more and t < 4:
                        (low_w1 if t < 2 else low_w2)(e + 1, 1 - par, t % 2)

            for n in range(NTURN):
                keep_turned(0, 0, n)
            for k in range(2):
                low_w1(0, 0, k)
            for k in range(2):
                low_w2(0, 0, k)
            expert_pairs(dve, body)


def combine(nc, x1_dram, ye_dram, out_rows, slot_of, weight_of):
    NTOK, C = x1_dram.shape
    GT = 4
    GROUPS = NTOK // (GT * P)
    assert GROUPS % 2 == 0

    with ExitStack() as ctx:
        def sb(name, shape, dt=F32):
            return ctx.enter_context(nc.sbuf_tensor(name, shape, dt))

        def sem(name):
            return ctx.enter_context(nc.semaphore(name))

        place = sb("place", [P, 2, GT, 2], U32)
        weight = sb("weight", [P, 2, GT, 2])
        rows = sb("rows", [P, 2, GT, 2, C])
        acc = sb("acc", [P, 2, GT, C])
        stats = sb("c_stats", [P, 2, GT, 6])
        mv = sb("c_mv", [P, 2, GT, 2])
        rstd = sb("c_rstd", [P, 2, GT])
        eps_col = sb("c_eps", [P, 1])

        eps_set = sem("eps_set")
        wait_carrier = sem("c_wait_carrier")
        picked = sem("picked")
        gathered = [sem(f"gathered{p}") for p in range(2)]
        x1_loaded = [sem(f"x1_loaded{p}") for p in range(2)]
        stored = [sem(f"stored{p}") for p in range(2)]
        step = sem("c_step")
        rooted = sem("rooted")

        ACC_AT = 2 * GT
        STAT_AT = 4 * GT
        OUT_AT = 5 * GT + 1
        NSTEP = OUT_AT

        def groups(eng, body):
            body(0, 0)
            body(1, 1)
            with eng.Fori(1, GROUPS // 2) as n:
                body(2 * n, 0)
                body(2 * n + 1, 1)

        block = ctx.enter_context(nc.Block())

        @block.gpsimd
        def _(pool):
            def body(g, par):
                pool.wait_ge(picked, stage_value(g, 2, 2))
                wait_from(pool, step, stage_value(g, NSTEP, -NSTEP))
                pool.sem_inc(wait_carrier, 1)
                for t in range(GT):
                    for c in range(2):
                        pool.indirect_dma_start(
                            out=rows[:, par, t, c, :], out_offset=None, in_=ye_dram[:, :],
                            in_offset=bass.IndirectOffsetOnAxis(ap=place[:, par, t, c:c + 1], axis=0)
                        ).then_inc(gathered[par], 16)

            groups(pool, body)

        @block.sync
        def _(sp):
            def load(g, par):
                wait_from(sp, stored[par], stage_value(g - par, 8, 0))
                sp.dma_start(acc[:, par], x1_dram[bass.ds(g * (GT * P), GT * P), :]
                             .rearrange("(t p) c -> p t c", p=P)).then_inc(x1_loaded[par], 16)

            def store(g, par):
                sp.wait_ge(step, stage_value(g, NSTEP, OUT_AT))
                sp.dma_start(out_rows[bass.ds(g * (GT * P), GT * P), :].rearrange("(t p) c -> p t c", p=P),
                             acc[:, par]).then_inc(stored[par], 16)

            load(0, 0)
            load(1, 1)
            store(0, 0)
            with sp.Fori(1, GROUPS // 2) as n:
                load(2 * n, 0)
                store(2 * n - 1, 1)
                load(2 * n + 1, 1)
                store(2 * n, 0)
            store(GROUPS - 1, 1)
            for p in range(2):
                sp.wait_ge(stored[p], 8 * GROUPS)

        @block.scalar
        def _(act):
            act.wait_ge(eps_set, 1)

            def body(g, par):
                act.wait_ge(step, stage_value(g, NSTEP, STAT_AT))
                act.activation(rstd[:, par, :], mv[:, par, :, 1], ACT.Sqrt, bias=eps_col[:, 0:1]
                               ).then_inc(rooted, 1)

            groups(act, body)

        @block.vector
        def _(dve):
            nc.vector.memset(eps_col[:], LN_EPS).then_inc(eps_set, 1)

            def pick(g, par):
                wait_from(dve, gathered[par], stage_value(g - par, 16 * GT, 0))
                dve.tensor_scalar(place[:, par], slot_of[:, bass.ds(g * GT, GT), :], 0, None, ALU.bitwise_or
                                  ).then_inc(picked, 1)
                dve.tensor_scalar(weight[:, par], weight_of[:, bass.ds(g * GT, GT), :], 1.0, None, ALU.mult
                                  ).then_inc(picked, 1)

            def body(g, par, more=True):
                if more:
                    pick(g + 1, 1 - par)
                dve.wait_ge(x1_loaded[par], stage_value(g - par, 8, 16))
                dve.wait_ge(gathered[par], stage_value(g - par, 16 * GT, 32 * GT))
                dve.wait_ge(picked, stage_value(g, 2, 2))
                for c in range(2):
                    if c:
                        dve.wait_ge(step, stage_value(g, NSTEP, GT))
                    for t in range(GT):
                        dve.scalar_tensor_tensor(acc[:, par, t, :], rows[:, par, t, c, :], weight[:, par, t, c:c + 1],
                                                 acc[:, par, t, :], ALU.mult, ALU.add).then_inc(step, 1)
                dve.wait_ge(step, stage_value(g, NSTEP, ACC_AT))
                for t in range(GT):
                    dve.bn_stats(stats[:, par, t, :], acc[:, par, t, :]).then_inc(step, 1)
                dve.wait_ge(step, stage_value(g, NSTEP, 3 * GT))
                dve.sem_inc(wait_carrier, 1)
                for t in range(GT):
                    dve.bn_aggr(mv[:, par, t, :], stats[:, par, t, :]).then_inc(step, 1)
                dve.wait_ge(rooted, stage_value(g, 1, 1))
                dve.reciprocal(rstd[:, par, :], rstd[:, par, :]).then_inc(step, 1)
                dve.wait_ge(step, stage_value(g, NSTEP, STAT_AT + 1))
                for t in range(GT):
                    dve.tensor_scalar(acc[:, par, t, :], acc[:, par, t, :], mv[:, par, t, 0:1], rstd[:, par, t:t + 1],
                                      ALU.subtract, ALU.mult).then_inc(step, 1)

            pick(0, 0)
            body(0, 0)
            body(1, 1)
            with dve.Fori(1, GROUPS // 2 - 1) as n:
                body(2 * n, 0)
                body(2 * n + 1, 1)
            body(GROUPS - 2, 0)
            body(GROUPS - 1, 1, False)


_INS = ["L0_attn_x", "L0_attn_time_maa_x", "L0_attn_time_maa_w", "L0_attn_time_maa_k", "L0_attn_time_maa_v",
        "L0_attn_time_maa_r", "L0_attn_time_maa_w1", "L0_attn_time_maa_w2", "L0_attn_time_decay",
        "L0_attn_time_decay_w1", "L0_attn_time_decay_w2", "L0_attn_time_faaaa", "L0_attn_W_r", "L0_attn_W_k",
        "L0_attn_W_v", "L0_attn_W_o", "L0_attn_ln_g", "L0_attn_ln_b", "L0_ffn_gate_w", "L0_ffn_gate_b",
        "L0_ffn_w1", "L0_ffn_b1", "L0_ffn_w2", "L0_ffn_b2"]


def kernel(**inputs):
    import numpy as _np
    import concourse.bacc as _bacc
    from concourse import mybir as _mybir
    from concourse.bass_utils import run_bass_kernel_spmd as _run

    nc = _bacc.Bacc("TRN2", target_bir_lowering=False, num_devices=1)
    arrays, args = {}, []
    for name in _INS:
        a = _np.ascontiguousarray(inputs[name])
        arrays[f"in_{name}_dram"] = a
        args.append(nc.dram_tensor(f"in_{name}_dram", a.shape, _mybir.dt.from_np(a.dtype), kind="ExternalInput").ap())
    shape = arrays["in_L0_attn_x_dram"].shape
    out = nc.dram_tensor("out_0_dram", shape, _mybir.dt.float32, kind="ExternalOutput").ap()
    rwkv_moe(nc, *args, out)
    r = _run(nc, [arrays], core_ids=[0])
    return r.results[0]["out_0_dram"]
```

```python
from contextlib import ExitStack

import concourse.bass as bass
from concourse import mybir

F32 = mybir.dt.float32
BF16 = mybir.dt.bfloat16
F32R = mybir.dt.float32r
U32 = mybir.dt.uint32
ALU = mybir.AluOpType
ACT = mybir.ActivationFunctionType
AX = mybir.AxisListType

P = 128
BATCH = 2
LN_EPS = 1e-5
ROW_AT, WEIGHTS_AT, EXPERTS_AT, FIELDS = 0, 1, 3, 5


def stage_value(index, per_stage, within):
    return index * per_stage + within


def wait_from(eng, sem, value):
    if not isinstance(value, int) or value > 0:
        eng.wait_ge(sem, value)


def rwkv_moe(nc, x, maa_x, maa_w, maa_k, maa_v, maa_r, maa_w1, maa_w2, decay, decay_w1, decay_w2,
             faaaa, W_r, W_k, W_v, W_o, ln_g, ln_b, gate_w, gate_b, w1, b1, w2, b2, out):
    B, T, C = x.shape
    E = gate_w.shape[1]
    NTOK = B * T
    NSLOT = E * expert_slots(NTOK, E)
    assert B == BATCH

    x_rows = x.rearrange("b t c -> (b t) c")
    out_rows = out.rearrange("b t c -> (b t) c")
    sums = nc.dram_tensor("sums", (spare_rows(NTOK, E) + NTOK, C), F32, kind="Internal").ap()
    xe_dram = nc.dram_tensor("expert_in_rows", (NSLOT, C + FIELDS), F32, kind="Internal").ap()

    whole = ExitStack()
    with whole:
        def keep_sb(name, shape, dt):
            return whole.enter_context(nc.sbuf_tensor(name, shape, dt))

        ident = keep_sb("ident", [P, P], F32)
        b1_rows = keep_sb("b1_rows", [P, E * b1.shape[1] // (P * P), P], F32)
        w1_raw = keep_sb("w1_raw", [P, C // P, w1.shape[2]], F32)
        b1_loaded, w1_loaded = (whole.enter_context(nc.semaphore(name)) for name in ("b1_loaded", "w1_loaded"))

        def load_w1(sp, e):
            sp.dma_start(w1_raw[:], w1[bass.ds(e, 1)].rearrange("e (k p) f -> p (e k) f", p=P)
                         ).then_inc(w1_loaded, 16)

        def first_loads(sp):
            sp.dma_start(b1_rows[:], b1.rearrange("e (f p) -> (e f) p", p=P).rearrange("(r q) p -> q r p", q=P)
                         ).then_inc(b1_loaded, 16)
            load_w1(sp, 0)

        time_mix(nc, x_rows, sums, xe_dram, maa_x, maa_w, maa_k, maa_v, maa_r, maa_w1, maa_w2, decay,
                 decay_w1, decay_w2, faaaa, W_r, W_k, W_v, W_o, ln_g, ln_b, gate_w, gate_b, ident,
                 first_loads)
        experts(nc, xe_dram, sums, w2, b2, ident, b1_rows, b1_loaded, w1_raw, w1_loaded, load_w1)
        last_norm(nc, sums, out_rows)


def expert_slots(tokens, n_experts):
    return -(-tokens * 2 * 12 // (n_experts * 10))


def spare_rows(tokens, n_experts):
    return -(-expert_slots(tokens, n_experts) // P) * P


def time_mix(nc, x_rows, sums, xe_dram, maa_x, maa_w, maa_k, maa_v, maa_r, maa_w1, maa_w2, decay,
             decay_w1, decay_w2, faaaa, W_r, W_k, W_v, W_o, ln_g, ln_b, gate_w, gate_b, ident,
             first_loads):
    NTOK, C = x_rows.shape
    H, HS = faaaa.shape
    MIX, DMIX, _ = maa_w2.shape
    DDEC = decay_w1.shape[1]
    E = gate_w.shape[1]
    NH = C // P
    HPH = P // HS
    TC = 512
    NCHUNK = NTOK // TC
    CPB = NCHUNK // BATCH
    TPC = TC // P
    NU = NH * HS
    QUAD = 4
    NQ = NU // QUAD
    QH = NQ // NH
    NPAIR = NU // 2
    LAG = 4
    RING = 4
    JG = HS // 2
    SLOTS = 2 * NPAIR
    CAP = expert_slots(NTOK, E)
    NSLOT = E * CAP
    SPARE = spare_rows(NTOK, E)
    SKIP = 1 << 20
    assert NCHUNK % 2 == 0 and MIX * DMIX == P and NSLOT < SKIP

    with ExitStack() as ctx:
        def sb(name, shape, dt=F32):
            return ctx.enter_context(nc.sbuf_tensor(name, shape, dt))

        def psum(name, shape):
            return ctx.enter_context(nc.psum_tensor(name, shape, F32))

        def sem(name):
            return ctx.enter_context(nc.semaphore(name))

        mu_x = sb("mu_x", [P, NH])
        mu = sb("mu", [P, MIX, NH])
        u_col = sb("u_col", [P, NH])
        decay_col = sb("decay_col", [P, NH])
        g_col = sb("g_col", [P, NH])
        b_col = sb("b_col", [P, NH])
        eps_col = sb("eps_col", [P, 1])
        w1_sb = sb("maa_w1_sb", [P, NH, P])
        w1_before = sb("w1_before", [P, NH, P])
        w2_sb = sb("maa_w2_sb", [P, 2, MIX, C], F32R)
        dw1_sb = sb("dw1_sb", [P, NH, DDEC])
        dw2_sb = sb("dw2_sb", [DDEC, C])
        wr_sb = sb("wr_sb", [P, NH, C])
        wk_sb = sb("wk_sb", [P, NH, C])
        wv_sb = sb("wv_sb", [P, NH, C])
        wo_sb = sb("wo_sb", [P, NH, C])
        gate_sb = sb("gate_sb", [P, NH, E])
        gate_bias = sb("gate_bias", [P, E])
        pick_v = sb("pick_v", [P, JG, P], F32R)
        sum_y = sb("sum_y", [P, QUAD, 32])
        sum_head = sb("sum_head", [P, HS, HPH])
        sum_own = sb("sum_own", [P, NH, P])
        before = sb("before", [P, P], BF16)
        ones = sb("ones", [P, P], BF16)
        expert_id = sb("expert_id", [P, E])
        keep = sb("keep", [P, NCHUNK])
        keep_now = sb("keep_now", [P, 2])
        x_tok = sb("x_tok", [P, TPC, C])
        xT = sb("xT", [P, NH, TC + 1])
        xx = sb("xx", [P, NH, TC])
        xm = sb("xm", [P, 3, NH, TC])
        hid = sb("hid", [P, TC])
        hid_parts = sb("hid_parts", [P, 2, TC], F32R)
        hid_w = sb("hid_w", [DDEC, TC])
        to_jh = sb("to_jh", [P, P])
        v_full = sb("v_full", [P, NH, TC])
        wT = sb("wT", [P, 2, NH, TC])
        kT = sb("kT", [P, 2, NH, TC])
        rT = sb("rT", [P, 2, NH, TC])
        uT = sb("uT", [P, 2, NH, TC])
        v_parts = sb("v_parts", [P, 2, NH, TC], F32R)
        v_stack = sb("v_stack", [P, 2, NH, 2, TC], F32R)
        S = sb("S", [P, RING, QUAD, TC + 1])
        carry = sb("carry", [P, NQ, QUAD])
        prod = sb("prod", [P, 2, QUAD, TC])
        y_sum = sb("y_sum", [P, NH, TC])
        yT = sb("yT", [P, NH, TC])
        y_tok = sb("y_tok", [P, TPC, C])
        x_res = sb("x_res", [P, TPC, C])
        x1_row = sb("x1_row", [P, TPC, C + FIELDS])
        stats = sb("stats", [P, 2, TPC, 6])
        mv = sb("mv", [P, 2, TPC, 2])
        rstd = sb("rstd", [P, 2, TPC])
        offset = sb("offset", [P, 2, TPC])
        logits = sb("logits", [P, TPC, E])
        top = sb("top", [P, TPC, 8])
        top_i = sb("top_i", [P, TPC, 8], U32)
        onehot = sb("onehot", [P, 2, TPC, E])
        hits = sb("hits", [P, TPC, E], BF16)
        seen = sb("seen", [P, E], BF16)
        scratch = sb("scratch", [P, 2, TPC, E])
        pos = sb("pos", [P, 2, TPC])
        fresh = sb("fresh", [P, E])
        sum_row = sb("sum_row", [P, TPC])
        slot_f = sb("slot_f", [P, TPC, 2])
        past = sb("past", [P, 2, TPC])
        put_slot = sb("put_slot", [P, TPC, 2], U32)
        gap = sb("gap", [P, TPC])
        ratio = sb("ratio", [P, TPC])
        one_more = sb("one_more", [P, TPC])

        vb = psum("vb", [P, 2, 2, TC])
        ypsum = psum("ypsum", [P, TC])
        pa = psum("pa", [P, 2, TC])
        pc = psum("pc", [P, TC])

        s_const = sem("s_const")
        pick_set = sem("pick_set")
        w2_set = sem("w2_set")
        v_high = sem("v_high")
        v_low = sem("v_low")
        hid_split = sem("hid_split")
        v_stacked = sem("v_stacked")
        wo_kept = sem("wo_kept")
        wo_ordered = sem("wo_ordered")
        pool_const = sem("pool_const")
        s_w = sem("s_w")
        wv_ordered = sem("wv_ordered")
        s_zero = sem("s_zero")
        s_fill = sem("s_fill")
        x_loaded = sem("x_loaded")
        a_full = sem("a_full")
        a_drained = [sem(f"a_drained{b}") for b in range(2)]
        x_moved = sem("x_moved")
        keep_set = sem("keep_set")
        carried = sem("carried")
        wait_carrier = sem("wait_carrier")
        xx_done = sem("xx_done")
        w1_set = sem("w1_set")
        own_set = sem("own_set")
        mixed = sem("mixed")
        w_done = sem("w_done")
        rk_done = sem("rk_done")
        vb_full = sem("vb_full")
        kv_done = sem("kv_done")
        scanned = sem("scanned")
        start_set = sem("start_set")
        prod_done = sem("prod_done")
        reduced = sem("reduced")
        y_full = sem("y_full")
        y_summed = sem("y_summed")
        c_full = sem("c_full")
        c_drained = sem("c_drained")
        res_loaded = sem("res_loaded")
        x1_stored = sem("x1_stored")
        s_dve = sem("s_dve")
        root_done = sem("root_done")
        normed = sem("normed")
        ratio_done = sem("ratio_done")
        scattered = sem("scattered")

        x1 = x1_row[:, :, 0:C]
        row_experts = x1_row[:, :, C + EXPERTS_AT:C + EXPERTS_AT + 2]
        row_weights = x1_row[:, :, C + WEIGHTS_AT:C + WEIGHTS_AT + 2]
        pick_raw = xm[:, 2].rearrange("p h t -> p (h t)").rearrange("p (j m) -> p j m", m=P)
        zeros = y_tok[:].rearrange("p q c -> p (q c)")
        w2_raw = x1[:, 0, :]
        wo_raw = xm[:, 1]

        def per_chan(v):
            return v.rearrange("(h p) -> p h", p=P)

        loads = [
            (mu_x[:], per_chan(maa_x[0, 0])),
            (mu[:, 0, :], per_chan(maa_w[0, 0])),
            (mu[:, 1, :], per_chan(maa_k[0, 0])),
            (mu[:, 2, :], per_chan(maa_v[0, 0])),
            (mu[:, 3, :], per_chan(maa_r[0, 0])),
            (decay_col[:], per_chan(decay[0, 0])),
            (u_col[:], per_chan(faaaa.rearrange("h i -> (h i)"))),
            (w1_sb[:], maa_w1.rearrange("(h p) n -> p h n", p=P)),
            (dw1_sb[:], decay_w1.rearrange("(h p) n -> p h n", p=P)),
            (dw2_sb[:], decay_w2),
            (w2_raw, maa_w2.rearrange("f d c -> (f d) c")),
            (wr_sb[:], W_r.rearrange("(h p) n -> p h n", p=P)),
            (wk_sb[:], W_k.rearrange("(h p) n -> p h n", p=P)),
            (xm[:, 0, :, 0:C], W_v.rearrange("(h p) n -> p h n", p=P)),
            (gate_sb[:], gate_w.rearrange("(h p) n -> p h n", p=P)),
            (gate_bias[:], gate_b.partition_broadcast(P)),
            (wo_raw[:, :, 0:C], W_o.rearrange("(h p) n -> p h n", p=P)),
            (wo_raw[:, :, C], per_chan(ln_g)),
            (wo_raw[:, :, C + 1], per_chan(ln_b)),
        ]
        FQ = 15
        FILL = FQ * P
        FILLS = -(-NSLOT // FILL) + 1
        assert NSLOT % FQ == 0
        AT = {"x0": 0, "x1": 1, "hid": 2, "mw0": 5, "mw1": 6, "mk0": 7, "mk1": 8, "mv0": 9, "mv1": 10, "dw": 11,
              "K0": 12, "K1": 13, "V0": 15, "V1": 16, "mr0": 18, "mr1": 19, "e0": 20, "e1": 21, "R0": 23, "R1": 24,
              "B0": 27, "B1": 28}
        FA = {name: k for k, name in enumerate(AT)}
        LATER = {"hid": 3, "V": 3, "B": 3}
        NA = len(FA)
        NAB = NA // 2
        assert NA % 2 == 0
        MIXES = ["w", "k", "v", "r"]
        XM_OF = {"w": 0, "k": 1, "v": 2, "r": 0}
        C_AT = {"turn": 6, "stat1": 9, "root1": 11, "norm1": 11, "back": 14, "wo0": 17, "z0": 18, "wo1": 19,
                "z1": 20, "stat2": 21, "root2": 22, "norm2": 23, "x1T": 25, "gate": 27, "top": 28, "ratio": 28,
                "count": 30, "place": 30, "scatter": 31}
        NCF = 10
        LN1_AT = 2 * TPC + 2
        X1_AT = LN1_AT + 2 * TPC + 2
        GAP_AT = X1_AT + 2 * TPC + 1
        HITS_AT = GAP_AT + 4
        PUT_AT = HITS_AT + 12
        NCH = PUT_AT
        N_CONST_POOL = 1
        N_CONST = N_CONST_POOL + 5 + NCHUNK // CPB

        def pa_of(name):
            return pa[:, FA[name] % 2, :]

        def drained_sem(name):
            return a_drained[FA[name] % 2]

        def wait_drained(eng, i, name):
            wait_from(eng, drained_sem(name), stage_value(i, NAB, FA[name] // 2 + 1))

        block = ctx.enter_context(nc.Block())

        @block.sync
        def _(sp):
            sp.dma_start(x_tok[:], x_rows[0:TC, :].rearrange("(q p) c -> p q c", p=P)).then_inc(x_loaded, 16)
            for to, of in loads[0::2]:
                sp.dma_start(to, of, allow_slow_non_contiguous=True).then_inc(s_w, 16)

            def stack_v(i, par):
                sp.wait_ge(v_low, stage_value(i, NH, NH))
                for part in range(2):
                    for g in range(2):
                        sp.dma_start(v_stack[part * (P // 2):(part + 1) * (P // 2), par, :, g, :].bitcast(F32),
                                     v_parts[g * (P // 2):(g + 1) * (P // 2), part, :, :].bitcast(F32)
                                     ).then_inc(v_stacked, 16)

            def chunk_io(i, par, do_a, do_c, more_x=True):
                if do_c:
                    wait_from(sp, c_drained, stage_value(i - 1, NCF, 0) if isinstance(i, int)
                              else stage_value(i, NCF, -NCF))
                    sp.dma_start(x_res[:], x_rows[bass.ds(i * TC - TC, TC), :].rearrange("(q p) c -> p q c", p=P)
                                 ).then_inc(res_loaded, 16)
                if do_a:
                    if more_x:
                        sp.wait_ge(a_full, stage_value(i + 1, NA, NH))
                        sp.dma_start(x_tok[:], x_rows[bass.ds(i * TC + 2 * TC, TC), :]
                                     .rearrange("(q p) c -> p q c", p=P)).then_inc(x_loaded, 16)
                    stack_v(i + 1, 1 - par)
                if do_c:
                    store_x1(i - 1)

            def store_x1(c):
                sp.wait_ge(normed, stage_value(c, 2 * TPC, 2 * TPC))
                sp.dma_start(sums[bass.ds(SPARE + c * TC, TC), :].rearrange("(q p) c -> p q c", p=P), x1
                             ).then_inc(x1_stored, 16)

            sp.wait_ge(a_full, NH)
            sp.dma_start(x_tok[:], x_rows[TC:2 * TC, :].rearrange("(q p) c -> p q c", p=P)).then_inc(x_loaded, 16)
            stack_v(0, 0)
            sp.wait_ge(s_zero, 1)
            for row in range(0, NSLOT, FILL):
                n = min(FILL, NSLOT - row)
                rows = xe_dram[row:row + n, :]
                sp.dma_start(rows.rearrange("(p q) c -> p q c", q=FQ),
                             zeros[0:n // FQ, None, 0:C + FIELDS].to_broadcast([n // FQ, FQ, C + FIELDS])
                             ).then_inc(s_fill, 16)
            sp.dma_start(sums[0:SPARE, :].rearrange("(p q) c -> p q c", p=P),
                         zeros[:, None, 0:C].to_broadcast([P, SPARE // P, C])).then_inc(s_fill, 16)
            chunk_io(0, 0, True, False)
            chunk_io(1, 1, True, True)
            chunk_io(2, 0, True, True)
            with sp.Fori(1, NCHUNK // 2 - 2) as n:
                chunk_io(2 * n + 1, 1, True, True)
                chunk_io(2 * n + 2, 0, True, True)
            chunk_io(NCHUNK - 3, 1, True, True)
            chunk_io(NCHUNK - 2, 0, True, True, False)
            first_loads(sp)
            chunk_io(NCHUNK - 1, 1, False, True)
            sp.wait_ge(c_drained, stage_value(NCHUNK - 1, NCF, 0))
            sp.dma_start(x_res[:], x_rows[NTOK - TC:NTOK, :]
                         .rearrange("(q p) c -> p q c", p=P)).then_inc(res_loaded, 16)
            store_x1(NCHUNK - 1)
            sp.wait_ge(x1_stored, 16 * NCHUNK)

        def chunks(eng, body, stage_a, stage_c):
            for s in range(SLOTS):
                stage_a(0, 0, s)
            body(0, 0, True, False)
            body(1, 1, True, True)
            body(2, 0, True, True)
            with eng.Fori(1, NCHUNK // 2 - 1) as n:
                body(2 * n + 1, 1, True, True)
                body(2 * n + 2, 0, True, True)
            body(NCHUNK - 1, 1, False, True)
            for s in range(SLOTS + 1):
                stage_c(NCHUNK - 1, 1, s)

        @block.tensor
        def _(pe):
            pe.wait_ge(s_const, N_CONST)
            pe.wait_ge(s_w, 16 * len(loads))
            for half, bank in enumerate((pa[:, 0, :], pc)):
                pe.matmul(bank[:, 0:C + 2], to_jh[:], wo_raw[:, half, 0:C + 2], start=True, stop=True
                          ).then_inc(wo_ordered, 1)
            pe.wait_ge(wo_kept, 3 * NH)
            pe.wait_ge(wv_ordered, 1)
            pe.wait_ge(w1_set, NH + 1)
            pe.wait_ge(own_set, NH)
            pe.wait_ge(w2_set, 2 * MIX + 1)
            pe.wait_ge(pick_set, 1)

            def a_fill(i, name):
                wait_from(pe, drained_sem(name), stage_value(i, NAB, FA[name] // 2))

            def stage_a(i, par, s):
                if s == AT["x0"]:
                    pe.wait_ge(x_loaded, stage_value(i, 16, 16))
                for h in range(NH):
                    if s == AT[f"x{h}"]:
                        a_fill(i, f"x{h}")
                        for q in range(TPC):
                            last = pe.transpose(pa_of(f"x{h}")[:, q * P:(q + 1) * P], x_tok[:, q, h * P:(h + 1) * P],
                                                ident[:])
                        last.then_inc(a_full, 1)
                if s == AT["hid"]:
                    a_fill(i, "hid")
                    wait_drained(pe, i, "x1")
                    wait_drained(pe, i, "x0")
                    pe.wait_ge(x_moved, stage_value(i, 1, 1))
                    for h in range(NH):
                        pe.matmul(pa_of("hid"), w1_sb[:, h, :], xT[:, h, 1:TC + 1], start=h == 0, stop=False)
                    for h in range(NH):
                        last = pe.matmul(pa_of("hid"), w1_before[:, h, :], xT[:, h, 0:TC], start=False,
                                         stop=h == NH - 1)
                    last.then_inc(a_full, 1)
                for f, n in enumerate(MIXES):
                    for h in range(NH):
                        if s == AT[f"m{n}{h}"]:
                            a_fill(i, f"m{n}{h}")
                            for k, (wp, hp) in enumerate(((0, 0), (1, 0), (0, 1))):
                                if f == 0 and h == 0 and k != 1:
                                    pe.wait_ge(hid_split, stage_value(i, 2, 1 + hp))
                                last = pe.matmul(pa_of(f"m{n}{h}"), w2_sb[:, wp, f, h * P:(h + 1) * P],
                                                 hid_parts[:, hp, :], start=k == 0, stop=k == 2)
                            last.then_inc(a_full, 1)
                if s == AT["dw"]:
                    a_fill(i, "dw")
                    pe.wait_ge(mixed, stage_value(i, MIX * NH, NH))
                    for h in range(NH):
                        last = pe.matmul(pa_of("dw")[0:DDEC, :], dw1_sb[:, h, :], xm[:, XM_OF["w"], h, :],
                                         start=h == 0, stop=h == NH - 1)
                    last.then_inc(a_full, 1)
                for n, w_sb, order in (("K", wk_sb, 1), ("V", wv_sb, 2), ("R", wr_sb, 3)):
                    for h in range(NH):
                        if s == AT[f"{n}{h}"]:
                            a_fill(i, f"{n}{h}")
                            pe.wait_ge(mixed, stage_value(i, MIX * NH, (order + 1) * NH))
                            for g in range(NH):
                                last = pe.matmul(pa_of(f"{n}{h}"), w_sb[:, g, h * P:(h + 1) * P],
                                                 xm[:, XM_OF[n.lower()], g, :], start=g == 0, stop=g == NH - 1)
                            last.then_inc(a_full, 1)
                for h in range(NH):
                    if s == AT[f"e{h}"]:
                        a_fill(i, f"e{h}")
                        pe.matmul(pa_of(f"e{h}"), dw2_sb[:, h * P:(h + 1) * P], hid_w[:], start=True, stop=True
                                  ).then_inc(a_full, 1)
                    if s == AT[f"B{h}"]:
                        a_fill(i, f"B{h}")
                        pe.wait_ge(rk_done, stage_value(i, NH, h + 1))
                        pe.matmul(pa_of(f"B{h}"), sum_own[:, h, :], xx[:, h, :],
                                  start=True, stop=True).then_inc(a_full, 1)

            def c_fill(i, k):
                wait_from(pe, c_drained, stage_value(i, NCF, k))

            def stage_c(i, par, s):
                for k in range(2):
                    if s == C_AT["turn"] + k:
                        c_fill(i, k)
                        pe.wait_ge(y_summed, stage_value(i, NH, NH))
                        for t in range(2):
                            for h in range(NH):
                                last = pe.transpose(pc[:, t * C + h * P:t * C + (h + 1) * P],
                                                    y_sum[:, h, (2 * k + t) * P:(2 * k + t + 1) * P], ident[:])
                        last.then_inc(c_full, 1)
                    if s == C_AT["back"] + k:
                        c_fill(i, 2 + k)
                        pe.wait_ge(normed, stage_value(i, 2 * TPC, TPC))
                        for h in range(NH):
                            for t in range(2):
                                last = pe.transpose(pc[:, h * 2 * P + t * P:h * 2 * P + (t + 1) * P],
                                                    y_tok[:, 2 * k + t, h * P:(h + 1) * P], ident[:])
                        last.then_inc(c_full, 1)
                    if s == C_AT[f"wo{k}"]:
                        c_fill(i, 4 + k)
                        for t in range(2):
                            for h in range(NH):
                                at = (2 * k + t) * P
                                last = pe.matmul(pc[:, t * C:(t + 1) * C], yT[:, h, at:at + P],
                                                 wo_sb[:, h, :], start=h == 0, stop=h == NH - 1)
                        last.then_inc(c_full, 1)
                    if s == C_AT["x1T"] + k:
                        c_fill(i, 6 + k)
                        pe.wait_ge(normed, stage_value(i, 2 * TPC, 2 * TPC))
                        for h in range(NH):
                            for t in range(2):
                                last = pe.transpose(pc[:, h * 2 * P + t * P:h * 2 * P + (t + 1) * P],
                                                    x1[:, 2 * k + t, h * P:(h + 1) * P], ident[:])
                        last.then_inc(c_full, 1)
                if s == C_AT["gate"]:
                    c_fill(i, 8)
                    for t in range(TPC):
                        for h in range(NH):
                            last = pe.matmul(pc[:, t * E:(t + 1) * E], yT[:, h, t * P:(t + 1) * P],
                                             gate_sb[:, h, :], start=h == 0, stop=h == NH - 1)
                    last.then_inc(c_full, 1)
                if s == C_AT["count"]:
                    c_fill(i, 9)
                    pe.wait_ge(s_dve, stage_value(i, NCH, HITS_AT))
                    for t in range(TPC):
                        pe.matmul(pc[:, t * E:(t + 1) * E], ones[:], seen[:], start=True, stop=False)
                        for b in range(t):
                            pe.matmul(pc[:, t * E:(t + 1) * E], ones[:], hits[:, b, :], start=False, stop=False)
                        last = pe.matmul(pc[:, t * E:(t + 1) * E], before[:], hits[:, t, :], start=False, stop=True)
                    last.then_inc(c_full, 1)

            def spread_v(i, par, p):
                half, jj, g0 = p // (NPAIR // NH), (p % (NPAIR // NH)) // 2, 2 * (p % 2)
                wait_from(pe, scanned, stage_value(i, NU, 2 * p - 2))
                if p == 0:
                    pe.wait_ge(v_stacked, stage_value(i, 16 * 4, 16 * 4))
                for g in range(2):
                    j = (g0 + g) * QH + jj
                    pe.matmul(vb[:, p % 2, g, :], pick_v[:, j % JG, :], v_stack[:, par, half, j // JG, :],
                              start=True, stop=True).then_inc(vb_full, 1)

            def reduce_y(i, par, q):
                half, jj = q // QH, q % QH
                pe.wait_ge(prod_done, stage_value(i, NQ, q + 1))
                if jj == 0:
                    wait_from(pe, y_summed, stage_value(i, NH, half))
                for g in range(QUAD):
                    last = pe.matmul(ypsum[32 * g:32 * g + 32, :], sum_y[:, jj, :], prod[:, q % 2, g, :],
                                     start=jj == 0, stop=False)
                last.then_inc(reduced, 1)
                if jj == QH - 1:
                    wait_drained(pe, i, f"B{half}")
                    pe.matmul(ypsum[:], ident[:], uT[:, par, half, :], start=False, stop=True).then_inc(y_full, 1)

            def body(i, par, do_a, do_c):
                for p in range(NPAIR):
                    if p + 1 < NPAIR:
                        spread_v(i, par, p + 1)
                    elif do_a:
                        spread_v(i + 1, 1 - par, 0)
                    if do_a:
                        stage_a(i + 1, 1 - par, 2 * p)
                    if p in (LAG - 4, LAG - 2) and do_c:
                        reduce_y(i - 1, 1 - par, NQ + (p - LAG) // 2)
                    if p >= LAG and p % 2 == 0:
                        reduce_y(i, par, (p - LAG) // 2)
                    if do_c:
                        stage_c(i - 1, 1 - par, 2 * p)
                    if do_a:
                        stage_a(i + 1, 1 - par, 2 * p + 1)
                    if do_c:
                        stage_c(i - 1, 1 - par, 2 * p + 1)

            def last_c(i, par, s):
                if s == 0:
                    for q in (NQ - 2, NQ - 1):
                        reduce_y(i, par, q)
                stage_c(i, par, s)

            def first_a(i, par, s):
                stage_a(i, par, s)
                if s == SLOTS - 1:
                    spread_v(i, par, 0)

            chunks(pe, body, first_a, last_c)

        @block.vector
        def _(dve):
            nc.vector.memset(zeros, 0.0).then_inc(s_zero, 1)
            nc.vector.memset(seen[:], 0.0).then_inc(s_const, 1)
            nc.vector.memset(carry[:], 0.0).then_inc(s_const, 1)
            nc.vector.memset(xT[:], 0.0).then_inc(s_const, 1)
            nc.vector.memset(eps_col[:], LN_EPS).then_inc(s_const, 1)
            nc.vector.memset(keep[:], 1.0).then_inc(s_const, 1)
            dve.wait_ge(s_const, N_CONST_POOL + 5)
            for b in range(NCHUNK // CPB):
                nc.vector.memset(keep[:, b * CPB:b * CPB + 1], 0.0).then_inc(s_const, 1)
            dve.wait_ge(s_w, 16 * len(loads))
            for g in range(NH):
                last = nc.vector.tensor_copy(
                    wv_sb[:, g, :].rearrange("p (a j h) -> p a j h", a=NH, j=HS),
                    xm[:, 0, g, 0:C].rearrange("p (a h j) -> p a j h", a=NH, j=HS))
            last.then_inc(wv_ordered, 1)
            dve.wait_ge(wo_ordered, NH)
            for half, bank in enumerate((pa[:, 0, :], pc)):
                nc.vector.tensor_copy(wo_sb[:, half, :], bank[:, 0:C]).then_inc(wo_kept, 1)
                nc.vector.tensor_copy(g_col[:, half:half + 1], bank[:, C:C + 1]).then_inc(wo_kept, 1)
                nc.vector.tensor_copy(b_col[:, half:half + 1], bank[:, C + 1:C + 2]).then_inc(wo_kept, 1)
            dve.wait_ge(wo_kept, 3 * NH)
            dve.wait_ge(wv_ordered, 1)
            dve.wait_ge(s_const, N_CONST)
            for h in range(NH):
                nc.vector.tensor_scalar(sum_own[:, h, :], sum_head[:].rearrange("p j h -> p (j h)"),
                                        u_col[:, h:h + 1], None, ALU.mult).then_inc(own_set, 1)
            for h in range(NH):
                nc.vector.tensor_scalar(w1_before[:, h, :], w1_sb[:, h, :], mu_x[:, h:h + 1], None, ALU.mult
                                        ).then_inc(w1_set, 1)
            dve.wait_ge(w1_set, NH)
            nc.vector.tensor_tensor(w1_sb[:], w1_sb[:], w1_before[:], ALU.subtract).then_inc(w1_set, 1)
            nc.vector.memset(w2_sb[:].bitcast(F32), 0.0).then_inc(w2_set, 1)
            dve.wait_ge(w2_set, 1)
            blocks = [slice(f * DMIX, (f + 1) * DMIX) for f in range(MIX)]
            for f, rows in enumerate(blocks):
                nc.vector.tensor_copy(w2_sb[rows, 0, f, :], w2_raw[rows]).then_inc(w2_set, 1)
            dve.wait_ge(w2_set, MIX + 1)
            for f, rows in enumerate(blocks):
                nc.vector.tensor_tensor(w2_sb[rows, 1, f, :], w2_raw[rows], w2_sb[rows, 0, f, :].bitcast(F32),
                                        ALU.subtract).then_inc(w2_set, 1)
            nc.vector.tensor_copy(pick_v[:], pick_raw).then_inc(pick_set, 1)
            dve.wait_ge(pick_set, 1)
            dve.wait_ge(s_const, N_CONST)

            def stage_a(i, par, s):
                if s == 0:
                    dve.tensor_scalar(keep_now[:, par:par + 1], keep[:, bass.ds(i, 1)], 1.0, None, ALU.mult
                                      ).then_inc(keep_set, 1)
                if s == AT["x1"] + 1:
                    wait_drained(dve, i, "x1")
                    wait_from(dve, a_full, stage_value(i, NA, 0))
                    dve.tensor_tensor(xx[:], xT[:, :, 0:TC], xT[:, :, 1:TC + 1], ALU.subtract).then_inc(xx_done, 1)
                for f, n in enumerate(MIXES):
                    for h in range(NH):
                        if s == AT[f"m{n}{h}"] + 1:
                            dve.wait_ge(xx_done, stage_value(i, 1, 1))
                            dve.wait_ge(a_full, stage_value(i, NA, FA[f"m{n}{h}"] + 1))
                            if n == "r":
                                dve.wait_ge(a_full, stage_value(i, NA, FA["dw"] + 1))
                            dve.scalar_tensor_tensor(xm[:, XM_OF[n], h, :], pa_of(f"m{n}{h}"), mu[:, f, h:h + 1],
                                                     xx[:, h, :], ALU.add, ALU.mult
                                                     ).then_inc(drained_sem(f"m{n}{h}"), 1)
                if s == AT["hid"] + LATER["hid"]:
                    dve.wait_ge(hid_split, stage_value(i, 2, 1))
                    dve.tensor_tensor(hid_parts[:, 1, :], hid[:], hid_parts[:, 0, :].bitcast(F32), ALU.subtract
                                      ).then_inc(hid_split, 1)
                for h in range(NH):
                    if s == AT[f"V{h}"] + LATER["V"]:
                        dve.wait_ge(v_high, stage_value(i, NH, h + 1))
                        wait_drained(dve, i, f"V{h}")
                        dve.tensor_tensor(v_parts[:, 1, h, :], v_full[:, h, :], v_parts[:, 0, h, :].bitcast(F32),
                                          ALU.subtract).then_inc(v_low, 1)
                for h in range(NH):
                    if s == AT[f"B{h}"] + LATER["B"]:
                        dve.wait_ge(a_full, stage_value(i, NA, FA[f"B{h}"] + 1))
                        dve.tensor_tensor(uT[:, par, h, :], pa_of(f"B{h}"), v_full[:, h, :], ALU.mult
                                          ).then_inc(drained_sem(f"B{h}"), 1)

            def chain(i, k):
                dve.wait_ge(s_dve, stage_value(i, NCH, k))

            def invert(i, k, which):
                dve.wait_ge(root_done, stage_value(i, 2, which + 1))
                dve.reciprocal(rstd[:, which, :], rstd[:, which, :]).then_inc(s_dve, 1)
                chain(i, k + 1)
                dve.scalar_tensor_tensor(offset[:, which, :], mv[:, which, :, 0], -1.0, rstd[:, which, :],
                                         ALU.mult, ALU.mult).then_inc(s_dve, 1)

            def statistics(src, which):
                for t in range(TPC):
                    dve.bn_stats(stats[:, which, t, :], src[:, t, :]).then_inc(s_dve, 1)

            def stage_c(i, par, s):
                if s == C_AT["stat1"]:
                    dve.wait_ge(c_drained, stage_value(i, NCF, 2))
                    statistics(y_tok, 0)
                    chain(i, TPC)
                    dve.sem_inc(wait_carrier, 1)
                    for t in range(TPC):
                        dve.bn_aggr(mv[:, 0, t, :], stats[:, 0, t, :]).then_inc(s_dve, 1)
                if s == C_AT["norm1"]:
                    invert(i, LN1_AT - 2, 0)
                for k in range(2):
                    if s == C_AT[f"z{k}"]:
                        dve.wait_ge(c_full, stage_value(i, NCF, 5 + k))
                        if k == 0:
                            dve.wait_ge(res_loaded, stage_value(i, 16, 16))
                            wait_from(dve, x1_stored, stage_value(i, 16, 0))
                            wait_from(dve, scattered, stage_value(i, 16 * 2 * TPC, 0))
                        dve.tensor_tensor(x1[:, 2 * k:2 * k + 2, :], pc[:].rearrange("p (t c) -> p t c", t=2),
                                          x_res[:, 2 * k:2 * k + 2, :], ALU.add).then_inc(c_drained, 1)
                if s == C_AT["stat2"]:
                    dve.wait_ge(c_drained, stage_value(i, NCF, 6))
                    statistics(x1, 1)
                    chain(i, LN1_AT + TPC)
                    dve.sem_inc(wait_carrier, 1)
                    for t in range(TPC):
                        dve.bn_aggr(mv[:, 1, t, :], stats[:, 1, t, :]).then_inc(s_dve, 1)
                if s == C_AT["norm2"]:
                    invert(i, X1_AT - 2, 1)
                if s == C_AT["top"]:
                    dve.wait_ge(c_full, stage_value(i, NCF, 9))
                    dve.tensor_tensor(logits[:], pc[:, 0:TPC * E].rearrange("p (t e) -> p t e", t=TPC),
                                      gate_bias[:, None, :].to_broadcast([P, TPC, E]), ALU.add
                                      ).then_inc(c_drained, 1)
                if s == C_AT["top"]:
                    dve.wait_ge(c_drained, stage_value(i, NCF, 9))
                    dve.sem_inc(wait_carrier, 1)
                    for t in range(TPC):
                        dve.max(top[:, t, :], logits[:, t, :]).then_inc(s_dve, 1)
                    chain(i, X1_AT + TPC)
                    dve.sem_inc(wait_carrier, 1)
                    for t in range(TPC):
                        dve.max_index(top_i[:, t, :], top[:, t, :], logits[:, t, :]).then_inc(s_dve, 1)
                    dve.tensor_tensor(gap[:], top[:, :, 1], top[:, :, 0], ALU.subtract).then_inc(s_dve, 1)
                    chain(i, GAP_AT)
                    dve.tensor_copy(row_experts, top_i[:, :, 0:2]).then_inc(s_dve, 1)
                    chain(i, GAP_AT + 1)
                    for c in range(2):
                        dve.tensor_tensor(onehot[:, c], expert_id[:, None, :].to_broadcast([P, TPC, E]),
                                          row_experts[:, :, c:c + 1].to_broadcast([P, TPC, E]), ALU.is_equal
                                          ).then_inc(s_dve, 1)
                    chain(i, GAP_AT + 3)
                    dve.tensor_tensor(hits[:], onehot[:, 0], onehot[:, 1], ALU.add).then_inc(s_dve, 1)
                if s == C_AT["place"]:
                    dve.wait_ge(c_full, stage_value(i, NCF, 10))
                    for c in range(2):
                        dve.tensor_tensor(scratch[:, c], pc[:, 0:TPC * E].rearrange("p (t e) -> p t e", t=TPC),
                                          onehot[:, c], ALU.mult).then_inc(s_dve, 1)
                    dve.tensor_reduce(fresh[:], hits[:].rearrange("p t e -> p e t"), AX.X, ALU.add).then_inc(s_dve, 1)
                    chain(i, HITS_AT + 3)
                    dve.tensor_reduce(pos[:], scratch[:], AX.X, ALU.add).then_inc(c_drained, 1)
                    dve.tensor_tensor(seen[:], seen[:], fresh[:], ALU.add).then_inc(s_dve, 1)
                    dve.wait_ge(ratio_done, stage_value(i, 1, 1))
                    dve.tensor_scalar(one_more[:], ratio[:], 1.0, None, ALU.add).then_inc(s_dve, 1)
                    chain(i, HITS_AT + 5)
                    dve.reciprocal(row_weights[:, :, 0], one_more[:]).then_inc(s_dve, 1)
                    dve.wait_ge(c_drained, stage_value(i, NCF, 10))
                    dve.tensor_scalar(past[:], pos[:], float(CAP), float(SKIP), ALU.is_ge, ALU.mult
                                      ).then_inc(s_dve, 1)
                    dve.scalar_tensor_tensor(slot_f[:], row_experts, float(CAP), pos[:].rearrange("p c t -> p t c"),
                                             ALU.mult, ALU.add).then_inc(s_dve, 1)
                    chain(i, HITS_AT + 6)
                    dve.tensor_tensor(row_weights[:, :, 1], row_weights[:, :, 0], ratio[:], ALU.mult
                                      ).then_inc(s_dve, 1)
                    dve.tensor_copy(x1_row[:, :, C + ROW_AT], sum_row[:]).then_inc(s_dve, 1)
                    dve.tensor_scalar(sum_row[:], sum_row[:], float(TC), None, ALU.add).then_inc(s_dve, 1)
                    wait_from(dve, scattered, stage_value(i, 16 * 2 * TPC, 0))
                    chain(i, HITS_AT + 8)
                    dve.tensor_tensor(put_slot[:], slot_f[:], past[:].rearrange("p c t -> p t c"), ALU.add
                                      ).then_inc(s_dve, 1)

            def body(i, par, do_a, do_c):
                for p in range(NPAIR):
                    half = p // (NPAIR // NH)
                    q = p // 2
                    if do_a:
                        stage_a(i + 1, 1 - par, 2 * p)
                    if p == 0:
                        wait_drained(dve, i, "R1")
                        dve.wait_ge(w_done, stage_value(i, NH, NH))
                    for g in range(2):
                        dve.wait_ge(vb_full, stage_value(i, NU, 2 * p + g + 1))
                        dve.tensor_tensor(vb[:, p % 2, g, :], vb[:, p % 2, g, :], kT[:, par, half, :], ALU.mult
                                          ).then_inc(kv_done, 1)
                    if p % 2 == 0:
                        dve.wait_ge(start_set, stage_value(i, NQ, q + 1))
                    for g in range(2):
                        line = S[:, q % RING, 2 * (p % 2) + g, :]
                        dve.wait_ge(kv_done, stage_value(i, NU, 2 * p + g + 1))
                        dve.tensor_tensor_scan(line[:, 1:TC + 1], wT[:, par, half, :], vb[:, p % 2, g, :],
                                               line[:, 0:1], ALU.mult, ALU.add).then_inc(scanned, 1)
                    if do_c:
                        stage_c(i - 1, 1 - par, 2 * p)
                    if do_a:
                        stage_a(i + 1, 1 - par, 2 * p + 1)
                    if do_c:
                        stage_c(i - 1, 1 - par, 2 * p + 1)

            chunks(dve, body, stage_a, stage_c)

        @block.scalar
        def _(act):
            for to, of in loads[1::2]:
                act.dma_start(to, of, allow_slow_non_contiguous=True).then_inc(s_w, 16)
            act.wait_ge(s_w, 16 * len(loads))
            act.wait_ge(wo_kept, 3 * NH)
            act.wait_ge(s_const, N_CONST)

            def drain(i, name):
                act.wait_ge(a_full, stage_value(i, NA, FA[name] + 1))

            def stage_a(i, par, s):
                if isinstance(i, int) and i == 0 and s == SLOTS - 1:
                    set_start(0, 0, 0)
                if s == 0:
                    wait_from(act, mixed, stage_value(i, MIX * NH, 0))
                    wait_from(act, drained_sem("x1"), stage_value(i, NAB, FA["x1"] // 2 + 1 - NAB))
                    act.wait_ge(keep_set, stage_value(i, 1, 1))
                    act.activation(xT[:, :, 0], xT[:, :, TC], ACT.Copy, scale=keep_now[:, par:par + 1]
                                   ).then_inc(x_moved, 1)
                    act.wait_ge(x_moved, stage_value(i, 1, 1))
                for h in range(NH):
                    if s == AT[f"x{h}"]:
                        drain(i, f"x{h}")
                        act.activation(xT[:, h, 1:TC + 1], pa_of(f"x{h}"), ACT.Copy).then_inc(drained_sem(f"x{h}"), 1)
                if s == AT["hid"]:
                    drain(i, "hid")
                    act.activation(hid[:], pa_of("hid"), ACT.Tanh).then_inc(drained_sem("hid"), 1)
                    wait_drained(act, i, "hid")
                    act.activation(hid_parts[:, 0, :], hid[:], ACT.Copy).then_inc(hid_split, 1)
                if s == AT["dw"]:
                    drain(i, "dw")
                    act.activation(hid_w[:], pa_of("dw")[0:DDEC, :], ACT.Tanh).then_inc(drained_sem("dw"), 1)
                for h in range(NH):
                    if s == AT[f"K{h}"]:
                        drain(i, f"K{h}")
                        wait_from(act, scanned, stage_value(i, NU, -NU) if not isinstance(i, int) else (i - 1) * NU)
                        act.activation(kT[:, par, h, :], pa_of(f"K{h}"), ACT.Copy).then_inc(drained_sem(f"K{h}"), 1)
                    if s == AT[f"V{h}"]:
                        drain(i, f"V{h}")
                        wait_from(act, v_stacked, stage_value(i, 16 * 4, 0))
                        act.activation(v_parts[:, 0, h, :], pa_of(f"V{h}"), ACT.Copy).then_inc(v_high, 1)
                        act.activation(v_full[:, h, :], pa_of(f"V{h}"), ACT.Copy).then_inc(drained_sem(f"V{h}"), 1)
                    if s == AT[f"e{h}"]:
                        drain(i, f"e{h}")
                        wait_from(act, w_done, stage_value(i, NH, h))
                        act.activation(hid[:], pa_of(f"e{h}"), ACT.Exp, bias=decay_col[:, h:h + 1]
                                       ).then_inc(drained_sem(f"e{h}"), 1)
                        wait_drained(act, i, f"e{h}")
                        act.activation(wT[:, par, h, :], hid[:], ACT.Exp, scale=-1.0).then_inc(w_done, 1)
                    if s == AT[f"R{h}"]:
                        drain(i, f"R{h}")
                        wait_from(act, prod_done, stage_value(i, NQ, -NQ) if not isinstance(i, int) else (i - 1) * NQ)
                        act.activation(rT[:, par, h, :], pa_of(f"R{h}"), ACT.Copy).then_inc(drained_sem(f"R{h}"), 1)

            def stage_c(i, par, s):
                for k in range(2):
                    if s == C_AT["turn"] + k:
                        act.wait_ge(c_full, stage_value(i, NCF, 1 + k))
                        if isinstance(i, int) and i == 0:
                            act.wait_ge(s_fill, 16 * FILLS)
                        act.activation(y_tok[:, 2 * k:2 * k + 2, :], pc[:].rearrange("p (t c) -> p t c", t=2),
                                       ACT.Copy).then_inc(c_drained, 1)
                    if s == C_AT["back"] + k:
                        act.wait_ge(c_full, stage_value(i, NCF, 3 + k))
                        for h in range(NH):
                            ins = act.activation(yT[:, h, 2 * k * P:(2 * k + 2) * P], pc[:, h * 2 * P:(h + 1) * 2 * P],
                                                 ACT.Identity, bias=b_col[:, h:h + 1], scale=g_col[:, h:h + 1])
                        ins.then_inc(c_drained, 1)
                    if s == C_AT["x1T"] + k:
                        act.wait_ge(c_full, stage_value(i, NCF, 7 + k))
                        act.activation(yT[:, :, 2 * k * P:(2 * k + 2) * P], pc[:].rearrange("p (h t) -> p h t", h=NH),
                                       ACT.Copy).then_inc(c_drained, 1)
                for which, name in enumerate(("root1", "root2")):
                    if s == C_AT[name]:
                        act.wait_ge(s_dve, stage_value(i, NCH, (2 * TPC, LN1_AT + 2 * TPC)[which]))
                        act.activation(rstd[:, which, :], mv[:, which, :, 1], ACT.Sqrt, bias=eps_col[:, 0:1]
                                       ).then_inc(root_done, 1)
                for which, (name, rows, ready) in enumerate((("norm1", y_tok, LN1_AT), ("norm2", x1, X1_AT))):
                    if s == C_AT[name]:
                        act.wait_ge(s_dve, stage_value(i, NCH, ready))
                        for t in range(TPC):
                            act.activation(rows[:, t, :], rows[:, t, :], ACT.Identity, bias=offset[:, which, t:t + 1],
                                           scale=rstd[:, which, t:t + 1]).then_inc(normed, 1)
                if s == C_AT["ratio"]:
                    act.wait_ge(s_dve, stage_value(i, NCH, GAP_AT))
                    act.activation(ratio[:], gap[:], ACT.Exp).then_inc(ratio_done, 1)

            def set_start(i, par, q):
                wait_from(act, prod_done, stage_value(i, NQ, q + 1 - RING))
                wait_from(act, carried, stage_value(i, NQ, q + 1 - NQ))
                if q == 0:
                    act.wait_ge(keep_set, stage_value(i, 1, 1))
                act.activation(S[:, q % RING, :, 0], carry[:, q, :], ACT.Copy, scale=keep_now[:, par:par + 1]
                               ).then_inc(start_set, 1)

            def save_last(i, q):
                act.wait_ge(scanned, stage_value(i, NU, QUAD * (q + 1)))
                act.wait_ge(start_set, stage_value(i, NQ, q + 1))
                act.activation(carry[:, q, :], S[:, q % RING, :, TC], ACT.Copy).then_inc(carried, 1)

            def keep_y(i, half):
                act.wait_ge(y_full, stage_value(i, NH, half + 1))
                act.activation(y_sum[:, half, :], ypsum[:], ACT.Copy).then_inc(y_summed, 1)

            def body(i, par, do_a, do_c):
                for p in range(NPAIR):
                    q = p // 2
                    if p == LAG - 1 and do_c:
                        keep_y(i - 1, 1)
                    if p == LAG + 2 * QH:
                        keep_y(i, 0)
                    if p % 2 == 0 and q + 1 < NQ:
                        set_start(i, par, q + 1)
                    if p % 2 == 0 and q >= 1:
                        save_last(i, q - 1)
                    if do_a:
                        stage_a(i + 1, 1 - par, 2 * p)
                    if p == NPAIR - 2 and do_a:
                        set_start(i + 1, 1 - par, 0)
                    if do_c:
                        stage_c(i - 1, 1 - par, 2 * p)
                    if do_a:
                        stage_a(i + 1, 1 - par, 2 * p + 1)
                    if do_c:
                        stage_c(i - 1, 1 - par, 2 * p + 1)
                    if p == NPAIR - 1:
                        save_last(i, q)

            def last_c(i, par, s):
                if s == 0:
                    keep_y(i, 1)
                stage_c(i, par, s)

            chunks(act, body, stage_a, last_c)

        @block.gpsimd
        def _(pool):
            done = [0]

            def const(ins):
                done[0] += 1
                ins.then_inc(pool_const, 1)
                pool.wait_ge(pool_const, done[0])

            def indicator(t, view, conditions):
                const(pool.memset(t, 1.0))
                for pattern, start, step, comparison in conditions:
                    const(pool.affine_select(out=view, in_=view, pattern=pattern, compare_op=comparison,
                                             fill=0.0, base=start, channel_multiplier=step))

            indicator(to_jh[:], to_jh[:].rearrange("p (j h) -> p j h", h=HPH),
                      [([[-1, HS], [-HS, HPH]], 0, 1, ALU.is_equal)])
            indicator(ident[:], ident[:], [([[-1, P]], 0, 1, ALU.is_equal)])
            for part in range(2):
                rows = pick_raw[part * (P // 2):(part + 1) * (P // 2)]
                indicator(rows, rows.rearrange("p j (h i) -> p j h i", h=HPH),
                          [([[-HPH, JG], [-1, HPH], [0, HS]], 0, 1, ALU.is_equal)])
            indicator(sum_head[:], sum_head[:], [([[0, HS], [-HS, HPH]], 0, 1, ALU.is_ge),
                                                 ([[0, HS], [HS, HPH]], HS - 1, -1, ALU.is_ge)])
            sy = sum_y[:].rearrange("p a (b h) -> p a b h", h=HPH)
            indicator(sum_y[:], sy, [([[0, QUAD], [0, QUAD], [-HS, HPH]], 0, 1, ALU.is_ge),
                                     ([[0, QUAD], [0, QUAD], [HS, HPH]], HS - 1, -1, ALU.is_ge),
                                     ([[1, QUAD], [-1, QUAD], [0, HPH]], 0, 0, ALU.is_equal)])
            indicator(before[:], before[:], [([[1, P]], 0, -1, ALU.is_gt)])
            const(pool.memset(ones[:], 1.0))
            const(pool.iota(expert_id[:], pattern=[[1, E]], base=0, channel_multiplier=0,
                            allow_small_or_imprecise_dtypes=True))
            pool.iota(sum_row[:], pattern=[[P, TPC]], base=SPARE, channel_multiplier=1,
                      allow_small_or_imprecise_dtypes=True).then_inc(s_const, 1)

            def stage_a(i, par, s):
                for f, n in enumerate(MIXES):
                    for h in range(NH):
                        if s == AT[f"m{n}{h}"] + 1:
                            wait_drained(pool, i, f"m{n}{h}")
                            m = xm[:, XM_OF[n], h, :]
                            pool.tensor_tensor(m, m, xT[:, h, 1:TC + 1], ALU.add).then_inc(mixed, 1)
                for h in range(NH):
                    if s == AT[f"R{h}"] + 1:
                        wait_drained(pool, i, f"R{h}")
                        pool.tensor_tensor(xx[:, h, :], rT[:, par, h, :], kT[:, par, h, :], ALU.mult
                                           ).then_inc(rk_done, 1)

            def multiply(i, par, q):
                half = q // QH
                pool.wait_ge(scanned, stage_value(i, NU, QUAD * (q + 1)))
                wait_from(pool, reduced, stage_value(i, NQ, q - 1))
                pool.tensor_tensor(prod[:, q % 2], S[:, q % RING, :, 0:TC],
                                   rT[:, par, half, None, :].to_broadcast([P, QUAD, TC]), ALU.mult
                                   ).then_inc(prod_done, 1)

            def stage_c(i, par, s):
                if s == C_AT["scatter"]:
                    pool.wait_ge(s_dve, stage_value(i, NCH, PUT_AT))
                    if isinstance(i, int) and i == 0:
                        pool.wait_ge(s_fill, 16 * FILLS)
                    pool.sem_inc(wait_carrier, 1)
                    for t in range(TPC):
                        for c in range(2):
                            pool.indirect_dma_start(
                                out=xe_dram[:, :],
                                out_offset=bass.IndirectOffsetOnAxis(ap=put_slot[:, t, c:c + 1], axis=0),
                                in_=x1_row[:, t, :], in_offset=None, bounds_check=NSLOT - 1, oob_is_err=False
                            ).then_inc(scattered, 16)

            def body(i, par, do_a, do_c):
                for p in range(NPAIR):
                    if do_a:
                        stage_a(i + 1, 1 - par, 2 * p)
                    if do_c:
                        stage_c(i - 1, 1 - par, 2 * p)
                    if do_a:
                        stage_a(i + 1, 1 - par, 2 * p + 1)
                    if p % 2 == 1:
                        multiply(i, par, p // 2)
                    if do_c:
                        stage_c(i - 1, 1 - par, 2 * p + 1)

            chunks(pool, body, stage_a, stage_c)
            pool.wait_ge(scattered, 16 * 2 * TPC * NCHUNK)


def experts(nc, xe_dram, sums, w2, b2, ident, b1_rows, b1_loaded, w1_raw, w1_loaded, load_w1):
    E, F, C = w2.shape
    CAP = xe_dram.shape[0] // E
    NSUM = sums.shape[0]
    KC = C // P
    FC = F // P
    TILES = -(-CAP // P)
    FULL = CAP // P
    REST = CAP - FULL * P
    HC = (CAP + 1) // 2
    assert 2 * HC == CAP + 1
    TURNS = [(t, min(t + 2, TILES)) for t in range(0, TILES, 2)]
    NTURN = len(TURNS)
    NSLOT_STEPS = 5
    TURN_AT = [2 * n + 1 for n in range(NTURN)]
    BR = E * FC // P
    HALF_F = FC // 2
    assert E % 2 == 0 and KC == 2 and TILES >= 4

    def rows_of(t):
        return min(P, CAP - t * P)

    with ExitStack() as ctx:
        def sb(name, shape, dt=F32):
            return ctx.enter_context(nc.sbuf_tensor(name, shape, dt))

        def psum(name, shape):
            return ctx.enter_context(nc.psum_tensor(name, shape, F32))

        def sem(name):
            return ctx.enter_context(nc.semaphore(name))

        b1T = sb("b1T", [P, E, FC])
        w2_raw = sb("w2_raw", [P, FC, C])
        w1_parts = sb("w1_parts", [P, 2, 2, KC, F], F32R)
        w2_parts = sb("w2_parts", [P, 2, 2, FC, C], F32R)
        b2_sb = sb("b2_sb", [P, 2, C])
        xe = sb("xe", [P, 2, TILES, C + FIELDS])
        expert_id = sb("expert_no", [P, E])
        expert_now = sb("expert_now", [P, 1])
        spare = sb("spare", [P, TILES])
        spare_now = sb("spare_now", [P, TILES])
        shares = sb("shares", [P, TILES, 2])
        weight = sb("weight", [P, 2, TILES])
        sum_at = sb("sum_at", [P, 2, TILES], U32)
        b1_now = sb("b1_now", [P, 2, FC])
        x_parts = sb("x_parts", [P, 2, 2, KC, 2 * HC], F32R)
        h_full = sb("h_full", [P, 2, 2 * HC])
        h_parts = sb("h_parts", [P, 2, FC, 2 * HC], F32R)
        ye = sb("ye", [P, 2, TILES, C])
        turn = psum("turn", [P, 2, 512])
        up = psum("up", [P, 2, 2, 512])
        down = psum("down", [P, 2, 512])

        b1_turned = sem("b1_turned")
        b1_kept = sem("b1_kept")
        x_loaded = [sem(f"xe_loaded{p}") for p in range(2)]
        w2_loaded = sem("w2_loaded")
        b2_loaded = [sem(f"b2_loaded{p}") for p in range(2)]
        w1_high = sem("w1_high")
        w2_high = sem("w2_high")
        w1_low = sem("w1_low")
        w2_low = sem("w2_low")
        x_high = sem("x_high")
        h_low = sem("h_low")
        ids_set = sem("ids_set")
        fields_cleared = sem("fields_cleared")
        slots_read = sem("slots_read")
        y_weighed = sem("y_weighed")
        added = sem("added")
        wait_carrier = sem("e_wait_carrier")
        b1_now_set = sem("b1_now_set")
        turned = sem("turned")
        turn_kept = sem("turn_kept")
        up_done = sem("up_done")
        gelu_done = sem("gelu_done")
        down_done = sem("down_done")
        y_kept = sem("y_kept")

        block = ctx.enter_context(nc.Block())

        @block.sync
        def _(sp):
            def load(e, par):
                wait_from(sp, turned, stage_value(e, NTURN, -NTURN))
                wait_from(sp, slots_read, stage_value(e, NSLOT_STEPS, -NSLOT_STEPS))
                at = e * CAP
                sp.dma_start(xe[:, par, 0:FULL, :], xe_dram[bass.ds(at, FULL * P), :]
                             .rearrange("(t p) c -> p t c", p=P)).then_inc(x_loaded[par], 16)
                sp.dma_start(xe[0:REST, par, FULL, :], xe_dram[bass.ds(at + FULL * P, REST), :]
                             ).then_inc(x_loaded[par], 16)
                wait_from(sp, y_kept, stage_value(e, TILES, -TILES))
                sp.dma_start(b2_sb[:, par], b2[bass.ds(e, 1)].rearrange("e c -> (e c)").partition_broadcast(P)
                             ).then_inc(b2_loaded[par], 16)
                if not (isinstance(e, int) and e == 0):
                    sp.wait_ge(w1_low, stage_value(e, KC, 0))
                    load_w1(sp, e)
                wait_from(sp, w2_low, stage_value(e, 2, 0))
                sp.dma_start(w2_raw[:], w2[bass.ds(e, 1)].rearrange("e (k p) c -> p (e k) c", p=P)
                             ).then_inc(w2_loaded, 16)

            sp.wait_ge(fields_cleared, 1)
            load(0, 0)
            load(1, 1)
            with sp.Fori(1, E // 2) as n:
                load(2 * n, 0)
                load(2 * n + 1, 1)

        def expert_pairs(eng, body):
            body(0, 0, True)
            body(1, 1, True)
            with eng.Fori(1, E // 2 - 1) as n:
                body(2 * n, 0, True)
                body(2 * n + 1, 1, True)
            body(E - 2, 0, True)
            body(E - 1, 1, False)

        @block.tensor
        def _(pe):
            pe.wait_ge(b1_loaded, 16)
            for r in range(BR):
                last = pe.transpose(up[:, 0, 0, r * P:(r + 1) * P], b1_rows[:, r, :], ident[:])
            last.then_inc(b1_turned, 1)

            def turn_x(e, par, n):
                if n == 0:
                    pe.wait_ge(x_loaded[par], stage_value(e - par, 16, 32))
                t0, t1 = TURNS[n]
                bank = turn[:, (par * NTURN + n) % 2, :]
                wait_from(pe, turn_kept, stage_value(e, NTURN, n - 1))
                for k in range(KC):
                    for t in range(t0, t1):
                        m = rows_of(t)
                        at = k * 2 * P + (t - t0) * P
                        last = pe.transpose(bank[:, at:at + m], xe[0:m, par, t, k * P:(k + 1) * P],
                                            ident[0:m, 0:m])
                last.then_inc(turned, 1)

            PARTS = ((0, 0), (0, 1), (1, 0))

            def body(e, par, more):
                pe.wait_ge(w1_low, stage_value(e, KC, KC))
                pe.wait_ge(turn_kept, stage_value(e, NTURN, NTURN))
                for f in range(FC):
                    wait_from(pe, gelu_done, stage_value(e, 2 * FC, 2 * (f - 1)))
                    for half in range(2):
                        for k in range(KC):
                            for n, (wp, xp) in enumerate(PARTS):
                                last = pe.matmul(up[:, f % 2, half, 0:HC],
                                                 w1_parts[:, par, wp, k, f * P:(f + 1) * P],
                                                 x_parts[:, par, xp, k, half * HC:(half + 1) * HC],
                                                 start=(k, n) == (0, 0), stop=(k, n) == (KC - 1, 2))
                    last.then_inc(up_done, 1)
                    if more and f in TURN_AT:
                        turn_x(e + 1, 1 - par, TURN_AT.index(f))
                pe.wait_ge(w2_low, stage_value(e, 2, 2))
                for t in range(TILES):
                    m = rows_of(t)
                    wait_from(pe, y_kept, stage_value(e, TILES, t - 1))
                    for f in range(FC):
                        if t == 0:
                            pe.wait_ge(h_low, stage_value(e, FC, f + 1))
                        for n, (wp, hp) in enumerate(PARTS):
                            last = pe.matmul(down[0:m, (par * TILES + t) % 2, 0:C],
                                             h_parts[:, hp, f, t * P:t * P + m], w2_parts[:, par, wp, f, :],
                                             start=(f, n) == (0, 0), stop=(f, n) == (FC - 1, 2))
                    last.then_inc(down_done, 1)

            pe.wait_ge(b1_kept, 1)
            for n in range(NTURN):
                turn_x(0, 0, n)
            expert_pairs(pe, body)

        @block.scalar
        def _(act):
            act.wait_ge(b1_kept, 2)

            def high_parts(e, par):
                act.wait_ge(w1_loaded, stage_value(e, 16, 16))
                for k in range(KC):
                    act.activation(w1_parts[:, par, 0, k, :], w1_raw[:, k, :], ACT.Copy).then_inc(w1_high, 1)
                act.wait_ge(w2_loaded, stage_value(e, 16, 16))
                for k in range(2):
                    act.activation(w2_parts[:, par, 0, HALF_F * k:HALF_F * (k + 1), :],
                                   w2_raw[:, HALF_F * k:HALF_F * (k + 1), :], ACT.Copy).then_inc(w2_high, 1)

            def body(e, par, more):
                for f in range(FC):
                    act.wait_ge(up_done, stage_value(e, FC, f + 1))
                    if f == 0:
                        wait_from(act, down_done, stage_value(e, TILES, 0))
                        act.wait_ge(b1_now_set, stage_value(e, 1, 1))
                    wait_from(act, h_low, stage_value(e, FC, f - 1))
                    for out in (h_full[:, f % 2, :], h_parts[:, 0, f, :]):
                        act.activation(out.rearrange("p (a b) -> p a b", a=2), up[:, f % 2, :, 0:HC],
                                       ACT.Gelu, bias=b1_now[:, par, f:f + 1]).then_inc(gelu_done, 1)
                if more:
                    high_parts(e + 1, 1 - par)

            high_parts(0, 0)
            expert_pairs(act, body)

        @block.gpsimd
        def _(pool):
            pool.iota(expert_id[:], pattern=[[1, E]], base=0, channel_multiplier=0,
                      allow_small_or_imprecise_dtypes=True).then_inc(ids_set, 1)
            pool.iota(spare[:], pattern=[[P, TILES]], base=0, channel_multiplier=1,
                      allow_small_or_imprecise_dtypes=True).then_inc(ids_set, 1)

            def body(e, par, more):
                for t in range(TILES):
                    m = rows_of(t)
                    pool.wait_ge(y_kept, stage_value(e, TILES, t + 1))
                    if t == 0:
                        pool.wait_ge(slots_read, stage_value(e, NSLOT_STEPS, NSLOT_STEPS))
                    pool.tensor_tensor(ye[0:m, par, t, :], ye[0:m, par, t, :],
                                       weight[0:m, par, t:t + 1].to_broadcast([m, C]), ALU.mult
                                       ).then_inc(y_weighed, 1)
                    pool.wait_ge(y_weighed, stage_value(e, TILES, t + 1))
                    if t == 0:
                        wait_from(pool, added, stage_value(e, 16 * TILES, 0))
                    pool.sem_inc(wait_carrier, 1)
                    pool.indirect_dma_start(
                        out=sums[:, :], out_offset=bass.IndirectOffsetOnAxis(ap=sum_at[0:m, par, t:t + 1], axis=0),
                        in_=ye[0:m, par, t, :], in_offset=None, bounds_check=NSUM - 1, compute_op=ALU.add
                    ).then_inc(added, 16)

            expert_pairs(pool, body)
            pool.wait_ge(added, 16 * TILES * E)

        @block.vector
        def _(dve):
            nc.vector.memset(xe[:, :, FULL, C:C + FIELDS], 0.0).then_inc(fields_cleared, 1)
            nc.vector.memset(x_parts[:, :, :, :, CAP:2 * HC].bitcast(F32), 0.0).then_inc(b1_kept, 1)
            dve.wait_ge(b1_turned, 1)
            nc.vector.tensor_copy(b1T[:].rearrange("p e f -> p (e f)"), up[:, 0, 0, 0:BR * P]).then_inc(b1_kept, 1)
            dve.wait_ge(b1_kept, 2)

            def keep_turned(e, par, n):
                t0, t1 = TURNS[n]
                dve.wait_ge(turned, stage_value(e, NTURN, n + 1))
                bank = turn[:, (par * NTURN + n) % 2, :].rearrange("p (k t) -> p k t", k=KC)
                cols = min(t1 * P, CAP) - t0 * P
                high, low = (x_parts[:, par, part, :, t0 * P:t0 * P + cols] for part in range(2))
                dve.tensor_copy(high, bank[:, :, 0:cols]).then_inc(x_high, 1)
                dve.wait_ge(x_high, stage_value(e, NTURN, n + 1))
                dve.tensor_tensor(low, bank[:, :, 0:cols], high.bitcast(F32), ALU.subtract).then_inc(turn_kept, 1)

            def low_w1(e, par, k):
                dve.wait_ge(w1_high, stage_value(e, KC, k + 1))
                dve.tensor_tensor(w1_parts[:, par, 1, k, :], w1_raw[:, k, :], w1_parts[:, par, 0, k, :].bitcast(F32),
                                  ALU.subtract).then_inc(w1_low, 1)

            def low_w2(e, par, k):
                rows = slice(HALF_F * k, HALF_F * (k + 1))
                dve.wait_ge(w2_high, stage_value(e, 2, k + 1))
                dve.tensor_tensor(w2_parts[:, par, 1, rows, :], w2_raw[:, rows, :],
                                  w2_parts[:, par, 0, rows, :].bitcast(F32), ALU.subtract).then_inc(w2_low, 1)

            def read_slots(e, par):
                fields = xe[:, par, :, C:C + FIELDS]
                k = NSLOT_STEPS
                dve.wait_ge(x_loaded[par], stage_value(e - par, 16, 32))
                wait_from(dve, added, stage_value(e, 16 * TILES, -16 * TILES))
                dve.tensor_scalar(expert_now[:], expert_id[:, bass.ds(e, 1)], 1.0, None, ALU.mult
                                  ).then_inc(slots_read, 1)
                dve.scalar_tensor_tensor(spare_now[:], fields[:, :, ROW_AT], 0.0, spare[:],
                                         ALU.is_equal, ALU.mult).then_inc(slots_read, 1)
                dve.wait_ge(slots_read, stage_value(e, k, 2))
                dve.scalar_tensor_tensor(shares[:], fields[:, :, EXPERTS_AT:EXPERTS_AT + 2], expert_now[:, 0:1],
                                         fields[:, :, WEIGHTS_AT:WEIGHTS_AT + 2], ALU.is_equal, ALU.mult
                                         ).then_inc(slots_read, 1)
                dve.tensor_tensor(sum_at[:, par, :], fields[:, :, ROW_AT], spare_now[:], ALU.add
                                  ).then_inc(slots_read, 1)
                dve.wait_ge(slots_read, stage_value(e, k, 4))
                dve.tensor_tensor(weight[:, par, :], shares[:, :, 0], shares[:, :, 1], ALU.add
                                  ).then_inc(slots_read, 1)

            dve.wait_ge(ids_set, 2)

            def body(e, par, more):
                wait_from(dve, gelu_done, stage_value(e, 2 * FC, -2 * FC))
                dve.tensor_scalar(b1_now[:, par, :], b1T[:, bass.ds(e, 1), :].rearrange("p e f -> p (e f)"),
                                  1.0, None, ALU.mult).then_inc(b1_now_set, 1)
                for f in range(FC):
                    dve.wait_ge(gelu_done, stage_value(e, 2 * FC, 2 * (f + 1)))
                    dve.tensor_tensor(h_parts[:, 1, f, :], h_full[:, f % 2, :], h_parts[:, 0, f, :].bitcast(F32),
                                      ALU.subtract).then_inc(h_low, 1)
                    if more and f in TURN_AT:
                        keep_turned(e + 1, 1 - par, TURN_AT.index(f))
                read_slots(e, par)
                dve.wait_ge(b2_loaded[par], stage_value(e - par, 8, 16))
                for t in range(TILES):
                    m = rows_of(t)
                    dve.wait_ge(down_done, stage_value(e, TILES, t + 1))
                    dve.tensor_tensor(ye[0:m, par, t, :], down[0:m, (par * TILES + t) % 2, 0:C], b2_sb[0:m, par, :],
                                      ALU.add).then_inc(y_kept, 1)
                    if more and t < 4:
                        (low_w1 if t < 2 else low_w2)(e + 1, 1 - par, t % 2)

            for k in range(2):
                low_w1(0, 0, k)
            for n in range(NTURN):
                keep_turned(0, 0, n)
            for k in range(2):
                low_w2(0, 0, k)
            expert_pairs(dve, body)


def last_norm(nc, sums, out_rows):
    NTOK, C = out_rows.shape
    SPARE = sums.shape[0] - NTOK
    GT = 4
    RING = 8
    GROUPS = NTOK // (GT * P)
    assert GROUPS % RING == 0

    with ExitStack() as ctx:
        def sb(name, shape, dt=F32):
            return ctx.enter_context(nc.sbuf_tensor(name, shape, dt))

        def sem(name):
            return ctx.enter_context(nc.semaphore(name))

        rows = sb("rows", [P, RING, GT, C])
        stats = sb("l_stats", [P, RING, GT, 6])
        mv = sb("l_mv", [P, RING, GT, 2])
        rstd = sb("l_rstd", [P, RING, GT])
        offset = sb("l_offset", [P, RING, GT])
        eps_col = sb("l_eps", [P, 1])

        eps_set = sem("eps_set")
        wait_carrier = sem("l_wait_carrier")
        loaded = [sem(f"l_loaded{p}") for p in range(RING)]
        stored = [sem(f"l_stored{p}") for p in range(RING)]
        stats_done = sem("stats_done")
        mean_done = sem("mean_done")
        rooted = sem("rooted")
        inverted = sem("inverted")
        scaled = sem("scaled")
        normed = sem("normed")

        def rows_of(dram, first, g):
            return dram[bass.ds(g * (GT * P) + first, GT * P), :].rearrange("(t p) c -> p t c", p=P)

        def groups(eng, body):
            for g in range(RING):
                body(g, g)
            with eng.Fori(1, GROUPS // RING) as n:
                for r in range(RING):
                    body(n * RING + r, r)

        block = ctx.enter_context(nc.Block())

        @block.sync
        def _(sp):
            def load(g, r):
                wait_from(sp, stored[r], stage_value(g - r, 16 // RING, 0))
                sp.dma_start(rows[:, r], rows_of(sums, SPARE, g)).then_inc(loaded[r], 16)

            groups(sp, load)

        @block.scalar
        def _(act):
            act.wait_ge(eps_set, 1)

            def finish(g, r):
                act.wait_ge(scaled, stage_value(g, 1, 1))
                for t in range(GT):
                    act.activation(rows[:, r, t, :], rows[:, r, t, :], ACT.Identity, bias=offset[:, r, t:t + 1],
                                   scale=rstd[:, r, t:t + 1]).then_inc(normed, 1)
                act.wait_ge(normed, stage_value(g, GT, GT))
                act.dma_start(rows_of(out_rows, 0, g), rows[:, r]).then_inc(stored[r], 16)

            def body(g, r):
                act.wait_ge(mean_done, stage_value(g, GT, GT))
                act.activation(rstd[:, r, :], mv[:, r, :, 1], ACT.Sqrt, bias=eps_col[:, 0:1]).then_inc(rooted, 1)
                if not (isinstance(g, int) and g == 0):
                    finish(g - 1, (r - 1) % RING)

            groups(act, body)
            finish(GROUPS - 1, RING - 1)
            for r in range(RING):
                act.wait_ge(stored[r], 16 * GROUPS // RING)

        @block.vector
        def _(dve):
            nc.vector.memset(eps_col[:], LN_EPS).then_inc(eps_set, 1)

            def means(g, r):
                dve.wait_ge(loaded[r], stage_value(g - r, 16 // RING, 16))
                for t in range(GT):
                    dve.bn_stats(stats[:, r, t, :], rows[:, r, t, :]).then_inc(stats_done, 1)
                dve.wait_ge(stats_done, stage_value(g, GT, GT))
                dve.sem_inc(wait_carrier, 1)
                for t in range(GT):
                    dve.bn_aggr(mv[:, r, t, :], stats[:, r, t, :]).then_inc(mean_done, 1)

            def invert(g, r):
                dve.wait_ge(rooted, stage_value(g, 1, 1))
                dve.reciprocal(rstd[:, r, :], rstd[:, r, :]).then_inc(inverted, 1)
                dve.wait_ge(inverted, stage_value(g, 1, 1))
                dve.scalar_tensor_tensor(offset[:, r, :], mv[:, r, :, 0], -1.0, rstd[:, r, :], ALU.mult, ALU.mult
                                         ).then_inc(scaled, 1)

            def body(g, r):
                means(g, r)
                if not (isinstance(g, int) and g == 0):
                    invert(g - 1, (r - 1) % RING)

            groups(dve, body)
            invert(GROUPS - 1, RING - 1)


_INS = ["L0_attn_x", "L0_attn_time_maa_x", "L0_attn_time_maa_w", "L0_attn_time_maa_k", "L0_attn_time_maa_v",
        "L0_attn_time_maa_r", "L0_attn_time_maa_w1", "L0_attn_time_maa_w2", "L0_attn_time_decay",
        "L0_attn_time_decay_w1", "L0_attn_time_decay_w2", "L0_attn_time_faaaa", "L0_attn_W_r", "L0_attn_W_k",
        "L0_attn_W_v", "L0_attn_W_o", "L0_attn_ln_g", "L0_attn_ln_b", "L0_ffn_gate_w", "L0_ffn_gate_b",
        "L0_ffn_w1", "L0_ffn_b1", "L0_ffn_w2", "L0_ffn_b2"]


def kernel(**inputs):
    import numpy as _np
    import concourse.bacc as _bacc
    from concourse import mybir as _mybir
    from concourse.bass_utils import run_bass_kernel_spmd as _run

    nc = _bacc.Bacc("TRN2", target_bir_lowering=False, num_devices=1)
    arrays, args = {}, []
    for name in _INS:
        a = _np.ascontiguousarray(inputs[name])
        arrays[f"in_{name}_dram"] = a
        args.append(nc.dram_tensor(f"in_{name}_dram", a.shape, _mybir.dt.from_np(a.dtype), kind="ExternalInput").ap())
    shape = arrays["in_L0_attn_x_dram"].shape
    out = nc.dram_tensor("out_0_dram", shape, _mybir.dt.float32, kind="ExternalOutput").ap()
    rwkv_moe(nc, *args, out)
    r = _run(nc, [arrays], core_ids=[0])
    return r.results[0]["out_0_dram"]
```
